# Optimizing a Trainium2 kernel written in Bass

```python
import numpy as np
import jax
import jax.numpy as jnp

def _softmax(x, axis=-1):
    return jax.nn.softmax(x, axis=axis)

def _gelu(x):
    return jax.nn.gelu(x, approximate=True)

def _silu(x):
    return jax.nn.silu(x)

def _sigmoid(x):
    return jax.nn.sigmoid(x)

def _layernorm(x, axis=-1, eps=1e-05):
    m = jnp.mean(x, axis=axis, keepdims=True)
    v = jnp.var(x, axis=axis, keepdims=True)
    return (x - m) / jnp.sqrt(v + eps)

def _scatter_add(tgt, idx, src, axis=0):
    return tgt.at[idx].add(src)

def _segment_sum(src, seg, n):
    return jax.ops.segment_sum(src, seg, n)
kernel_name = 'mk_decoder_postln_d1_seqx_r4_87b41d'

def setup_inputs(seed: int=0):
    np.random.seed(seed)
    _w = jnp.asarray

    def _rec_inputs():
        import jax
        import jax.numpy as jnp
        _rk = jax.random.key(seed)
        x = 7.22e-05 + 1 * jax.random.normal(jax.random.fold_in(_rk, 1), (32, 128, 256), jnp.float32)
        _lenS = 128 - jax.random.randint(jax.random.fold_in(_rk, 7), (32,), 0, max(1, 128 // 4) + 1, jnp.int32)
        _lenS2 = 128 - jax.random.randint(jax.random.fold_in(_rk, 8), (32,), 0, max(1, 128 // 4) + 1, jnp.int32)
        _ctx_1024P = jax.random.normal(jax.random.fold_in(_rk, 11), (32, 16, 256), jnp.float32)
        _ctx_1024c = jax.random.dirichlet(jax.random.fold_in(_rk, 511), 0.3 * jnp.ones((16,), jnp.float32), (32, 128))
        _ctx_1024t = jnp.einsum('bsk,bkd->bsd', _ctx_1024c, _ctx_1024P)
        _ctx_1024t = _ctx_1024t * jax.lax.rsqrt(jnp.mean(jnp.square(_ctx_1024t)) + 1e-12) * 0.953939
        ctx_1024 = 4.13588e-05 + 0.999923 * (_ctx_1024t + 0.3 * jax.random.normal(jax.random.fold_in(_rk, 611), (32, 128, 256), jnp.float32))
        return (x, ctx_1024)
    x, ctx_1024 = _rec_inputs()

    def _L0_attn_setup():
        import jax, jax.numpy as jnp
        import numpy as np
        NUM_HEADS = 16
        USE_MASKING = True
        NEG_INF = -1000000000.0
        key = jax.random.key(seed)
        k1, k2 = jax.random.split(key)
        B, S, D = (2, 512, 256)
        x = jax.random.normal(k1, (B, S, D), dtype=jnp.float32)
        qkv_weights = jax.random.normal(k2, (D, 3 * D), dtype=jnp.float32) * (1.0 / np.sqrt(D))
        return {'x': x, 'qkv_weights': qkv_weights}
    _L0_attn_all = _L0_attn_setup()
    _L0_attn_in = {k: v for k, v in _L0_attn_all.items() if k in ('qkv_weights',)}
    del _L0_attn_all

    def _L0_xattn_setup():
        import jax, jax.numpy as jnp
        import numpy as np
        EMBED_DIM = 256
        HEAD_DIM = 256
        GAMMA = 0.96875
        THETA = 10000.0
        SCALE_BASE = 512.0

        def _dup_interleave(x):
            return jnp.repeat(x, 2, axis=-1)

        def _rotate_half(x):
            x_even = x[..., ::2]
            x_odd = x[..., 1::2]
            return jnp.stack((-x_odd, x_even), axis=-1).reshape(x.shape)

        def _xpos(x, offset=0, inverse_scale=False):
            l = x.shape[-2]
            half = HEAD_DIM // 2
            scale_vec = (jnp.arange(0, HEAD_DIM, 2, dtype=jnp.float32) + 0.4 * HEAD_DIM) / (1.4 * HEAD_DIM)
            pos = jnp.arange(offset, offset + l, dtype=jnp.float32)
            scale = scale_vec[None, :] ** (pos / SCALE_BASE)[:, None]
            freqs = 1.0 / THETA ** (jnp.arange(half, dtype=jnp.float32) / half)
            sin_in = pos[:, None] * freqs[None, :]
            sin, cos = (jnp.sin(sin_in), jnp.cos(sin_in))
            if inverse_scale:
                scale = 1.0 / scale
            return x * _dup_interleave(cos * scale) + _rotate_half(x) * _dup_interleave(sin * scale)

        def _decay_mask(l, gamma):
            idx = jnp.arange(l, dtype=jnp.float32)
            diff = idx[:, None] - idx[None, :]
            return jnp.where(diff >= 0, gamma ** diff, 0.0)
        key = jax.random.key(seed)
        k1, k2, k3, k4, k5, k6 = jax.random.split(key, 6)
        B, L = (4, 512)
        s = 1.0 / np.sqrt(EMBED_DIM)
        return {'q': jax.random.normal(k1, (B, L, EMBED_DIM), dtype=jnp.float32), 'k': jax.random.normal(k2, (B, L, EMBED_DIM), dtype=jnp.float32), 'v': jax.random.normal(k3, (B, L, EMBED_DIM), dtype=jnp.float32), 'Wq': jax.random.normal(k4, (EMBED_DIM, HEAD_DIM), dtype=jnp.float32) * s, 'Wk': jax.random.normal(k5, (EMBED_DIM, HEAD_DIM), dtype=jnp.float32) * s, 'Wv': jax.random.normal(k6, (EMBED_DIM, HEAD_DIM), dtype=jnp.float32) * s}
    _L0_xattn_all = _L0_xattn_setup()
    _L0_xattn_in = {k: v for k, v in _L0_xattn_all.items() if k in ('Wq', 'Wk', 'Wv')}
    del _L0_xattn_all

    def _L0_ffn_setup():
        import jax, jax.numpy as jnp
        import numpy as np
        D_MODEL = 256
        FFN = 256
        N_EXPERTS = 8
        N_SHARED = 1
        TOP_K = 2
        B, S = (2, 512)

        def _swiglu(h):
            a, b = jnp.split(h, 2, axis=-1)
            return jax.nn.silu(a) * b
        key = jax.random.key(seed)
        ks = jax.random.split(key, 12)
        sc = 0.02
        return {'x': jax.random.normal(ks[0], (B, S, D_MODEL), dtype=jnp.float32), 'gate_w': jax.random.normal(ks[1], (D_MODEL, N_EXPERTS), dtype=jnp.float32) * sc, 'gate_b': jnp.zeros((N_EXPERTS,), dtype=jnp.float32), 'sw1': jax.random.normal(ks[2], (N_SHARED, D_MODEL, 2 * FFN), dtype=jnp.float32) * sc, 'sb1': jnp.zeros((N_SHARED, 2 * FFN), dtype=jnp.float32), 'sw2': jax.random.normal(ks[3], (N_SHARED, FFN, D_MODEL), dtype=jnp.float32) * sc, 'sb2': jnp.zeros((N_SHARED, D_MODEL), dtype=jnp.float32), 'rw1': jax.random.normal(ks[4], (N_EXPERTS, D_MODEL, 2 * FFN), dtype=jnp.float32) * sc, 'rb1': jnp.zeros((N_EXPERTS, 2 * FFN), dtype=jnp.float32), 'rw2': jax.random.normal(ks[5], (N_EXPERTS, FFN, D_MODEL), dtype=jnp.float32) * sc, 'rb2': jnp.zeros((N_EXPERTS, D_MODEL), dtype=jnp.float32)}
    _L0_ffn_all = _L0_ffn_setup()
    _L0_ffn_in = {k: v for k, v in _L0_ffn_all.items() if k in ('gate_w', 'gate_b', 'sw1', 'sb1', 'sw2', 'sb2', 'rw1', 'rb1', 'rw2', 'rb2')}
    del _L0_ffn_all
    return {'x': x, 'ctx_1024': ctx_1024, 'L0_attn_qkv_weights': _L0_attn_in['qkv_weights'], 'L0_xattn_Wq': _L0_xattn_in['Wq'], 'L0_xattn_Wk': _L0_xattn_in['Wk'], 'L0_xattn_Wv': _L0_xattn_in['Wv'], 'L0_ffn_gate_w': _L0_ffn_in['gate_w'], 'L0_ffn_gate_b': _L0_ffn_in['gate_b'], 'L0_ffn_sw1': _L0_ffn_in['sw1'], 'L0_ffn_sb1': _L0_ffn_in['sb1'], 'L0_ffn_sw2': _L0_ffn_in['sw2'], 'L0_ffn_sb2': _L0_ffn_in['sb2'], 'L0_ffn_rw1': _L0_ffn_in['rw1'], 'L0_ffn_rb1': _L0_ffn_in['rb1'], 'L0_ffn_rw2': _L0_ffn_in['rw2'], 'L0_ffn_rb2': _L0_ffn_in['rb2']}

def reference(x, ctx_1024, L0_attn_qkv_weights, L0_xattn_Wq, L0_xattn_Wk, L0_xattn_Wv, L0_ffn_gate_w, L0_ffn_gate_b, L0_ffn_sw1, L0_ffn_sb1, L0_ffn_sw2, L0_ffn_sb2, L0_ffn_rw1, L0_ffn_rb1, L0_ffn_rw2, L0_ffn_rb2):
    import jax
    import jax.numpy as jnp

    def _L0_attn_ref(x, qkv_weights):
        import jax, jax.numpy as jnp
        import numpy as np
        NUM_HEADS = 16
        USE_MASKING = True
        NEG_INF = -1000000000.0
        B, S, D = x.shape
        H = NUM_HEADS
        Dh = D // H
        qkv = jnp.einsum('bsd,de->bse', x, qkv_weights)
        qkv = qkv.reshape(-1, 3 * D)
        pre_q = qkv[:, 0 * D:1 * D].reshape(-1, S, H, Dh)
        pre_k = qkv[:, 1 * D:2 * D].reshape(-1, S, H, Dh)
        pre_v = qkv[:, 2 * D:3 * D].reshape(-1, S, H, Dh)
        q = jnp.transpose(pre_q, (0, 2, 1, 3)).reshape(-1, S, Dh)
        v = jnp.transpose(pre_v, (0, 2, 1, 3)).reshape(-1, S, Dh)
        k = jnp.transpose(pre_k, (0, 2, 3, 1)).reshape(-1, S, Dh)
        scale = jnp.asarray(np.sqrt(Dh), dtype=x.dtype)
        a = jnp.einsum('aib,ajb->aij', q, k) / scale
        if USE_MASKING:
            tril = jnp.tril(jnp.ones((S, S), dtype=x.dtype))[None]
            a = tril * a + NEG_INF * (1.0 - tril)
        a = jax.nn.softmax(a, axis=-1)
        heads = jnp.einsum('aij,ajb->aib', a, v)
        heads = heads.reshape(-1, H, S, Dh)
        heads = jnp.transpose(heads, (0, 2, 1, 3)).reshape(-1, S, D)
        return heads

    def _L0_xattn_ref(q, k, v, Wq, Wk, Wv):
        import jax, jax.numpy as jnp
        import numpy as np
        EMBED_DIM = 256
        HEAD_DIM = 256
        GAMMA = 0.96875
        THETA = 10000.0
        SCALE_BASE = 512.0

        def _dup_interleave(x):
            return jnp.repeat(x, 2, axis=-1)

        def _rotate_half(x):
            x_even = x[..., ::2]
            x_odd = x[..., 1::2]
            return jnp.stack((-x_odd, x_even), axis=-1).reshape(x.shape)

        def _xpos(x, offset=0, inverse_scale=False):
            l = x.shape[-2]
            half = HEAD_DIM // 2
            scale_vec = (jnp.arange(0, HEAD_DIM, 2, dtype=jnp.float32) + 0.4 * HEAD_DIM) / (1.4 * HEAD_DIM)
            pos = jnp.arange(offset, offset + l, dtype=jnp.float32)
            scale = scale_vec[None, :] ** (pos / SCALE_BASE)[:, None]
            freqs = 1.0 / THETA ** (jnp.arange(half, dtype=jnp.float32) / half)
            sin_in = pos[:, None] * freqs[None, :]
            sin, cos = (jnp.sin(sin_in), jnp.cos(sin_in))
            if inverse_scale:
                scale = 1.0 / scale
            return x * _dup_interleave(cos * scale) + _rotate_half(x) * _dup_interleave(sin * scale)

        def _decay_mask(l, gamma):
            idx = jnp.arange(l, dtype=jnp.float32)
            diff = idx[:, None] - idx[None, :]
            return jnp.where(diff >= 0, gamma ** diff, 0.0)
        qh = _xpos(q @ Wq, offset=0, inverse_scale=False)
        kh = _xpos(k @ Wk, offset=0, inverse_scale=True)
        vh = v @ Wv
        L = qh.shape[-2]
        mask = _decay_mask(L, GAMMA)
        scores = jnp.einsum('bld,bmd->blm', qh, kh) * mask[None, :, :]
        return scores @ vh

    def _L0_ffn_ref(x, gate_w, gate_b, sw1, sb1, sw2, sb2, rw1, rb1, rw2, rb2):
        import jax, jax.numpy as jnp
        import numpy as np
        D_MODEL = 256
        FFN = 256
        N_EXPERTS = 8
        N_SHARED = 1
        TOP_K = 2
        B, S = (2, 512)

        def _swiglu(h):
            a, b = jnp.split(h, 2, axis=-1)
            return jax.nn.silu(a) * b
        hs = jnp.einsum('bsd,ndf->nbsf', x, sw1) + sb1[:, None, None, :]
        shared_out = jnp.einsum('nbsf,nfd->bsd', _swiglu(hs), sw2) + sb2.sum(0)
        probs = jax.nn.softmax(x @ gate_w + gate_b, axis=-1)
        topk_probs, topk_idx = jax.lax.top_k(probs, TOP_K)
        cw = jnp.sum(jax.nn.one_hot(topk_idx, N_EXPERTS, dtype=x.dtype) * topk_probs[..., None], axis=2)
        hr = jnp.einsum('bsd,edf->ebsf', x, rw1) + rb1[:, None, None, :]
        out_e = jnp.einsum('ebsf,efd->ebsd', _swiglu(hr), rw2) + rb2[:, None, None, :]
        routed_out = jnp.einsum('ebsd,bse->bsd', out_e, cw)
        return shared_out + routed_out
    x = _layernorm(x + _L0_attn_ref(x, L0_attn_qkv_weights), axis=-1)
    x = _layernorm(x + _L0_xattn_ref(x, ctx_1024, ctx_1024, L0_xattn_Wq, L0_xattn_Wk, L0_xattn_Wv), axis=-1)
    x = _layernorm(x + _L0_ffn_ref(x, L0_ffn_gate_w, L0_ffn_gate_b, L0_ffn_sw1, L0_ffn_sb1, L0_ffn_sw2, L0_ffn_sb2, L0_ffn_rw1, L0_ffn_rb1, L0_ffn_rw2, L0_ffn_rb2), axis=-1)
    return x

_drawn_inputs = setup_inputs


def setup_inputs(seed=0):
    import zlib

    import numpy as np

    out = dict(_drawn_inputs(seed))
    spreads = {'L0_ffn_gate_b': (0.0, 0.561),
     'L0_ffn_sb1': (0.0, 0.8),
     'L0_ffn_sb2': (0.0, 0.352),
     'L0_ffn_rb1': (0.0, 0.8),
     'L0_ffn_rb2': (0.0, 0.99)}
    factors = {'L0_ffn_sw1': 3.098, 'L0_ffn_sw2': 3.075, 'L0_ffn_rw1': 8.0, 'L0_ffn_rw2': 8.0}
    for name, (base, spread) in spreads.items():
        noise = np.random.default_rng([zlib.crc32(name.encode()), seed]).standard_normal(out[name].shape)
        drawn = base * np.exp(spread * noise) if base else spread * noise
        out[name] = jnp.asarray(drawn.astype(out[name].dtype))
    for name, factor in factors.items():
        out[name] = (out[name] * factor).astype(out[name].dtype)
    return out
```

```python
from contextlib import ExitStack

import numpy as np
import concourse.bass as bass
from concourse import mybir

F32 = mybir.dt.float32
BF16 = mybir.dt.bfloat16
U32 = mybir.dt.uint32
I32 = mybir.dt.int32
ALU = mybir.AluOpType
ACT = mybir.ActivationFunctionType
AX_X = mybir.AxisListType.X

P = 128
B, S, D = 32, 128, 256
DC = D // P
H, DH = 16, 16
NU = S // DH
GB = P // DH
NG = B // GB
NE, TOPK, FFN = 8, 2, 256
VW = DH + 1
BANK = 512
REGION = B * S + P
NTILE = B * S * TOPK // P + NE - 1
TILES = NTILE + NTILE % 2
IDLE_ROW = NE * REGION
IDLE = TILES - B * S * TOPK // P
XROWS = IDLE_ROW + IDLE * P
QB = 4
NQ = B // QB
EPS = 1e-5
NEG_INF = -1000000000.0
GAMMA, THETA, SCALE_BASE = 0.96875, 10000.0, 512.0

assert S == P and GB * DH == P and H * DH == D


def shape_tables():
    i = np.arange(P)
    ident = np.eye(P, dtype=np.float32)
    causal = np.where(i[None, :] <= i[:, None], 0.0, NEG_INF).astype(np.float32)
    diff = (i[None, :] - i[:, None]).astype(np.float64)
    decay = np.where(diff >= 0, GAMMA ** np.maximum(diff, 0), 0.0).astype(np.float32)
    half = D // 2
    pos = i.astype(np.float32)
    scale_vec = (np.arange(0, D, 2, dtype=np.float32) + np.float32(0.4 * D)) / np.float32(1.4 * D)
    scale = scale_vec[:, None] ** (pos / np.float32(SCALE_BASE))[None, :]
    freqs = (1.0 / THETA ** (np.arange(half, dtype=np.float32) / half)).astype(np.float32)
    angle = freqs[:, None] * pos[None, :]
    cos, sin = np.cos(angle), np.sin(angle)
    kc, ks, qc, qs = cos / scale, sin / scale, cos * scale, sin * scale
    rot_cos = np.concatenate([kc, kc, qc, qc], 1)
    rot_sin = np.concatenate([ks, -ks, qs, -qs], 1)
    f32 = np.concatenate([ident, decay, rot_cos, rot_sin,
                          np.tile(np.arange(NE), (P, 1)), np.tile(np.arange(NE) * REGION, (P, 1)),
                          i[:, None], np.tile((np.arange(NE)[None, :] <= np.arange(NE)[:, None]).reshape(-1), (P, 1)),
                          np.tile(np.arange(TILES), (P, 1)), np.tile(np.arange(TILES) * P, (P, 1))], 1)
    before = (i[:, None] < i[None, :]).astype(np.float32)
    bf = np.concatenate([ident, causal, before, np.ones((P, P))], 1)
    return np.ascontiguousarray(f32, np.float32), np.ascontiguousarray(bf, np.float32)


def at(k, s, lag):
    off = s - lag
    return k + off // 2, off % 2


def decoder_kernel(nc, x, ctx_1024, wqkv, xwq, xwk, xwv, gate_w, gate_b, sw1, sb1, sw2, sb2,
                   rw1, rb1, rw2, rb2, table_f32, table_bf16, out):
    ctx = ExitStack()
    with ctx:
        def sb(name, shape, dt=F32):
            return ctx.enter_context(nc.sbuf_tensor(name, shape, dt))

        def sem(name):
            return ctx.enter_context(nc.semaphore(name))

        xT_dram = nc.dram_tensor("xT_dram", (B, P, DC, P), F32).ap()
        cT_dram = nc.dram_tensor("cT_dram", (B, P, DC, P), F32).ap()
        k_dram = nc.dram_tensor("k_dram", (B, DH, GB, 2 * DH * NU), F32).ap()

        x2_dram = nc.dram_tensor("x2_dram", (B, P, D), F32).ap()
        x2T_dram = nc.dram_tensor("x2T_dram", (B, P, DC, P), F32).ap()
        sent = nc.dram_tensor("sent", (XROWS, D), F32).ap()
        back = nc.dram_tensor("back", (TILES * P, D), F32).ap()
        NBIAS = NE * 2 * FFN + NE * D + D
        bias_dram = nc.dram_tensor("bias_dram", (3, NBIAS), BF16).ap()

        ps = ctx.enter_context(nc.psum_tensor("ps", [P, 8, BANK], F32))
        SCORE = [ps[:, 0, :], ps[:, 1, :]]
        PROBT = [ps[:, 2, :], ps[:, 3, :]]
        HEADS = ps[:, 4, 0:H * VW].rearrange("p (h v) -> p h v", v=VW)
        QV = ps[:, 5, :]
        YX = ps[:, 5, 0:D]
        XV = ps[:, 6, 0:D]
        SCX = ps[:, 6, 0:P]
        KQ = ps[:, 6:8, :].rearrange("p b c -> p (b c)")[:, D:3 * D].rearrange("p (r t) -> p r t", t=P)
        TR = ps[:, 7, D:2 * D]
        GATE = ps[:, 7, 0:3 * NE]

        tf = sb("tf", [P, 10 * P + 2 * NE + 1 + NE * NE + 2 * TILES])
        ident = tf[:, 0:P]
        decay = tf[:, P:2 * P]
        rot_cos = tf[:, 2 * P:6 * P].rearrange("p (r t) -> p r t", t=P)
        rot_sin = tf[:, 6 * P:10 * P].rearrange("p (r t) -> p r t", t=P)
        o = 10 * P
        expert_ids = tf[:, o:o + NE]
        region_rows = tf[:, o + NE:o + 2 * NE]
        lane_id = tf[:, o + 2 * NE:o + 2 * NE + 1]
        o += 2 * NE + 1
        not_later = tf[:, o:o + NE * NE].rearrange("p (e f) -> p e f", f=NE)
        o += NE * NE
        tile_ids = tf[:, o:o + TILES]
        tile_rows = tf[:, o + TILES:o + 2 * TILES]
        tb = sb("tb", [P, 4 * P], BF16)
        before_bf = tb[:, 2 * P:3 * P]
        ones_bf = tb[:, 3 * P:4 * P]
        ident_bf = tb[:, 0:P]
        causal_bf = tb[:, P:2 * P]
        wqkv_sb = sb("wqkv_sb", [P, DC, 3 * D])
        xwq_sb = sb("xwq_sb", [P, DC, D])
        xwk_sb = sb("xwk_sb", [P, DC, D])
        xwv_sb = sb("xwv_sb", [P, DC, D])

        gate_w_sb = sb("gate_w_sb", [P, DC, NE])
        gate_b_sb = sb("gate_b_sb", [1, NE])
        ones_row = sb("ones_row", [1, P])
        sw1_sb = sb("sw1_sb", [P, DC, 2 * FFN])
        sw2_sb = sb("sw2_sb", [P, FFN // P, D])
        sb1_sb = sb("sb1_sb", [P, 2 * FFN // P])
        bias_rows = sb("bias_rows", [3, NBIAS], BF16)
        bias_in = sb("bias_in", [P, NBIAS // P])
        bias_left = sb("bias_left", [P, 2, NBIAS // P])
        bias_parts = sb("bias_parts", [P, 3, NBIAS // P], BF16)

        first_use = sb("first_use", [P, 6 * GB * D])

        def part(n, *dims):
            names = "abcd"[:len(dims)]
            return first_use[:, n * GB * D:(n + 1) * GB * D].rearrange(
                f"p ({' '.join(names)}) -> p {' '.join(names)}", **dict(zip(names, dims)))

        xin = part(0, GB, D)
        cin = part(1, GB, D)
        xTn = part(2, GB, DC, P)
        cTn = part(3, GB, DC, P)
        xTu = part(4, DC, NU, GB, DH)
        kk = part(5, GB, 2 * DH, NU)
        RW1 = NE * DC * 2 * FFN
        rw1_sb = first_use[:, 0:RW1]
        rw2_sb = first_use[:, RW1:RW1 + NE * FFN // P * D]
        assert RW1 + NE * FFN // P * D <= 6 * GB * D

        xT = sb("xT", [P, 2, DC, P])
        cT = sb("cT", [P, 2, DC, P])
        xn = sb("xn", [P, 2, D])
        kp = sb("kp", [P, 2, 2, 2 * DH, NU])
        qT = sb("qT", [P, 2, DC, P])
        va = sb("va", [P, 2, H, VW])
        nmax = sb("nmax", [P, 2, H])
        prob = sb("prob", [P, 2, H, P])
        pT = sb("pT", [P, 2, 4, P])
        rden = sb("rden", [P, 2, H])
        att = sb("att", [P, 2, D])
        res1 = sb("res1", [P, 2, D])
        bn1 = sb("bn1", [P, 2, 6])
        mv1 = sb("mv1", [P, 2, 2])
        rstd1 = sb("rstd1", [P, 2, 1])
        x1 = sb("x1", [P, 2, D])
        x1T = sb("x1T", [P, 2, DC, P])
        xv = sb("xv", [P, 2, D])
        ra = sb("ra", [P, 2, 4, P])
        rb = sb("rb", [P, 2, 4, P])
        rot = sb("rot", [P, 2, 4, P])
        scx = sb("scx", [P, 2, P])
        res2 = sb("res2", [P, 2, D])
        bn2 = sb("bn2", [P, 2, 6])
        mv2 = sb("mv2", [P, 2, 2])
        rstd2 = sb("rstd2", [P, 2, 1])
        x2 = sb("x2", [P, 2, D])
        neg_half = sb("neg_half", [P, QB])
        x2T = sb("x2T", [P, 2, DC, P])
        x2s = sb("x2s", [P, 2, D])
        gc = sb("gc", [P, 2, 3 * NE])
        lmax = sb("lmax", [P, 2, 1])
        gexp = sb("gexp", [P, 2, NE])
        gsum = sb("gsum", [P, 2, 1])
        ginv = sb("ginv", [P, 2, 1])
        gprob = sb("gprob", [P, 2, NE])
        top_p = sb("top_p", [P, 2, 8])
        top_i = sb("top_i", [P, 2, 8], U32)
        top_f = sb("top_f", [P, 2, TOPK])
        pick = sb("pick", [P, 2, TOPK, NE])
        pick_all = sb("pick_all", [P, B, TOPK, NE])
        shifts = sb("shifts", [P, NE])
        shifted = sb("shifted", [P, B, TOPK, NE])
        shift = sb("shift", [P, B, TOPK])
        back_rows = sb("back_rows", [P, B, TOPK], U32)
        picks = sb("picks", [P, 2, NE], BF16)
        base = sb("base", [P, NE])
        place = sb("place", [P, 2, NE])
        mine = sb("mine", [P, 2, TOPK, NE])
        pos = sb("pos", [P, 2, TOPK], U32)
        pos_all = sb("pos_all", [P, B, TOPK], U32)
        cw_all = sb("cw_all", [P, B, TOPK])
        zeros = sb("zeros", [P, D])
        tail_rows = sb("tail_rows", [P, NE], U32)
        counts = sb("counts", [P, 4, NE])
        counts_i = sb("counts_i", [P, 2, NE], I32)
        upto = sb("upto", [P, NE, NE])
        passed = sb("passed", [1, TILES, NE])
        skipped = sb("skipped", [1, TILES, NE])
        tile_f = sb("tile_f", [1, 2, TILES])
        tile_expert = sb("tile_expert", [1, TILES], I32)
        tile_row = sb("tile_row", [1, TILES], I32)

        xg = sb("xg", [P, 4, D])
        xgT = sb("xgT", [P, 2, DC, P])
        sil = sb("sil", [P, 2, FFN])
        gate_h = sb("gate_h", [P, 2, FFN])
        ghT = sb("ghT", [P, 2, FFN // P, P])
        yg = sb("yg", [P, 2, D])

        x2T4 = prob[:, 0, :, :].rearrange("p h t -> p (h t)").rearrange("p (r b c t) -> p r b c t", r=2, b=QB, c=DC)
        x2n = prob[:, 1, :, :].rearrange("p h t -> p (h t)").rearrange("p (r b d) -> p r b d", r=2, b=QB)
        ssil = first_use[:, 0:2048].rearrange("p (r f t) -> p r f t", r=2, f=FFN // P)
        sgh = first_use[:, 2048:4096].rearrange("p (r f t) -> p r f t", r=2, f=FFN // P)
        ya = first_use[:, 4096:6144].rearrange("p (r b d) -> p r b d", r=2, b=QB)
        yb = first_use[:, 6144:8192].rearrange("p (r b d) -> p r b d", r=2, b=QB)
        got = first_use[:, 8192:12288].rearrange("p (r b j d) -> p r b j d", r=2, b=QB, j=TOPK)
        y3 = sb("y3", [P, 2, QB, D])
        pos4 = sb("pos4", [P, 2, QB, TOPK], U32)
        cw4 = sb("cw4", [P, 2, QB, TOPK])
        bn3 = sb("bn3", [P, 2, QB, 6])
        mv3 = sb("mv3", [P, 2, QB, 2])
        var3 = sb("var3", [P, 2, QB])
        rstd3 = sb("rstd3", [P, 2, QB])

        tables_in = sem("tables_in")
        w_in = sem("w_in")
        xw_in = sem("xw_in")
        consts_set = sem("consts_set")
        xin_in = sem("xin_in")
        cin_in = sem("cin_in")
        x_turned = sem("x_turned")
        c_turned = sem("c_turned")
        k_made = sem("k_made")
        xTn_set = sem("xTn_set")
        cTn_set = sem("cTn_set")
        xTu_set = sem("xTu_set")
        kk_set = sem("kk_set")
        xT_stored = sem("xT_stored")
        cT_stored = sem("cT_stored")
        k_stored = sem("k_stored")

        xT_in = [sem("xT_in0"), sem("xT_in1")]
        cT_in = [sem("cT_in0"), sem("cT_in1")]
        xn_in = [sem("xn_in0"), sem("xn_in1")]
        kp_in = [sem("kp_in0"), sem("kp_in1")]
        qv_made = sem("qv_made")
        q_set = sem("q_set")
        v_set = sem("v_set")
        scored = sem("scored")
        maxed = sem("maxed")
        expd = sem("expd")
        p_turned = sem("p_turned")
        pT_even = sem("pT_even")
        pT_odd = sem("pT_odd")
        heads_made = sem("heads_made")
        den_set = sem("den_set")
        att_set = sem("att_set")
        res1_set = sem("res1_set")
        bn1_set = sem("bn1_set")
        mv1_set = sem("mv1_set")
        rstd1_set = sem("rstd1_set")
        x1_set = sem("x1_set")
        x1_turned = sem("x1_turned")
        x1T_set = sem("x1T_set")
        xkv_made = sem("xkv_made")
        xv_set = sem("xv_set")
        xq_made = sem("xq_made")
        rot_a = sem("rot_a")
        rot_b = sem("rot_b")
        rot_set = sem("rot_set")
        scx_made = sem("scx_made")
        scx_set = sem("scx_set")
        yx_made = sem("yx_made")
        res2_set = sem("res2_set")
        bn2_set = sem("bn2_set")
        mv2_set = sem("mv2_set")
        rstd2_set = sem("rstd2_set")
        x2_set = sem("x2_set")
        x2_stored = [sem("x2_stored0"), sem("x2_stored1")]
        x2T_stored = [sem("x2T_stored0"), sem("x2T_stored1")]
        small_in = sem("small_in")
        ffn_in = sem("ffn_in")
        bias_split = sem("bias_split")
        bias_out = sem("bias_out")
        bias_back = sem("bias_back")
        base_set = sem("base_set")
        tail_made = sem("tail_made")
        x2T_set = sem("x2T_set")
        gc_set = sem("gc_set")
        x2s_set = sem("x2s_set")
        lmax_set = sem("lmax_set")
        gexp_set = sem("gexp_set")
        ginv_set = sem("ginv_set")
        gprob_set = sem("gprob_set")
        top_p_set = sem("top_p_set")
        top_i_set = sem("top_i_set")
        top_f_set = sem("top_f_set")
        pick_set = sem("pick_set")
        picks_set = sem("picks_set")
        place_set = sem("place_set")
        mine_set = sem("mine_set")
        pos_set = sem("pos_set")
        kept_set = sem("kept_set")
        sent_in = [sem("sent_in0"), sem("sent_in1")]
        zeros_sent = sem("zeros_sent")
        idle_sent = sem("idle_sent")
        plan_step = sem("plan_step")
        xg_in = [sem(f"xg_in{i}") for i in range(4)]
        yg_out = [sem("yg_out0"), sem("yg_out1")]
        xg_turned = sem("xg_turned")
        xgT_set = sem("xgT_set")
        hid_made = sem("hid_made")
        sil_set = sem("sil_set")
        gh_set = sem("gh_set")
        gh_turned = sem("gh_turned")
        ghT_set = sem("ghT_set")
        yg_made = sem("yg_made")
        yg_set = sem("yg_set")
        x2T4_in = [sem("x2T4_in0"), sem("x2T4_in1")]
        x2n_in = [sem("x2n_in0"), sem("x2n_in1")]
        got_in = [sem("got_in0"), sem("got_in1")]
        shid_made = sem("shid_made")
        ssil_set = sem("ssil_set")
        sgh_set = sem("sgh_set")
        sy_made = sem("sy_made")
        mix_a = sem("mix_a")
        mix_b = sem("mix_b")
        mix_c = sem("mix_c")
        bn3_set = sem("bn3_set")
        mv3_set = sem("mv3_set")
        rstd3_set = sem("rstd3_set")
        y3_set = sem("y3_set")
        pos4_set = sem("pos4_set")
        cw4_set = sem("cw4_set")
        PLAN_STEPS = 20
        out_stored = [sem("out_stored0"), sem("out_stored1")]

        block = ctx.enter_context(nc.Block())
        LOAD_AHEAD, LAST_LAG = 2, 6
        FIRST_K, END_K = LAST_LAG // 2, (B - LOAD_AHEAD) // 2

        def phases(eng, step):
            def peeled(first, end):
                for k in range(first, end):
                    for s in range(2):
                        step(k, s, lambda lag: 0 <= 2 * k + s - lag < B)

            peeled(-LOAD_AHEAD // 2, FIRST_K)
            with eng.Fori(FIRST_K, END_K) as k:
                for s in range(2):
                    step(k, s, lambda lag: True)
            peeled(END_K, (B + LAST_LAG + 1) // 2)

        def groups(eng, body):
            body(0)
            with eng.Fori(1, NG) as g:
                body(g)

        def after(eng, what, count):
            if not isinstance(count, int) or count > 0:
                eng.wait_ge(what, count)

        @block.sync
        def _(eng):
            eng.dma_start(tf[:, :], table_f32).then_inc(tables_in, 16)
            eng.dma_start(tb[:, :], table_bf16).then_inc(tables_in, 16)
            eng.dma_start(wqkv_sb[:, :, :], wqkv.rearrange("(c p) n -> p c n", p=P)).then_inc(w_in, 16)
            eng.dma_start(gate_w_sb[:, :, :], gate_w.rearrange("(c p) n -> p c n", p=P)).then_inc(small_in, 16)
            eng.dma_start(gate_b_sb[:, :], gate_b.rearrange("(o n) -> o n", o=1)).then_inc(small_in, 16)
            eng.dma_start(sb1_sb[:, :], sb1[0].rearrange("(c p) -> p c", p=P), allow_slow_non_contiguous=True).then_inc(small_in, 16)
            o1, o2 = NE * 2 * FFN // P, (NE * 2 * FFN + NE * D) // P
            spans = ((0, o1, rb1.rearrange("e n -> (e n)")), (o1, o2, rb2.rearrange("e n -> (e n)")),
                     (o2, NBIAS // P, sb2.rearrange("e n -> (e n)")))
            for lo, hi, src in spans:
                eng.dma_start(bias_in[:, lo:hi], src.rearrange("(p n) -> p n", p=P)).then_inc(small_in, 16)

            def prepare(g):
                after(eng, x_turned, g * 4)
                eng.dma_start(xin[:, :, :], x[bass.ds(g * GB, GB)].rearrange("b p d -> p b d")).then_inc(xin_in, 16)
                after(eng, c_turned, g * 4)
                eng.dma_start(cin[:, :, :], ctx_1024[bass.ds(g * GB, GB)].rearrange("b p d -> p b d")).then_inc(cin_in, 16)
                eng.wait_ge(xTn_set, g * 4 + 4)
                eng.dma_start(xT_dram[bass.ds(g * GB, GB)].rearrange("b p c t -> p b c t"), xTn[:, :, :, :]).then_inc(xT_stored, 16)
                eng.wait_ge(cTn_set, g * 4 + 4)
                eng.dma_start(cT_dram[bass.ds(g * GB, GB)].rearrange("b p c t -> p b c t"), cTn[:, :, :, :]).then_inc(cT_stored, 16)
                eng.wait_ge(kk_set, g * 4 + 4)
                eng.dma_start(k_dram[bass.ds(g * GB, GB)].rearrange("b i g f -> (b i) (g f)"),
                              first_use[:, 5 * GB * D:6 * GB * D]).then_inc(k_stored, 16)
            groups(eng, prepare)
            for w, src in ((xwq_sb, xwq), (xwk_sb, xwk), (xwv_sb, xwv)):
                eng.dma_start(w[:, :, :], src.rearrange("(c p) n -> p c n", p=P)).then_inc(xw_in, 16)
            eng.wait_ge(bias_split, 5)
            for n in range(3):
                for lo, hi, _ in spans:
                    eng.dma_start(bias_dram[n, lo * P:hi * P].rearrange("(p n) -> p n", p=P),
                                  bias_parts[:, n, lo:hi]).then_inc(bias_out, 16)
            eng.wait_ge(bias_out, 9 * 16)
            eng.dma_start(bias_rows[:, :], bias_dram).then_inc(bias_back, 16)
            eng.wait_ge(xT_stored, 16 * NG)
            eng.wait_ge(cT_stored, 16 * NG)
            eng.wait_ge(k_stored, 16 * NG)
            eng.dma_start(sw1_sb[:, :, :], sw1[0].rearrange("(c p) n -> p c n", p=P)).then_inc(ffn_in, 16)
            eng.dma_start(sw2_sb[:, :, :], sw2[0].rearrange("(c p) n -> p c n", p=P)).then_inc(ffn_in, 16)
            eng.wait_ge(k_made, 4 * NG)
            eng.wait_ge(c_turned, 4 * NG)
            eng.dma_start(rw1_sb.rearrange("p (e c n) -> p e c n", e=NE, c=DC),
                          rw1.rearrange("e (c p) n -> p e c n", p=P)).then_inc(ffn_in, 16)
            eng.dma_start(rw2_sb.rearrange("p (e c n) -> p e c n", e=NE, c=FFN // P),
                          rw2.rearrange("e (c p) n -> p e c n", p=P)).then_inc(ffn_in, 16)

            def step(k, s, live):
                if live(-2):
                    kk_, r = at(k, s, -2)
                    t = kk_ * 2 + r
                    after(eng, qv_made, t - 1)
                    eng.dma_start(xT[:, r, :, :], xT_dram[t]).then_inc(xT_in[r], 16)
                if live(-1):
                    kk_, r = at(k, s, -1)
                    t = kk_ * 2 + r
                    after(eng, scored, (t - 1) * 4)
                    if isinstance(t, int) and t < 2:
                        eng.wait_ge(consts_set, 1)
                    for j in range(GB):
                        lo = 16 * j
                        eng.dma_start(kp[lo:lo + DH, r, j % 2, :, :].rearrange("p a u -> p (a u)"),
                                      k_dram[t, :, j, :]).then_inc(kp_in[r], 16)
                if live(1):
                    kk_, r = at(k, s, 1)
                    t = kk_ * 2 + r
                    after(eng, xkv_made, t - 1)
                    eng.dma_start(cT[:, r, :, :], cT_dram[t]).then_inc(cT_in[r], 16)
                    after(eng, res1_set, t - 1)
                    eng.dma_start(xn[:, r, :], x[t]).then_inc(xn_in[r], 16)
                if live(4):
                    kk_, r = at(k, s, 4)
                    t = kk_ * 2 + r
                    eng.wait_ge(x2_set, t + 1)
                    eng.dma_start(x2_dram[t], x2[:, r, :]).then_inc(x2_stored[r], 16)
                    eng.wait_ge(x2T_set, t + 1)
                    eng.dma_start(x2T_dram[t], x2T[:, r, :, :]).then_inc(x2T_stored[r], 16)

            phases(eng, step)
            for r in range(2):
                eng.wait_ge(x2_stored[r], 16 * (B // 2))
                eng.wait_ge(x2T_stored[r], 16 * (B // 2))
            for r in range(2):
                eng.wait_ge(sent_in[r], 32 * (B // 2))

            def load(q, r):
                rows = bass.ds(q * QB, QB)
                eng.dma_start(x2T4[:, r, :, :, :], x2T_dram[rows].rearrange("b p c t -> p b c t")).then_inc(x2T4_in[r], 16)
                eng.dma_start(x2n[:, r, :, :], x2_dram[rows].rearrange("b p d -> p b d")).then_inc(x2n_in[r], 16)

            for r in range(2):
                load(r, r)
            def turn(k, r, more):
                q = 2 * k + r
                if more:
                    eng.wait_ge(shid_made, 2 * q + 2)
                    eng.dma_start(x2T4[:, r, :, :, :], x2T_dram[bass.ds((q + 2) * QB, QB)].rearrange("b p c t -> p b c t")
                                  ).then_inc(x2T4_in[r], 16)
                    eng.wait_ge(mix_a, (q + 1) * QB)
                    eng.dma_start(x2n[:, r, :, :], x2_dram[bass.ds((q + 2) * QB, QB)].rearrange("b p d -> p b d")
                                  ).then_inc(x2n_in[r], 16)
                eng.wait_ge(y3_set, (q + 1) * QB)
                eng.dma_start(out[bass.ds(q * QB, QB)].rearrange("b p d -> p b d"), y3[:, r, :, :]).then_inc(out_stored[r], 16)
            with eng.Fori(0, NQ // 2 - 1) as k:
                for r in range(2):
                    turn(k, r, True)
            for r in range(2):
                turn(NQ // 2 - 1, r, False)
            for r in range(2):
                eng.wait_ge(out_stored[r], 16 * (NQ // 2))

        @block.gpsimd
        def _(eng):
            eng.memset(neg_half[:, :], -0.5)
            eng.memset(zeros[:, :], 0.0)
            eng.memset(ones_row[:, :], 1.0)
            eng.memset(va[:, :, :, :], 1.0)
            eng.memset(kp[:, :, :, :, :], 0.0).then_inc(consts_set, 1)
            eng.wait_ge(consts_set, 1)

            def step(k, s, live):
                if live(2):
                    kk_, r = at(k, s, 2)
                    t = kk_ * 2 + r
                    eng.wait_ge(mv1_set, 2 * t + 2)
                    eng.tensor_tensor(rstd1[:, r, :], mv1[:, r, 1:2], neg_half[:, 0:1], ALU.pow).then_inc(rstd1_set, 1)
                if live(3):
                    kk_, r = at(k, s, 3)
                    t = kk_ * 2 + r
                    eng.wait_ge(mv2_set, 2 * t + 2)
                    eng.tensor_tensor(rstd2[:, r, :], mv2[:, r, 1:2], neg_half[:, 0:1], ALU.pow).then_inc(rstd2_set, 1)
                if live(6):
                    kk_, r = at(k, s, 6)
                    eng.wait_ge(pos_set, kk_ * 2 + r + 1)
                if live(2):
                    kk_, r = at(k, s, 2)
                    t = kk_ * 2 + r
                    eng.wait_ge(rot_a, t + 1)
                    eng.wait_ge(rot_b, t + 1)
                    after(eng, scx_made, t - 1)
                    swapped = rb[:, r, :, :].rearrange("p (q e) t -> p q e t", e=2)
                    into = rot[:, r, :, :].rearrange("p (q e) t -> p q e t", e=2)
                    plain = ra[:, r, :, :].rearrange("p (q e) t -> p q e t", e=2)
                    for e in range(2):
                        eng.tensor_tensor(into[:, :, e, :], plain[:, :, e, :], swapped[:, :, 1 - e, :],
                                          ALU.add).then_inc(rot_set, 1)
                if live(6):
                    kk_, r = at(k, s, 6)
                    for j in range(TOPK):
                        eng.indirect_dma_start(sent, bass.IndirectOffsetOnAxis(ap=pos[:, r, j:j + 1], axis=0),
                                               x2s[:, r, :], None).then_inc(sent_in[r], 16)

            phases(eng, step)
            eng.wait_ge(plan_step, 1)
            for e in range(NE):
                eng.indirect_dma_start(sent, bass.IndirectOffsetOnAxis(ap=tail_rows[:, e:e + 1], axis=0),
                                       zeros[:, :], None).then_inc(zeros_sent, 16)
            eng.dma_start(sent[IDLE_ROW:XROWS, :].rearrange("(n p) d -> p n d", p=P),
                          zeros[:, :].unsqueeze(1).broadcast_to([P, IDLE, D])).then_inc(idle_sent, 16)

            for r in range(2):
                eng.wait_ge(yg_out[r], 16 * (TILES // 2))
            def fetch(r):
                for b in range(QB):
                    for j in range(TOPK):
                        eng.indirect_dma_start(got[:, r, b, j, :], None, back,
                                               bass.IndirectOffsetOnAxis(ap=pos4[:, r, b, j:j + 1], axis=0)
                                               ).then_inc(got_in[r], 16)

            def root(q, r):
                eng.wait_ge(mv3_set, (q + 1) * (QB + 1))
                eng.tensor_tensor(rstd3[:, r, :], var3[:, r, :], neg_half[:, :], ALU.pow).then_inc(rstd3_set, 1)

            eng.wait_ge(pos4_set, TOPK)
            for r in range(2):
                fetch(r)
            with eng.Fori(0, NQ // 2 - 1) as k:
                for r in range(2):
                    q = 2 * k + r
                    eng.wait_ge(mix_c, (q + 1) * QB)
                    eng.wait_ge(pos4_set, q + 3)
                    root(q, r)
                    fetch(r)
            for r in range(2):
                root(NQ - 2 + r, r)

        @block.tensor
        def _(eng):
            eng.wait_ge(tables_in, 32)
            eng.wait_ge(w_in, 16)
            def prepare(g):
                for what, loaded, turned, bank0 in ((xin, xin_in, x_turned, 0), (cin, cin_in, c_turned, 4)):
                    eng.wait_ge(loaded, g * 16 + 16)
                    if bank0 == 0:
                        after(eng, kk_set, g * 4)
                    else:
                        after(eng, cTn_set, g * 4)
                    for j in range(4):
                        for i in range(4):
                            mm = eng.transpose(ps[:, bank0 + j, i * P:(i + 1) * P],
                                               what[:, 2 * j + i // 2, (i % 2) * P:(i % 2 + 1) * P], ident)
                        mm.then_inc(turned, 1)
                eng.wait_ge(xTu_set, g * 8 + 8)
                eng.wait_ge(xTn_set, g * 4 + 4)
                for j in range(4):
                    for i in range(2):
                        for c in range(DC):
                            mm = eng.matmul(ps[:, j, i * D:(i + 1) * D].rearrange("p (g c d) -> p g c d", c=2, d=DH),
                                            xTu[:, c, 2 * j + i, :, :].rearrange("p b i -> p (b i)"),
                                            wqkv_sb[:, c, D:2 * D].rearrange("p (c g d) -> p g c d", c=2, d=DH),
                                            start=(c == 0), stop=(c == DC - 1))
                    mm.then_inc(k_made, 1)
            groups(eng, prepare)
            eng.wait_ge(kk_set, 4 * NG)
            eng.wait_ge(cTn_set, 4 * NG)
            eng.wait_ge(xw_in, 48)
            eng.wait_ge(small_in, 96)
            eng.wait_ge(consts_set, 1)

            def project(k, s, lag):
                kk_, r = at(k, s, lag)
                t = kk_ * 2 + r
                eng.wait_ge(xT_in[r], kk_ * 16 + 16)
                after(eng, res2_set, t - 3)
                after(eng, q_set, t)
                after(eng, v_set, t)
                for m in range(DC):
                    for c in range(DC):
                        eng.matmul(QV[:, m * P:(m + 1) * P], wqkv_sb[:, c, m * P:(m + 1) * P], xT[:, r, c, :],
                                   start=(c == 0), stop=(c == DC - 1))
                for c in range(DC):
                    mm = eng.matmul(QV[:, D:2 * D], xT[:, r, c, :], wqkv_sb[:, c, 2 * D:3 * D],
                                    start=(c == 0), stop=(c == DC - 1))
                mm.then_inc(qv_made, 1)

            def scores(k, s, u):
                kk_, r = at(k, s, 0)
                t = kk_ * 2 + r
                if u == 0:
                    eng.wait_ge(q_set, t + 1)
                    eng.wait_ge(kp_in[r], kk_ * 128 + 128)
                after(eng, expd, t * 4 + u - 1)
                bank = SCORE[u % 2]
                eng.matmul(bank.rearrange("p (h j) -> p h j", j=P), ident_bf,
                           causal_bf.unsqueeze(1).broadcast_to([P, 4, P]), start=True, stop=False,
                           skip_group_check=True)
                for c in range(2):
                    for e in range(2):
                        n = 2 * c + e
                        mm = eng.matmul(bank[:, n * P:(n + 1) * P].rearrange("p (d u) -> p d u", u=NU),
                                        qT[32 * u:32 * u + 32, r, c, :],
                                        kp[32 * u:32 * u + 32, r, e, c * DH:(c + 1) * DH, :],
                                        start=False, stop=(n == 3), skip_group_check=True)
                mm.then_inc(scored, 1)

            def turn_probs(k, s, u):
                kk_, r = at(k, s, 1)
                t = kk_ * 2 + r
                eng.wait_ge(expd, t * 4 + u + 1)
                after(eng, (pT_even, pT_odd)[u % 2], t * 2 + u // 2)
                for n in range(4):
                    mm = eng.transpose(PROBT[u % 2][:, n * P:(n + 1) * P], prob[:, r, 4 * u + n, :], ident)
                mm.then_inc(p_turned, 1)

            def weigh(k, s, u):
                kk_, r = at(k, s, 1)
                t = kk_ * 2 + r
                eng.wait_ge((pT_even, pT_odd)[u % 2], t * 2 + u // 2 + 1)
                if u == 0:
                    eng.wait_ge(v_set, t + 1)
                    after(eng, att_set, t)
                for n in range(4):
                    h = (n // 2) * 8 + 2 * u + n % 2
                    mm = eng.matmul(HEADS[:, h, :], pT[:, u % 2, n, :], va[:, r, h, :], start=True, stop=True)
                mm.then_inc(heads_made, 1)

            def step(k, s, live):
                if live(0):
                    scores(k, s, 0)
                if live(1):
                    turn_probs(k, s, 0)
                if live(0):
                    scores(k, s, 1)
                if live(3):
                    kk_, r = at(k, s, 3)
                    t = kk_ * 2 + r
                    eng.wait_ge(scx_set, t + 1)
                    if isinstance(t, int) and t + 3 >= B:
                        pass
                    if not isinstance(t, int) or t + 3 < B:
                        eng.wait_ge(q_set, t + 4)
                        eng.wait_ge(v_set, t + 4)
                    else:
                        eng.wait_ge(q_set, B)
                        eng.wait_ge(v_set, B)
                    after(eng, res2_set, t)
                    eng.matmul(YX, scx[:, r, :], xv[:, r, :], start=True, stop=True).then_inc(yx_made, 1)
                if live(1):
                    turn_probs(k, s, 1)
                if live(2):
                    kk_, r = at(k, s, 2)
                    t = kk_ * 2 + r
                    eng.wait_ge(x1_set, t + 1)
                    after(eng, x1T_set, t)
                    after(eng, x2T_set, t - 1)
                    after(eng, gc_set, t - 2)
                    for c in range(DC):
                        mm = eng.transpose(TR[:, c * P:(c + 1) * P], x1[:, r, c * P:(c + 1) * P], ident)
                    mm.then_inc(x1_turned, 1)
                if live(1):
                    weigh(k, s, 0)
                if live(2):
                    kk_, r = at(k, s, 2)
                    t = kk_ * 2 + r
                    eng.wait_ge(cT_in[r], kk_ * 16 + 16)
                    after(eng, scx_set, t)
                    after(eng, rot_b, t)
                    after(eng, xv_set, t)
                    for m in range(2):
                        for c in range(DC):
                            eng.matmul(KQ[:, m, :], xwk_sb[:, c, m:D:2], cT[:, r, c, :],
                                       start=(c == 0), stop=(c == DC - 1))
                    for c in range(DC):
                        mm = eng.matmul(XV, cT[:, r, c, :], xwv_sb[:, c, :], start=(c == 0), stop=(c == DC - 1))
                    mm.then_inc(xkv_made, 1)
                if live(0):
                    scores(k, s, 2)
                if live(1):
                    turn_probs(k, s, 2)
                if live(2):
                    kk_, r = at(k, s, 2)
                    t = kk_ * 2 + r
                    eng.wait_ge(x1T_set, t + 1)
                    for m in range(2):
                        for c in range(DC):
                            mm = eng.matmul(KQ[:, 2 + m, :], xwq_sb[:, c, m:D:2], x1T[:, r, c, :],
                                            start=(c == 0), stop=(c == DC - 1))
                    mm.then_inc(xq_made, 1)
                if live(1):
                    weigh(k, s, 1)
                if live(-1):
                    project(k, s, -1)
                if live(0):
                    scores(k, s, 3)
                if live(1):
                    turn_probs(k, s, 3)
                    weigh(k, s, 2)
                if live(2):
                    kk_, r = at(k, s, 2)
                    t = kk_ * 2 + r
                    eng.wait_ge(rot_set, 2 * t + 2)
                    eng.wait_ge(xv_set, t + 1)
                    for m in range(2):
                        mm = eng.matmul(SCX, rot[:, r, m, :], rot[:, r, 2 + m, :], start=(m == 0), stop=(m == 1))
                    mm.then_inc(scx_made, 1)
                if live(1):
                    weigh(k, s, 3)
                if live(3) or live(4) or live(5):
                    n = 2 * k + s
                    after(eng, gc_set, n - 4)
                if live(3):
                    kk_, r = at(k, s, 3)
                    t = kk_ * 2 + r
                    eng.wait_ge(x2_set, t + 1)
                    after(eng, x2T_set, t)
                    for c in range(DC):
                        mm = eng.transpose(TR[:, c * P:(c + 1) * P], x2[:, r, c * P:(c + 1) * P], ident)
                if live(4):
                    kk_, r = at(k, s, 4)
                    eng.wait_ge(x2T_set, kk_ * 2 + r + 1)
                    eng.matmul(GATE[:, 0:NE], ones_row[:, :], gate_b_sb[:, :], start=True, stop=False)
                    for c in range(DC):
                        mm = eng.matmul(GATE[:, 0:NE], x2T[:, r, c, :], gate_w_sb[:, c, :], start=False, stop=(c == DC - 1))
                if live(5):
                    kk_, r = at(k, s, 5)
                    eng.wait_ge(picks_set, kk_ * 2 + r + 1)
                    eng.matmul(GATE[:, NE:2 * NE], before_bf, picks[:, r, :], start=True, stop=True)
                    mm = eng.matmul(GATE[:, 2 * NE:3 * NE], ones_bf, picks[:, r, :], start=True, stop=True)
                if live(3) or live(4) or live(5):
                    mm.then_inc(tail_made, 1)

            phases(eng, step)

            eng.wait_ge(gc_set, B + 1)
            eng.wait_ge(x2T_set, B)
            eng.wait_ge(ffn_in, 64)
            eng.wait_ge(bias_back, 16)
            eng.wait_ge(plan_step, PLAN_STEPS)
            XGT = ps[:, 2, 0:D]
            GHT = ps[:, 3, 0:FFN]

            def turn_x(i, slot, loads, r):
                eng.wait_ge(xg_in[slot], loads * 16)
                after(eng, xgT_set, i)
                for c in range(DC):
                    mm = eng.transpose(XGT[:, c * P:(c + 1) * P], xg[:, slot, c * P:(c + 1) * P], ident)
                mm.then_inc(xg_turned, 1)

            def turn_h(i, r):
                eng.wait_ge(gh_set, i + 1)
                after(eng, ghT_set, i)
                for c in range(FFN // P):
                    mm = eng.transpose(GHT[:, c * P:(c + 1) * P], gate_h[:, r, c * P:(c + 1) * P], ident)
                mm.then_inc(gh_turned, 1)

            def hidden(i, r, e):
                eng.wait_ge(xgT_set, i + 1)
                after(eng, gh_set, i - 1)
                eng.matmul(ps[:, r, :], ones_bf[0:3, :], bias_rows[0:3, bass.ds(e * (2 * FFN), 2 * FFN)],
                           start=True, stop=False)
                for c in range(DC):
                    mm = eng.matmul(ps[:, r, :], xgT[:, r, c, :],
                                    rw1_sb[:, bass.ds(e * (DC * 2 * FFN) + c * 2 * FFN, 2 * FFN)],
                                    start=False, stop=(c == DC - 1))
                mm.then_inc(hid_made, 1)

            def result(i, r, e):
                eng.wait_ge(ghT_set, i + 1)
                after(eng, yg_set, i - 1)
                eng.matmul(ps[:, 4 + r, 0:D], ones_bf[0:3, :], bias_rows[0:3, bass.ds(e * D + NE * 2 * FFN, D)],
                           start=True, stop=False)
                for c in range(FFN // P):
                    mm = eng.matmul(ps[:, 4 + r, 0:D], ghT[:, r, c, :],
                                    rw2_sb[:, bass.ds(e * (FFN // P * D) + c * D, D)],
                                    start=False, stop=(c == FFN // P - 1))
                mm.then_inc(yg_made, 1)

            def expert(i):
                return eng.value_load(tile_expert[0:1, bass.ds(i, 1)], min_val=0, max_val=NE - 1)

            def tiles(k, first=False, last=False, many=4):
                for n in range(many):
                    i = 4 * k + n
                    if not (first and n == 0):
                        turn_h(i - 1, (n - 1) % 2)
                    hidden(i, n % 2, expert(i))
                    if not (last and n == many - 1):
                        turn_x(i + 1, (n + 1) % 4, k + 1 + (n + 1) // 4, (n + 1) % 2)
                    if not (first and n == 0):
                        result(i - 1, (n - 1) % 2, expert(i - 1))

            turn_x(0, 0, 1, 0)
            tiles(0, first=True)
            with eng.Fori(1, TILES // 4 - 1) as k:
                tiles(k)
            tiles(TILES // 4 - 1, last=True)
            turn_h(TILES - 1, 1)
            result(TILES - 1, 1, expert(TILES - 1))

            eng.wait_ge(yg_set, TILES)

            def shared(q, k, r):
                eng.wait_ge(x2T4_in[r], k * 16 + 16)
                for f in range(FFN // P):
                    after(eng, sgh_set, (q - 1) * 2 + f + 1)
                    for half in range(2):
                        cols = half * FFN + f * P
                        for c in range(DC):
                            mm = eng.matmul(ps[:, 2 * f + half, :].rearrange("p (b t) -> p b t", b=QB),
                                            sw1_sb[:, c, cols:cols + P], x2T4[:, r, :, c, :],
                                            start=(c == 0), stop=(c == DC - 1))
                    mm.then_inc(shid_made, 1)

            def outputs(q, r):
                for b in range(QB):
                    if b == 0:
                        eng.wait_ge(sgh_set, 2 * q + 2)
                    after(eng, mix_a, (q - 1) * QB + b + 1)
                    eng.matmul(ps[:, 4 + b, 0:D], ones_bf[0:3, :], bias_rows[0:3, NBIAS - D:NBIAS], start=True, stop=False)
                    for c in range(FFN // P):
                        mm = eng.matmul(ps[:, 4 + b, 0:D], sgh[:, r, c, b * P:(b + 1) * P], sw2_sb[:, c, :],
                                        start=False, stop=(c == FFN // P - 1))
                    mm.then_inc(sy_made, 1)

            shared(0, 0, 0)
            shared(1, 0, 1)
            outputs(0, 0)
            with eng.Fori(1, NQ // 2) as k:
                for r in range(2):
                    shared(2 * k + r, k, r)
                    outputs(2 * k + r - 1, 1 - r)
            outputs(NQ - 1, 1)

        @block.scalar
        def _(eng):
            def prepare(g):
                after(eng, xT_stored, g * 16)
                for j in range(4):
                    eng.wait_ge(x_turned, g * 4 + j + 1)
                    eng.copy(xTn[:, 2 * j:2 * j + 2, :, :].rearrange("p b c t -> p (b c t)"), ps[:, j, :]).then_inc(xTn_set, 1)
                after(eng, cT_stored, g * 16)
                for j in range(4):
                    eng.wait_ge(c_turned, g * 4 + j + 1)
                    eng.copy(cTn[:, 2 * j:2 * j + 2, :, :].rearrange("p b c t -> p (b c t)"), ps[:, 4 + j, :]).then_inc(cTn_set, 1)

            groups(eng, prepare)

            def exps(k, s, u):
                kk_, r = at(k, s, 0)
                t = kk_ * 2 + r
                eng.wait_ge(maxed, t * 4 + u + 1)
                after(eng, p_turned, (t - 2) * 4 + u + 1)
                for n in range(4):
                    ins = eng.activation(prob[:, r, 4 * u + n, :], SCORE[u % 2][:, n * P:(n + 1) * P], ACT.Exp,
                                         bias=nmax[:, r, 4 * u + n:4 * u + n + 1])
                ins.then_inc(expd, 1)

            def out_probs(k, s, u):
                kk_, r = at(k, s, 1)
                t = kk_ * 2 + r
                eng.wait_ge(p_turned, t * 4 + u + 1)
                after(eng, heads_made, t * 4 + u - 1)
                eng.copy(pT[:, u % 2, :, :].rearrange("p n t -> p (n t)"), PROBT[u % 2]).then_inc(pT_even, 1)

            def step(k, s, live):
                if live(0):
                    exps(k, s, 0)
                if live(1):
                    out_probs(k, s, 0)
                if live(0):
                    exps(k, s, 1)
                if live(5):
                    kk_, r = at(k, s, 5)
                    eng.wait_ge(lmax_set, kk_ * 2 + r + 1)
                    eng.activation(gexp[:, r, :], gc[:, r, 0:NE], ACT.Exp, bias=lmax[:, r, :],
                                   accum_out=gsum[:, r, :]).then_inc(gexp_set, 1)
                if live(2):
                    kk_, r = at(k, s, 2)
                    t = kk_ * 2 + r
                    eng.wait_ge(x1_turned, t + 1)
                    after(eng, xq_made, t - 1)
                    eng.copy(x1T[:, r, :, :].rearrange("p c t -> p (c t)"), TR).then_inc(x1T_set, 1)
                if live(2):
                    kk_, r = at(k, s, 2)
                    t = kk_ * 2 + r
                    eng.wait_ge(xkv_made, t + 1)
                    after(eng, yx_made, t - 1)
                    eng.copy(xv[:, r, :], XV).then_inc(xv_set, 1)
                if live(0):
                    exps(k, s, 2)
                if live(1):
                    out_probs(k, s, 2)
                if live(-1):
                    kk_, r = at(k, s, -1)
                    t = kk_ * 2 + r
                    eng.wait_ge(qv_made, t + 1)
                    after(eng, scored, (t - 1) * 4)
                    eng.mul(qT[:, r, :, :].rearrange("p c t -> p (c t)"), QV[:, 0:D], 1.0 / np.sqrt(DH)).then_inc(q_set, 1)
                if live(0):
                    exps(k, s, 3)
                if live(3):
                    kk_, r = at(k, s, 3)
                    t = kk_ * 2 + r
                    eng.wait_ge(tail_made, t + 1)
                    after(eng, x2T_stored[r], kk_ * 16)
                    eng.copy(x2T[:, r, :, :].rearrange("p c t -> p (c t)"), TR).then_inc(x2T_set, 1)

            phases(eng, step)

            eng.wait_ge(plan_step, PLAN_STEPS)
            for r in range(2):
                eng.wait_ge(sent_in[r], 32 * (B // 2))
            eng.wait_ge(zeros_sent, 16 * NE)
            eng.wait_ge(idle_sent, 16)

            def first_row(i):
                return eng.value_load(tile_row[0:1, bass.ds(i, 1)], min_val=0, max_val=XROWS - P)

            def load(i, slot):
                after(eng, xg_turned, i - 3)
                eng.dma_start(xg[:, slot, :], sent[bass.ds(first_row(i), P), :]).then_inc(xg_in[slot], 16)

            def silu(i, r):
                eng.wait_ge(hid_made, i + 1)
                after(eng, gh_set, i - 1)
                eng.activation(sil[:, r, :], ps[:, r, 0:FFN], ACT.Silu).then_inc(sil_set, 1)

            def out_x(i, r):
                eng.wait_ge(xg_turned, i + 1)
                after(eng, hid_made, i - 1)
                eng.copy(xgT[:, r, :, :].rearrange("p c t -> p (c t)"), ps[:, 2, 0:D]).then_inc(xgT_set, 1)

            def out_y(i, r, k):
                eng.wait_ge(yg_made, i + 1)
                after(eng, yg_out[r], k * 16)
                eng.copy(yg[:, r, :], ps[:, 4 + r, 0:D]).then_inc(yg_set, 1)
                eng.wait_ge(yg_set, i + 1)
                eng.dma_start(back[bass.ds(i * P, P), :], yg[:, r, :]).then_inc(yg_out[r], 16)

            def tiles(k, first=False, last=False):
                for n in range(4):
                    i = 4 * k + n
                    silu(i, n % 2)
                    if not (last and n == 3):
                        out_x(i + 1, (n + 1) % 2)
                    if not (first and n == 0):
                        out_y(i - 1, (n - 1) % 2, 2 * k + (n - 1) // 2)
                    if not (last and n > 0):
                        load(i + 3, (n + 3) % 4)

            for i in range(3):
                load(i, i)
            out_x(0, 0)
            tiles(0, first=True)
            with eng.Fori(1, TILES // 4 - 1) as k:
                tiles(k)
            tiles(TILES // 4 - 1, last=True)
            out_y(TILES - 1, 1, TILES // 2 - 1)

            def shared(q, r):
                for f in range(FFN // P):
                    eng.wait_ge(shid_made, 2 * q + f + 1)
                    after(eng, sgh_set, (q - 2) * 2 + f + 1)
                    eng.activation(ssil[:, r, f, :], ps[:, 2 * f, :], ACT.Silu, bias=sb1_sb[:, f:f + 1]).then_inc(ssil_set, 1)

            for r in range(2):
                shared(r, r)
            with eng.Fori(1, NQ // 2) as k:
                for r in range(2):
                    shared(2 * k + r, r)

        @block.vector
        def _(eng):
            def prepare(g):
                after(eng, k_made, g * 4)
                for j in range(4):
                    eng.wait_ge(xTn_set, g * 4 + j + 1)
                    for i in range(2):
                        eng.tensor_copy(xTu[:, :, :, 2 * j + i, :],
                                        ps[:, j, i * D:(i + 1) * D].rearrange("p (c u i) -> p c u i", c=DC, i=DH)
                                        ).then_inc(xTu_set, 1)
                after(eng, k_stored, g * 16)
                for j in range(4):
                    eng.wait_ge(k_made, g * 4 + j + 1)
                    eng.tensor_copy(kk[:, :, :, 2 * j:2 * j + 2].rearrange("p g a u -> p u (g a)"),
                                    ps[:, j, :].rearrange("p (u a) -> p u a", u=2)).then_inc(kk_set, 1)
            groups(eng, prepare)
            eng.wait_ge(small_in, 96)
            eng.wait_ge(tables_in, 32)
            eng.tensor_copy(bias_parts[:, 0, :], bias_in[:, :]).then_inc(bias_split, 1)
            for n in range(2):
                eng.wait_ge(bias_split, 2 * n + 1)
                left = bias_left[:, n, :]
                eng.tensor_tensor(left, (bias_in[:, :], bias_left[:, 0, :])[n], bias_parts[:, n, :], ALU.subtract).then_inc(bias_split, 1)
                eng.wait_ge(bias_split, 2 * n + 2)
                eng.tensor_copy(bias_parts[:, n + 1, :], left).then_inc(bias_split, 1)
            eng.tensor_copy(base[:, :], region_rows).then_inc(base_set, 1)
            eng.wait_ge(consts_set, 1)

            def maxes(k, s, u):
                kk_, r = at(k, s, 0)
                t = kk_ * 2 + r
                eng.wait_ge(scored, t * 4 + u + 1)
                after(eng, expd, (t - 2) * 4 + u + 1)
                eng.tensor_reduce(nmax[:, r, 4 * u:4 * u + 4], SCORE[u % 2].rearrange("p (h j) -> p h j", j=P),
                                  AX_X, ALU.max, negate=True).then_inc(maxed, 1)

            def out_probs(k, s, u):
                kk_, r = at(k, s, 1)
                t = kk_ * 2 + r
                eng.wait_ge(p_turned, t * 4 + u + 1)
                after(eng, heads_made, t * 4 + u - 1)
                eng.tensor_copy(pT[:, u % 2, :, :].rearrange("p n t -> p (n t)"), PROBT[u % 2]).then_inc(pT_odd, 1)

            def stats(t, r, res, bn, res_set, bn_set):
                eng.wait_ge(res_set, t + 1)
                eng.bn_stats(bn[:, r, :], res[:, r, :]).then_inc(bn_set, 1)

            def moments(t, r, bn, mv, mv_set):
                eng.bn_aggr(mv[:, r, :], bn[:, r, :]).then_inc(mv_set, 1)
                eng.wait_ge(mv_set, 2 * t + 1)
                eng.tensor_scalar(mv[:, r, 1:2], mv[:, r, 1:2], EPS, None, ALU.add).then_inc(mv_set, 1)

            def step(k, s, live):
                k2, r2 = at(k, s, 2)
                t2 = k2 * 2 + r2
                k3, r3 = at(k, s, 3)
                t3 = k3 * 2 + r3
                if live(5):
                    k5, r5 = at(k, s, 5)
                    t5 = k5 * 2 + r5
                    eng.wait_ge(gc_set, t5 + 1)
                    after(eng, gexp_set, t5 - 1)
                    eng.tensor_reduce(lmax[:, r5, :], gc[:, r5, 0:NE], AX_X, ALU.max, negate=True).then_inc(lmax_set, 1)
                if live(0):
                    maxes(k, s, 0)
                if live(2):
                    eng.wait_ge(heads_made, 4 * t2 + 4)
                    eng.reciprocal(rden[:, r2, :], HEADS[:, :, DH]).then_inc(den_set, 1)
                    eng.wait_ge(den_set, t2 + 1)
                    eng.tensor_tensor(att[:, r2, :].rearrange("p (h d) -> p h d", d=DH), HEADS[:, :, 0:DH],
                                      rden[:, r2, :].unsqueeze(2).broadcast_to([P, H, DH]), ALU.mult).then_inc(att_set, 1)
                    eng.wait_ge(att_set, t2 + 1)
                    eng.wait_ge(xn_in[r2], k2 * 16 + 16)
                    after(eng, x1_set, t2 - 1)
                    eng.tensor_tensor(res1[:, r2, :], att[:, r2, :], xn[:, r2, :], ALU.add).then_inc(res1_set, 1)
                    stats(t2, r2, res1, bn1, res1_set, bn1_set)
                    eng.wait_ge(bn1_set, t2 + 1)
                if live(0):
                    maxes(k, s, 1)
                if live(2):
                    moments(t2, r2, bn1, mv1, mv1_set)
                if live(3):
                    eng.wait_ge(yx_made, t3 + 1)
                    eng.tensor_tensor(res2[:, r3, :], YX, x1[:, r3, :], ALU.add).then_inc(res2_set, 1)
                    stats(t3, r3, res2, bn2, res2_set, bn2_set)
                    eng.wait_ge(bn2_set, t3 + 1)
                if live(2):
                    kk_, r = at(k, s, 2)
                    t = kk_ * 2 + r
                    eng.wait_ge(rstd1_set, t + 1)
                    after(eng, x1_turned, t - 1)
                    after(eng, res2_set, t - 1)
                    eng.tensor_scalar(x1[:, r, :], res1[:, r, :], mv1[:, r, 0:1], rstd1[:, r, :],
                                      ALU.subtract, ALU.mult).then_inc(x1_set, 1)
                if live(3):
                    moments(t3, r3, bn2, mv2, mv2_set)
                if live(1):
                    out_probs(k, s, 1)
                if live(3):
                    kk_, r = at(k, s, 3)
                    t = kk_ * 2 + r
                    eng.wait_ge(rstd2_set, t + 1)
                    after(eng, x2_stored[r], kk_ * 16)
                    after(eng, x2s_set, t - 1)
                    after(eng, tail_made, t - 1)
                    eng.tensor_scalar(x2[:, r, :], res2[:, r, :], mv2[:, r, 0:1], rstd2[:, r, :],
                                      ALU.subtract, ALU.mult).then_inc(x2_set, 1)
                if live(0):
                    maxes(k, s, 2)
                if live(6):
                    k6, r6 = at(k, s, 6)
                    t6 = k6 * 2 + r6
                if live(5):
                    eng.wait_ge(gexp_set, t5 + 1)
                    eng.reciprocal(ginv[:, r5, :], gsum[:, r5, :]).then_inc(ginv_set, 1)
                    eng.wait_ge(ginv_set, t5 + 1)
                    eng.tensor_scalar(gprob[:, r5, :], gexp[:, r5, :], ginv[:, r5, :], None, ALU.mult).then_inc(gprob_set, 1)
                    eng.wait_ge(gprob_set, t5 + 1)
                if live(6):
                    eng.wait_ge(gc_set, t6 + 2)
                    eng.wait_ge(base_set, t6 + 1)
                    eng.tensor_tensor(place[:, r6, :], gc[:, 1 - r6, NE:2 * NE], base[:, :], ALU.add).then_inc(place_set, 1)
                if live(5):
                    eng.max(top_p[:, r5, :], gprob[:, r5, :]).then_inc(top_p_set, 1)
                    eng.wait_ge(top_p_set, t5 + 1)
                if live(6):
                    eng.wait_ge(place_set, t6 + 1)
                    eng.tensor_tensor(mine[:, r6, :, :], pick[:, r6, :, :],
                                      place[:, r6, :].unsqueeze(1).broadcast_to([P, TOPK, NE]), ALU.mult).then_inc(mine_set, 1)
                if live(5):
                    eng.max_index(top_i[:, r5, :], top_p[:, r5, :], gprob[:, r5, :]).then_inc(top_i_set, 1)
                if live(6):
                    eng.wait_ge(mine_set, t6 + 1)
                    after(eng, sent_in[r6], k6 * 32)
                    with nc.allow_low_precision(reason="a whole number below 2**24, summed in float32: exact"):
                        eng.tensor_reduce(pos[:, r6, :], mine[:, r6, :, :], AX_X, ALU.add).then_inc(pos_set, 1)
                    eng.tensor_tensor(base[:, :], base[:, :], gc[:, 1 - r6, 2 * NE:3 * NE], ALU.add).then_inc(base_set, 1)
                    eng.wait_ge(pos_set, t6 + 1)
                    eng.tensor_scalar(pos_all[:, t6, :], pos[:, r6, :], 0.0, None, ALU.add).then_inc(kept_set, 1)
                if live(5):
                    eng.tensor_scalar(cw_all[:, t5, :], top_p[:, r5, 0:TOPK], 1.0, None, ALU.mult).then_inc(kept_set, 1)
                    eng.wait_ge(top_i_set, t5 + 1)
                    eng.tensor_copy(top_f[:, r5, :], top_i[:, r5, 0:TOPK]).then_inc(top_f_set, 1)
                    eng.wait_ge(top_f_set, t5 + 1)
                    eng.tensor_tensor(pick[:, r5, :, :], expert_ids.unsqueeze(1).broadcast_to([P, TOPK, NE]),
                                      top_f[:, r5, :].unsqueeze(2).broadcast_to([P, TOPK, NE]), ALU.is_equal).then_inc(pick_set, 1)
                    eng.wait_ge(pick_set, t5 + 1)
                    eng.tensor_scalar(pick_all[:, t5, :, :], pick[:, r5, :, :], 1.0, None, ALU.mult).then_inc(kept_set, 1)
                    after(eng, tail_made, t5 + 1)
                    eng.tensor_tensor(picks[:, r5, :], pick[:, r5, 0, :], pick[:, r5, 1, :], ALU.add).then_inc(picks_set, 1)
                if live(2):
                    kk_, r = at(k, s, 2)
                    t = kk_ * 2 + r
                    eng.wait_ge(xv_set, t + 1)
                    eng.wait_ge(xq_made, t + 1)
                    after(eng, rot_set, 2 * (t - 1))
                    eng.tensor_tensor(ra[:, r, :, :], KQ, rot_cos, ALU.mult).then_inc(rot_a, 1)
                    eng.tensor_tensor(rb[:, r, :, :], KQ, rot_sin, ALU.mult).then_inc(rot_b, 1)
                if live(0):
                    maxes(k, s, 3)
                if live(1):
                    out_probs(k, s, 3)
                if live(2):
                    kk_, r = at(k, s, 2)
                    t = kk_ * 2 + r
                    eng.wait_ge(scx_made, t + 1)
                    after(eng, yx_made, t - 1)
                    eng.tensor_tensor(scx[:, r, :], SCX, decay, ALU.mult).then_inc(scx_set, 1)
                if live(-1):
                    kk_, r = at(k, s, -1)
                    t = kk_ * 2 + r
                    eng.wait_ge(q_set, t + 1)
                    after(eng, heads_made, 4 * (t - 1))
                    eng.tensor_copy(va[:, r, :, 0:DH], QV[:, D:2 * D].rearrange("p (h d) -> p h d", d=DH)).then_inc(v_set, 1)

                if live(4) or live(5):
                    n = 2 * k + s
                    if live(3):
                        eng.wait_ge(x2T_set, n - 2)
                    else:
                        eng.wait_ge(tail_made, n - 2)
                    lo, hi = (0 if live(4) else NE), (3 * NE if live(5) else NE)
                    eng.tensor_copy(gc[:, s, lo:hi], GATE[:, lo:hi]).then_inc(gc_set, 1)
                if live(4):
                    k4, r4 = at(k, s, 4)
                    after(eng, sent_in[r4], k4 * 32)
                    eng.tensor_copy(x2s[:, r4, :], x2[:, r4, :]).then_inc(x2s_set, 1)

            phases(eng, step)

            steps = [0]

            def planned(ins):
                steps[0] += 1
                ins.then_inc(plan_step, 1)
                eng.wait_ge(plan_step, steps[0])

            eng.wait_ge(base_set, B + 1)
            planned(eng.tensor_scalar(tail_rows[:, :], base[:, :], lane_id, None, ALU.add))
            planned(eng.tensor_tensor(counts[:, 0, :], base[:, :], region_rows, ALU.subtract))
            planned(eng.tensor_scalar(counts_i[:, 0, :], counts[:, 0, :], float(P - 1), None, ALU.add))
            planned(eng.tensor_scalar(counts_i[:, 1, :], counts_i[:, 0, :], P.bit_length() - 1, None, ALU.arith_shift_right))
            planned(eng.tensor_copy(counts[:, 1, :], counts_i[:, 1, :]))
            planned(eng.tensor_tensor(upto[:, :, :], counts[:, 1, :].unsqueeze(1).broadcast_to([P, NE, NE]),
                                      not_later, ALU.mult))
            planned(eng.tensor_reduce(counts[:, 2, :], upto[:, :, :], AX_X, ALU.add))
            planned(eng.tensor_scalar(counts[:, 3, :], counts[:, 1, :], -float(P), float(REGION), ALU.mult, ALU.add))
            planned(eng.tensor_tensor(counts[:, 0, :], counts[:, 2, :], counts[:, 1, :], ALU.subtract))
            planned(eng.tensor_scalar(shifts[:, :], counts[:, 0, :], float(P), None, ALU.mult))
            planned(eng.tensor_tensor(shifts[:, :], shifts[:, :], region_rows, ALU.subtract))
            planned(eng.tensor_tensor(shifted[:, :, :, :].rearrange("p b j e -> p (b j) e"),
                                      pick_all[:, :, :, :].rearrange("p b j e -> p (b j) e"),
                                      shifts[:, :].unsqueeze(1).broadcast_to([P, B * TOPK, NE]), ALU.mult))
            planned(eng.tensor_reduce(shift[:, :, :], shifted[:, :, :, :], AX_X, ALU.add))
            planned(eng.tensor_tensor(back_rows[:, :, :], shift[:, :, :], pos_all[:, :, :], ALU.add))
            planned(eng.tensor_tensor(passed[:, :, :], counts[0:1, 2, :].unsqueeze(1).broadcast_to([1, TILES, NE]),
                                      tile_ids[0:1, :].unsqueeze(2).broadcast_to([1, TILES, NE]), ALU.is_le))
            planned(eng.tensor_reduce(tile_f[:, 0, :], passed[:, :, :], AX_X, ALU.add))
            planned(eng.tensor_scalar(tile_expert[:, :], tile_f[:, 0, :], float(NE - 1), None, ALU.min))
            planned(eng.tensor_tensor(skipped[:, :, :], passed[:, :, :],
                                      counts[0:1, 3, :].unsqueeze(1).broadcast_to([1, TILES, NE]), ALU.mult))
            planned(eng.tensor_reduce(tile_f[:, 1, :], skipped[:, :, :], AX_X, ALU.add))
            planned(eng.tensor_tensor(tile_row[:, :], tile_f[:, 1, :], tile_rows[0:1, :], ALU.add))
            assert steps[0] == PLAN_STEPS

            def product(i, r):
                eng.wait_ge(sil_set, i + 1)
                after(eng, gh_turned, i - 1)
                eng.tensor_tensor(gate_h[:, r, :], ps[:, r, FFN:2 * FFN], sil[:, r, :], ALU.mult).then_inc(gh_set, 1)

            def out_h(i, r):
                eng.wait_ge(gh_turned, i + 1)
                after(eng, yg_made, i - 1)
                eng.tensor_copy(ghT[:, r, :, :].rearrange("p c t -> p (c t)"), ps[:, 3, 0:FFN]).then_inc(ghT_set, 1)

            product(0, 0)
            out_h(0, 0)
            product(1, 1)
            out_h(1, 1)
            with eng.Fori(1, TILES // 2) as k:
                for r in range(2):
                    product(2 * k + r, r)
                    out_h(2 * k + r, r)

            for r in range(2):
                eng.wait_ge(yg_out[r], 16 * (TILES // 2))

            def indices(q, r):
                eng.tensor_scalar(pos4[:, r, :, :], back_rows[:, bass.ds(q * QB, QB), :], 0.0, None, ALU.add).then_inc(pos4_set, 1)

            def shared(q, r):
                for f in range(FFN // P):
                    eng.wait_ge(ssil_set, 2 * q + f + 1)
                    after(eng, sy_made, (q - 1) * QB)
                    eng.scalar_tensor_tensor(out=sgh[:, r, f, :], in0=ps[:, 2 * f + 1, :],
                                             scalar=sb1_sb[:, 2 + f:3 + f], in1=ssil[:, r, f, :],
                                             op0=ALU.add, op1=ALU.mult).then_inc(sgh_set, 1)

            def mix(q, k, r):
                eng.tensor_scalar(cw4[:, r, :, :], cw_all[:, bass.ds(q * QB, QB), :], 1.0, None, ALU.mult).then_inc(cw4_set, 1)
                eng.wait_ge(x2n_in[r], k * 16 + 16)
                eng.wait_ge(got_in[r], (k + 1) * (QB * TOPK * 16))
                for b in range(QB):
                    n = q * QB + b + 1
                    eng.wait_ge(sy_made, n)
                    eng.tensor_tensor(ya[:, r, b, :], ps[:, 4 + b, 0:D], x2n[:, r, b, :], ALU.add).then_inc(mix_a, 1)
                for b in range(QB):
                    n = q * QB + b + 1
                    if b == 0:
                        eng.wait_ge(cw4_set, q + 1)
                    eng.wait_ge(mix_a, n)
                    eng.scalar_tensor_tensor(out=yb[:, r, b, :], in0=got[:, r, b, 0, :], scalar=cw4[:, r, b, 0:1],
                                             in1=ya[:, r, b, :], op0=ALU.mult, op1=ALU.add).then_inc(mix_b, 1)
                for b in range(QB):
                    n = q * QB + b + 1
                    eng.wait_ge(mix_b, n)
                    eng.scalar_tensor_tensor(out=ya[:, r, b, :], in0=got[:, r, b, 1, :], scalar=cw4[:, r, b, 1:2],
                                             in1=yb[:, r, b, :], op0=ALU.mult, op1=ALU.add).then_inc(mix_c, 1)
                for b in range(QB):
                    eng.wait_ge(mix_c, q * QB + b + 1)
                    eng.bn_stats(bn3[:, r, b, :], ya[:, r, b, :]).then_inc(bn3_set, 1)

            def finish(q, k, r):
                for b in range(QB):
                    eng.bn_aggr(mv3[:, r, b, :], bn3[:, r, b, :]).then_inc(mv3_set, 1)
                eng.wait_ge(mv3_set, (q + 1) * QB + q)
                after(eng, rstd3_set, q - 1)
                eng.tensor_scalar(var3[:, r, :], mv3[:, r, :, 1], EPS, None, ALU.add).then_inc(mv3_set, 1)
                eng.wait_ge(rstd3_set, q + 1)
                after(eng, out_stored[r], k * 16)
                for b in range(QB):
                    eng.tensor_scalar(y3[:, r, b, :], ya[:, r, b, :], mv3[:, r, b, 0:1], rstd3[:, r, b:b + 1],
                                      ALU.subtract, ALU.mult).then_inc(y3_set, 1)

            def close(q, k, r, more):
                mix(q, k, r)
                eng.wait_ge(bn3_set, (q + 1) * QB)
                if more:
                    indices(q + 2, r)
                    shared(q + 2, r)
                finish(q, k, r)

            for r in range(2):
                indices(r, r)
            for r in range(2):
                shared(r, r)
            for r in range(2):
                close(r, 0, r, True)
            with eng.Fori(1, NQ // 2 - 1) as k:
                for r in range(2):
                    close(2 * k + r, k, r, True)
            for r in range(2):
                close(NQ - 2 + r, NQ // 2 - 1, r, False)


_INS = ['x', 'ctx_1024', 'L0_attn_qkv_weights', 'L0_xattn_Wq', 'L0_xattn_Wk', 'L0_xattn_Wv', 'L0_ffn_gate_w',
        'L0_ffn_gate_b', 'L0_ffn_sw1', 'L0_ffn_sb1', 'L0_ffn_sw2', 'L0_ffn_sb2', 'L0_ffn_rw1', 'L0_ffn_rb1',
        'L0_ffn_rw2', 'L0_ffn_rb2']


def kernel(**inputs):
    import concourse.bacc as _bacc
    from concourse.bass_utils import run_bass_kernel_spmd as _run
    import ml_dtypes

    nc = _bacc.Bacc("TRN2", target_bir_lowering=False, num_devices=1)
    arrays = {name: np.ascontiguousarray(inputs[name]) for name in _INS}
    table_f32, table_bf16 = shape_tables()
    arrays["table_f32"] = table_f32
    arrays["table_bf16"] = table_bf16.astype(ml_dtypes.bfloat16)
    args = [nc.dram_tensor(f"in_{name}", a.shape, mybir.dt.from_np(a.dtype), kind="ExternalInput").ap()
            for name, a in arrays.items()]
    out = nc.dram_tensor("out_0", (B, S, D), F32, kind="ExternalOutput").ap()
    decoder_kernel(nc, *args, out)
    r = _run(nc, [{f"in_{name}": a for name, a in arrays.items()}], core_ids=[0])
    return r.results[0]["out_0"]
```

```python
from contextlib import ExitStack

import numpy as np
import concourse.bass as bass
from concourse import mybir

F32 = mybir.dt.float32
BF16 = mybir.dt.bfloat16
U32 = mybir.dt.uint32
I32 = mybir.dt.int32
ALU = mybir.AluOpType
ACT = mybir.ActivationFunctionType
AX_X = mybir.AxisListType.X

P = 128
B, S, D = 32, 128, 256
DC = D // P
H, DH = 16, 16
NU = S // DH
GB = P // DH
NG = B // GB
NE, TOPK, FFN = 8, 2, 256
VW = 32
CG = P // VW
BANK = 512
REGION = B * S + P
NTILE = B * S * TOPK // P + NE - 1
TILES = NTILE + NTILE % 2
IDLE_ROW = NE * REGION
IDLE = TILES - B * S * TOPK // P
XROWS = IDLE_ROW + IDLE * P
QB = 4
NQ = B // QB
EPS = 1e-5
NEG_INF = -1000000000.0
GAMMA, THETA, SCALE_BASE = 0.96875, 10000.0, 512.0

assert S == P and GB * DH == P and H * DH == D


def shape_tables():
    i = np.arange(P)
    ident = np.eye(P, dtype=np.float32)
    causal = np.where(i[None, :] <= i[:, None], 0.0, NEG_INF).astype(np.float32)
    diff = (i[None, :] - i[:, None]).astype(np.float64)
    decay = np.where(diff >= 0, GAMMA ** np.maximum(diff, 0), 0.0).astype(np.float32)
    half = D // 2
    pos = i.astype(np.float32)
    scale_vec = (np.arange(0, D, 2, dtype=np.float32) + np.float32(0.4 * D)) / np.float32(1.4 * D)
    scale = scale_vec[:, None] ** (pos / np.float32(SCALE_BASE))[None, :]
    freqs = (1.0 / THETA ** (np.arange(half, dtype=np.float32) / half)).astype(np.float32)
    angle = freqs[:, None] * pos[None, :]
    cos, sin = np.cos(angle), np.sin(angle)
    kc, ks, qc, qs = cos / scale, sin / scale, cos * scale, sin * scale
    rot_cos = np.concatenate([kc, kc, qc, qc], 1)
    rot_sin = np.concatenate([ks, -ks, qs, -qs], 1)
    f32 = np.concatenate([ident, decay, rot_cos, rot_sin,
                          np.tile(np.arange(NE), (P, 1)), np.tile(np.arange(NE) * REGION, (P, 1)),
                          i[:, None], np.tile((np.arange(NE)[None, :] <= np.arange(NE)[:, None]).reshape(-1), (P, 1)),
                          np.tile(np.arange(TILES), (P, 1)), np.tile(np.arange(TILES) * P, (P, 1))], 1)
    before = (i[:, None] < i[None, :]).astype(np.float32)
    bf = np.concatenate([ident, causal, before, np.ones((P, P))], 1)
    return np.ascontiguousarray(f32, np.float32), np.ascontiguousarray(bf, np.float32)


def at(k, s, lag):
    off = s - lag
    return k + off // 2, off % 2


def decoder_kernel(nc, x, ctx_1024, wqkv, xwq, xwk, xwv, gate_w, gate_b, sw1, sb1, sw2, sb2,
                   rw1, rb1, rw2, rb2, table_f32, table_bf16, out):
    ctx = ExitStack()
    with ctx:
        def sb(name, shape, dt=F32):
            return ctx.enter_context(nc.sbuf_tensor(name, shape, dt))

        def sem(name):
            return ctx.enter_context(nc.semaphore(name))

        xT_dram = nc.dram_tensor("xT_dram", (B, P, DC, P), F32).ap()
        cT_dram = nc.dram_tensor("cT_dram", (B, P, DC, P), F32).ap()
        k_dram = nc.dram_tensor("k_dram", (B, DH, GB, 2 * DH * NU), F32).ap()

        x2_dram = nc.dram_tensor("x2_dram", (B, P, D), F32).ap()
        x2T_dram = nc.dram_tensor("x2T_dram", (B, P, DC, P), F32).ap()
        sent = nc.dram_tensor("sent", (XROWS, D), F32).ap()
        back = nc.dram_tensor("back", (TILES * P, D), F32).ap()
        NBIAS = NE * 2 * FFN + NE * D + D
        bias_dram = nc.dram_tensor("bias_dram", (3, NBIAS), BF16).ap()

        ps = ctx.enter_context(nc.psum_tensor("ps", [P, 8, BANK], F32))
        SCORE = [ps[:, 0, :], ps[:, 1, :]]
        PROBT = ps[:, 2, :]
        HEADS = ps[:, 3, :].rearrange("p (h v) -> p h v", v=VW)
        HEADS_T = ps[:, 4, :].rearrange("p (x t) -> p x t", t=P)
        QV = ps[:, 5, :]
        YX = ps[:, 5, 0:D]
        XV = ps[:, 6, 0:D]
        SCX = ps[:, 6, 0:P]
        KQ = ps[:, 6:8, :].rearrange("p b c -> p (b c)")[:, D:3 * D].rearrange("p (r t) -> p r t", t=P)
        TR = ps[:, 7, D:2 * D]
        GATE = ps[:, 7, 0:3 * NE]

        tf = sb("tf", [P, 10 * P + 2 * NE + 1 + NE * NE + 2 * TILES])
        ident = tf[:, 0:P]
        decay = tf[:, P:2 * P]
        rot_cos = tf[:, 2 * P:6 * P].rearrange("p (r t) -> p r t", t=P)
        rot_sin = tf[:, 6 * P:10 * P].rearrange("p (r t) -> p r t", t=P)
        o = 10 * P
        expert_ids = tf[:, o:o + NE]
        region_rows = tf[:, o + NE:o + 2 * NE]
        lane_id = tf[:, o + 2 * NE:o + 2 * NE + 1]
        o += 2 * NE + 1
        not_later = tf[:, o:o + NE * NE].rearrange("p (e f) -> p e f", f=NE)
        o += NE * NE
        tile_ids = tf[:, o:o + TILES]
        tile_rows = tf[:, o + TILES:o + 2 * TILES]
        tb = sb("tb", [P, 4 * P], BF16)
        before_bf = tb[:, 2 * P:3 * P]
        ones_bf = tb[:, 3 * P:4 * P]
        ident_bf = tb[:, 0:P]
        causal_bf = tb[:, P:2 * P]
        wqkv_sb = sb("wqkv_sb", [P, DC, 3 * D])
        xwq_sb = sb("xwq_sb", [P, DC, D])
        xwk_sb = sb("xwk_sb", [P, DC, D])
        xwv_sb = sb("xwv_sb", [P, DC, D])

        gate_w_sb = sb("gate_w_sb", [P, DC, NE])
        gate_b_sb = sb("gate_b_sb", [P, 3 * NE])
        sw1_sb = sb("sw1_sb", [P, DC, 2 * FFN])
        sw2_sb = sb("sw2_sb", [P, FFN // P, D])
        sb1_sb = sb("sb1_sb", [P, 2 * FFN // P])
        bias_rows = sb("bias_rows", [3, NBIAS], BF16)
        bias_in = sb("bias_in", [P, NBIAS // P])
        bias_left = sb("bias_left", [P, 2, NBIAS // P])
        bias_parts = sb("bias_parts", [P, 3, NBIAS // P], BF16)

        first_use = sb("first_use", [P, 6 * GB * D])

        def part(n, *dims):
            names = "abcd"[:len(dims)]
            return first_use[:, n * GB * D:(n + 1) * GB * D].rearrange(
                f"p ({' '.join(names)}) -> p {' '.join(names)}", **dict(zip(names, dims)))

        xin = part(0, GB, D)
        cin = part(1, GB, D)
        xTn = part(2, GB, DC, P)
        cTn = part(3, GB, DC, P)
        xTu = part(4, DC, NU, GB, DH)
        kk = part(5, GB, 2 * DH, NU)
        RW1 = NE * DC * 2 * FFN
        rw1_sb = first_use[:, 0:RW1]
        rw2_sb = first_use[:, RW1:RW1 + NE * FFN // P * D]
        assert RW1 + NE * FFN // P * D <= 6 * GB * D

        xT = sb("xT", [P, 2, DC, P])
        cT = sb("cT", [P, 2, DC, P])
        xn = sb("xn", [P, 2, D])
        kp = sb("kp", [P, 2, 2, 2 * DH, NU])
        qT = sb("qT", [P, 2, DC, P])
        va = sb("va", [P, 2, H, VW])
        nmax = sb("nmax", [P, 2, H])
        prob = sb("prob", [P, 2, H, P])
        pT = sb("pT", [P, 4, 4, P])
        oT = sb("oT", [P, H // CG, P])
        rden = sb("rden", [P, 2, H])
        att = sb("att", [P, 2, D])
        res1 = sb("res1", [P, 2, D])
        bn1 = sb("bn1", [P, 2, 6])
        mv1 = sb("mv1", [P, 2, 2])
        rstd1 = sb("rstd1", [P, 2, 1])
        x1 = sb("x1", [P, 2, D])
        x1T = sb("x1T", [P, 2, DC, P])
        xv = sb("xv", [P, 2, D])
        products = sb("products", [P, 2, 2, 4, P])
        ra, rb = products[:, 0, :, :, :], products[:, 1, :, :, :]
        rot = sb("rot", [P, 2, 4, P])
        scx = sb("scx", [P, 2, P])
        res2 = sb("res2", [P, 2, D])
        bn2 = sb("bn2", [P, 2, 6])
        mv2 = sb("mv2", [P, 2, 2])
        rstd2 = sb("rstd2", [P, 2, 1])
        x2 = sb("x2", [P, 2, D])
        neg_half = sb("neg_half", [P, QB])
        x2T = sb("x2T", [P, 2, DC, P])
        x2s = sb("x2s", [P, 2, D])
        gc = sb("gc", [P, 2, 3 * NE])
        lmax = sb("lmax", [P, 2, 1])
        gexp = sb("gexp", [P, 2, NE])
        gsum = sb("gsum", [P, 2, 1])
        ginv = sb("ginv", [P, 2, 1])
        gprob = sb("gprob", [P, 2, NE])
        top_p = sb("top_p", [P, 2, 8])
        top_i = sb("top_i", [P, 2, 8], U32)
        top_f = sb("top_f", [P, 2, TOPK])
        pick = sb("pick", [P, 2, TOPK, NE])
        pick_all = sb("pick_all", [P, B, TOPK, NE])
        shifts = sb("shifts", [P, NE])
        shifted = sb("shifted", [P, B, TOPK, NE])
        shift = sb("shift", [P, B, TOPK])
        back_rows = sb("back_rows", [P, B, TOPK], U32)
        picks = sb("picks", [P, 2, NE], BF16)
        base = sb("base", [P, NE])
        place = sb("place", [P, 2, NE])
        mine = sb("mine", [P, 2, TOPK, NE])
        pos = sb("pos", [P, 2, TOPK], U32)
        pos_all = sb("pos_all", [P, B, TOPK], U32)
        cw_all = sb("cw_all", [P, B, TOPK])
        zeros = sb("zeros", [P, D])
        tail_rows = sb("tail_rows", [P, NE], U32)
        counts = sb("counts", [P, 4, NE])
        counts_i = sb("counts_i", [P, 2, NE], I32)
        upto = sb("upto", [P, NE, NE])
        passed = sb("passed", [1, TILES, NE])
        skipped = sb("skipped", [1, TILES, NE])
        tile_f = sb("tile_f", [1, 2, TILES])
        tile_expert = sb("tile_expert", [1, TILES], I32)
        tile_row = sb("tile_row", [1, TILES], I32)

        xg = sb("xg", [P, 4, D])
        xgT = sb("xgT", [P, 2, DC, P])
        sil = sb("sil", [P, 2, FFN])
        gate_h = sb("gate_h", [P, 2, FFN])
        ghT = sb("ghT", [P, 2, FFN // P, P])
        yg = sb("yg", [P, 2, D])

        x2T4 = prob[:, 0, :, :].rearrange("p h t -> p (h t)").rearrange("p (r b c t) -> p r b c t", r=2, b=QB, c=DC)
        x2n = prob[:, 1, :, :].rearrange("p h t -> p (h t)").rearrange("p (r b d) -> p r b d", r=2, b=QB)
        ssil = pT[:, :, :, :].rearrange("p (r f) n t -> p r f (n t)", r=2)
        sgh = products[:, :, :, :, :].rearrange("p r f n t -> p r f (n t)")
        ya = first_use[:, 4096:6144].rearrange("p (r b d) -> p r b d", r=2, b=QB)
        yb = first_use[:, 6144:8192].rearrange("p (r b d) -> p r b d", r=2, b=QB)
        got = first_use[:, 8192:12288].rearrange("p (r b j d) -> p r b j d", r=2, b=QB, j=TOPK)
        y3 = sb("y3", [P, 2, QB, D])
        pos4 = sb("pos4", [P, 2, QB, TOPK], U32)
        cw4 = sb("cw4", [P, 2, QB, TOPK])
        bn3 = sb("bn3", [P, 2, QB, 6])
        mv3 = sb("mv3", [P, 2, QB, 2])
        var3 = sb("var3", [P, 2, QB])
        rstd3 = sb("rstd3", [P, 2, QB])
        shift3 = sb("shift3", [P, 2, QB])

        ident_in = sem("ident_in")
        tables_in = sem("tables_in")
        w_in = sem("w_in")
        xw_in = sem("xw_in")
        consts_set = sem("consts_set")
        xin_in = sem("xin_in")
        cin_in = sem("cin_in")
        x_turned = sem("x_turned")
        c_turned = sem("c_turned")
        k_made = sem("k_made")
        xTn_set = sem("xTn_set")
        cTn_set = sem("cTn_set")
        xTu_set = sem("xTu_set")
        kk_set = sem("kk_set")
        xT_stored = sem("xT_stored")
        cT_stored = sem("cT_stored")
        k_stored = sem("k_stored")

        xT_in = [sem("xT_in0"), sem("xT_in1")]
        cT_in = [sem("cT_in0"), sem("cT_in1")]
        xn_in = [sem("xn_in0"), sem("xn_in1")]
        kp_in = [sem("kp_in0"), sem("kp_in1")]
        qv_made = sem("qv_made")
        q_set = sem("q_set")
        v_set = sem("v_set")
        scored = sem("scored")
        maxed = sem("maxed")
        expd = sem("expd")
        p_turned = sem("p_turned")
        pT_set = sem("pT_set")
        oT_set = sem("oT_set")
        heads_turned = sem("heads_turned")
        heads_made = sem("heads_made")
        den_set = sem("den_set")
        att_set = sem("att_set")
        res1_set = sem("res1_set")
        bn1_set = sem("bn1_set")
        mv1_set = sem("mv1_set")
        rstd1_set = sem("rstd1_set")
        x1_set = sem("x1_set")
        x1T_set = sem("x1T_set")
        xkv_made = sem("xkv_made")
        xv_set = sem("xv_set")
        xq_made = sem("xq_made")
        rot_k = sem("rot_k")
        rot_q = sem("rot_q")
        rot_set = sem("rot_set")
        scx_made = sem("scx_made")
        scx_set = sem("scx_set")
        yx_made = sem("yx_made")
        res2_set = sem("res2_set")
        bn2_set = sem("bn2_set")
        mv2_set = sem("mv2_set")
        rstd2_set = sem("rstd2_set")
        x2_set = sem("x2_set")
        x2_stored = [sem("x2_stored0"), sem("x2_stored1")]
        x2T_stored = [sem("x2T_stored0"), sem("x2T_stored1")]
        small_in = sem("small_in")
        ffn_in = sem("ffn_in")
        bias_split = sem("bias_split")
        bias_out = sem("bias_out")
        bias_back = sem("bias_back")
        base_set = sem("base_set")
        x2_turned = sem("x2_turned")
        mid_made = sem("mid_made")
        x2T_set = sem("x2T_set")
        gc_set = sem("gc_set")
        x2s_set = sem("x2s_set")
        lmax_set = sem("lmax_set")
        gexp_set = sem("gexp_set")
        ginv_set = sem("ginv_set")
        gprob_set = sem("gprob_set")
        top_p_set = sem("top_p_set")
        top_i_set = sem("top_i_set")
        top_f_set = sem("top_f_set")
        pick_set = sem("pick_set")
        picks_set = sem("picks_set")
        place_set = sem("place_set")
        mine_set = sem("mine_set")
        pos_set = sem("pos_set")
        kept_set = sem("kept_set")
        sent_in = [sem("sent_in0"), sem("sent_in1")]
        zeros_sent = sem("zeros_sent")
        idle_sent = sem("idle_sent")
        plan_step = sem("plan_step")
        xg_in = [sem(f"xg_in{i}") for i in range(4)]
        yg_out = [sem("yg_out0"), sem("yg_out1")]
        xg_turned = sem("xg_turned")
        xgT_set = sem("xgT_set")
        hid_made = sem("hid_made")
        sil_set = sem("sil_set")
        gh_set = sem("gh_set")
        gh_turned = sem("gh_turned")
        ghT_set = sem("ghT_set")
        yg_made = sem("yg_made")
        yg_set = sem("yg_set")
        x2T4_in = [sem("x2T4_in0"), sem("x2T4_in1")]
        x2n_in = [sem("x2n_in0"), sem("x2n_in1")]
        got_in = [sem("got_in0"), sem("got_in1")]
        shid_made = sem("shid_made")
        ssil_set = sem("ssil_set")
        sgh_set = sem("sgh_set")
        sy_made = sem("sy_made")
        mix_a = sem("mix_a")
        mix_b = sem("mix_b")
        mix_c = sem("mix_c")
        bn3_set = sem("bn3_set")
        mv3_set = sem("mv3_set")
        rstd3_set = sem("rstd3_set")
        shift3_set = sem("shift3_set")
        y3_set = sem("y3_set")
        pos4_set = sem("pos4_set")
        cw4_set = sem("cw4_set")
        PLAN_STEPS = 20
        out_stored = [sem("out_stored0"), sem("out_stored1")]

        block = ctx.enter_context(nc.Block())
        LOAD_AHEAD, LAST_LAG = 2, 6
        FIRST_K, END_K = LAST_LAG // 2 + 1, (B - LOAD_AHEAD) // 2

        def phases(eng, step):
            def peeled(first, end):
                for k in range(first, end):
                    for s in range(2):
                        step(k, s, lambda lag: 0 <= 2 * k + s - lag < B)

            peeled(-LOAD_AHEAD // 2, FIRST_K)
            with eng.Fori(FIRST_K, END_K) as k:
                for s in range(2):
                    step(k, s, lambda lag: True)
            peeled(END_K, (B + LAST_LAG + 1) // 2)

        def groups(eng, body):
            body(0)
            with eng.Fori(1, NG) as g:
                body(g)

        def after(eng, what, count):
            if not isinstance(count, int) or count > 0:
                eng.wait_ge(what, count)

        def rows_done(count):
            return min(count, B) if isinstance(count, int) else count

        @block.sync
        def _(eng):
            def load_group(g, what, src, loaded):
                eng.dma_start(what[:, :, :], src[bass.ds(g * GB, GB)].rearrange("b p d -> p b d")).then_inc(loaded, 16)

            eng.dma_start(ident, table_f32[:, 0:P]).then_inc(ident_in, 16)
            load_group(0, xin, x, xin_in)
            eng.dma_start(wqkv_sb[:, :, :], wqkv.rearrange("(c p) n -> p c n", p=P)).then_inc(w_in, 16)
            load_group(0, cin, ctx_1024, cin_in)
            o1, o2 = NE * 2 * FFN // P, (NE * 2 * FFN + NE * D) // P
            spans = ((0, o1, rb1.rearrange("e n -> (e n)")), (o1, o2, rb2.rearrange("e n -> (e n)")),
                     (o2, NBIAS // P, sb2.rearrange("e n -> (e n)")))
            for lo, hi, src in spans:
                eng.dma_start(bias_in[:, lo:hi], src.rearrange("(p n) -> p n", p=P)).then_inc(small_in, 16)

            def load_small():
                eng.dma_start(gate_w_sb[:, :, :], gate_w.rearrange("(c p) n -> p c n", p=P)).then_inc(small_in, 16)
                eng.dma_start(gate_b_sb[:, 0:NE], gate_b.rearrange("(o n) -> o n", o=1).broadcast_to([P, NE])).then_inc(small_in, 16)
                eng.dma_start(sb1_sb[:, :], sb1[0].rearrange("(c p) -> p c", p=P), allow_slow_non_contiguous=True).then_inc(small_in, 16)
                eng.dma_start(tf[:, P:], table_f32[:, P:]).then_inc(tables_in, 16)
                eng.dma_start(tb[:, :], table_bf16).then_inc(tables_in, 16)
                for w, src in ((xwq_sb, xwq), (xwk_sb, xwk), (xwv_sb, xwv)):
                    eng.dma_start(w[:, :, :], src.rearrange("(c p) n -> p c n", p=P)).then_inc(xw_in, 16)

            def store_k(g):
                eng.wait_ge(kk_set, g * 4 + 4)
                eng.dma_start(k_dram[bass.ds(g * GB, GB)].rearrange("b i g f -> (b i) (g f)"),
                              first_use[:, 5 * GB * D:6 * GB * D]).then_inc(k_stored, 16)

            def prepare(g, more):
                if more:
                    eng.wait_ge(x_turned, g * 4 + 4)
                    load_group(g + 1, xin, x, xin_in)
                eng.wait_ge(xTn_set, g * 4 + 4)
                eng.dma_start(xT_dram[bass.ds(g * GB, GB)].rearrange("b p c t -> p b c t"), xTn[:, :, :, :]).then_inc(xT_stored, 16)
                if more:
                    eng.wait_ge(c_turned, g * 4 + 4)
                    load_group(g + 1, cin, ctx_1024, cin_in)
                eng.wait_ge(cTn_set, g * 4 + 4)
                eng.dma_start(cT_dram[bass.ds(g * GB, GB)].rearrange("b p c t -> p b c t"), cTn[:, :, :, :]).then_inc(cT_stored, 16)

            prepare(0, True)
            load_small()
            eng.wait_ge(bias_split, 5)
            for lo, hi, _ in spans:
                eng.dma_start(bias_dram[:, lo * P:hi * P].rearrange("n (p w) -> p n w", p=P),
                              bias_parts[:, :, lo:hi]).then_inc(bias_out, 16)
            store_k(0)
            with eng.Fori(1, NG - 1) as g:
                prepare(g, True)
                store_k(g)
            prepare(NG - 1, False)
            eng.wait_ge(bias_out, 3 * 16)
            eng.dma_start(bias_rows[:, :], bias_dram).then_inc(bias_back, 16)
            eng.dma_start(sw1_sb[:, :, :], sw1[0].rearrange("(c p) n -> p c n", p=P)).then_inc(ffn_in, 16)
            eng.dma_start(sw2_sb[:, :, :], sw2[0].rearrange("(c p) n -> p c n", p=P)).then_inc(ffn_in, 16)
            eng.wait_ge(xT_stored, 16 * (NG - 1))
            eng.wait_ge(cT_stored, 16 * (NG - 1))
            eng.wait_ge(k_stored, 16 * (NG - 1))

            def load_turned(q, r):
                eng.dma_start(x2T4[:, r, :, :, :], x2T_dram[bass.ds(q * QB, QB)].rearrange("b p c t -> p b c t")
                              ).then_inc(x2T4_in[r], 16)

            def load_rows(q, r):
                eng.dma_start(x2n[:, r, :, :], x2_dram[bass.ds(q * QB, QB)].rearrange("b p d -> p b d")
                              ).then_inc(x2n_in[r], 16)

            def step(k, s, live):
                if live(-2):
                    kk_, r = at(k, s, -2)
                    t = kk_ * 2 + r
                    after(eng, qv_made, t - 1)
                    eng.dma_start(xT[:, r, :, :], xT_dram[t]).then_inc(xT_in[r], 16)
                if live(-1):
                    kk_, r = at(k, s, -1)
                    t = kk_ * 2 + r
                    after(eng, scored, (t - 1) * 4)
                    if isinstance(t, int) and t < 2:
                        eng.wait_ge(consts_set, 2)
                    for j in range(GB):
                        lo = 16 * j
                        eng.dma_start(kp[lo:lo + DH, r, j % 2, :, :].rearrange("p a u -> p (a u)"),
                                      k_dram[t, :, j, :]).then_inc(kp_in[r], 16)
                if isinstance(k, int) and 2 * k + s == -1:
                    store_k(NG - 1)
                if isinstance(k, int) and 2 * k + s == 1:
                    eng.wait_ge(xT_stored, 16 * NG)
                    eng.wait_ge(cT_stored, 16 * NG)
                    eng.wait_ge(k_stored, 16 * NG)
                if isinstance(k, int) and 1 < 2 * k + s <= 1 + NE // 2:
                    for e in range(2 * (2 * k + s - 2), 2 * (2 * k + s - 1)):
                        lo = e * DC * 2 * FFN
                        eng.dma_start(rw1_sb[:, lo:lo + DC * 2 * FFN].rearrange("p (c n) -> p c n", c=DC),
                                      rw1[e].rearrange("(c p) n -> p c n", p=P)).then_inc(ffn_in, 16)
                        lo = e * FFN // P * D
                        eng.dma_start(rw2_sb[:, lo:lo + FFN // P * D].rearrange("p (c n) -> p c n", c=FFN // P),
                                      rw2[e].rearrange("(c p) n -> p c n", p=P)).then_inc(ffn_in, 16)
                if live(1):
                    kk_, r = at(k, s, 1)
                    t = kk_ * 2 + r
                    after(eng, xkv_made, t - 1)
                    eng.dma_start(cT[:, r, :, :], cT_dram[t]).then_inc(cT_in[r], 16)
                    after(eng, res1_set, t - 1)
                    eng.dma_start(xn[:, r, :], x[t]).then_inc(xn_in[r], 16)
                if live(4):
                    kk_, r = at(k, s, 4)
                    t = kk_ * 2 + r
                    eng.wait_ge(x2_set, t + 1)
                    eng.dma_start(x2_dram[t], x2[:, r, :]).then_inc(x2_stored[r], 16)
                    eng.wait_ge(x2T_set, t + 1)
                    eng.dma_start(x2T_dram[t], x2T[:, r, :, :]).then_inc(x2T_stored[r], 16)
                if isinstance(k, int) and 2 * k + s == B + 2:
                    eng.wait_ge(p_turned, 4 * B)
                    for q in range(2):
                        for row in range(2):
                            eng.wait_ge(x2T_stored[row], 16 * QB)
                        load_turned(q, q)

            phases(eng, step)
            for r in range(2):
                eng.wait_ge(x2_stored[r], 16 * (B // 2))
                eng.wait_ge(x2T_stored[r], 16 * (B // 2))
            for r in range(2):
                load_rows(r, r)

            def store_out(q, r):
                eng.wait_ge(y3_set, (q + 1) * QB)
                eng.dma_start(out[bass.ds(q * QB, QB)].rearrange("b p d -> p b d"), y3[:, r, :, :]).then_inc(out_stored[r], 16)

            def turn(k, r, first=False, more=True):
                q = 2 * k + r
                if more:
                    eng.wait_ge(shid_made, 2 * q + 2)
                    load_turned(q + 2, r)
                if not first:
                    store_out(q - 1, 1 - r)
                if more:
                    eng.wait_ge(mix_a, (q + 1) * QB)
                    load_rows(q + 2, r)

            turn(0, 0, first=True)
            turn(0, 1)
            with eng.Fori(1, NQ // 2 - 1) as k:
                for r in range(2):
                    turn(k, r)
            for r in range(2):
                turn(NQ // 2 - 1, r, more=False)
            store_out(NQ - 1, 1)
            for r in range(2):
                eng.wait_ge(out_stored[r], 16 * (NQ // 2))

        @block.gpsimd
        def _(eng):
            eng.memset(neg_half[:, :], -0.5)
            eng.memset(zeros[:, :], 0.0)
            eng.memset(gate_b_sb[:, NE:3 * NE], 0.0)
            eng.memset(va[:, :, :, :], 0.0).then_inc(consts_set, 1)
            eng.wait_ge(consts_set, 1)
            eng.memset(va[:, :, :, DH:DH + 1], 1.0)
            eng.memset(kp[:, :, :, :, :], 0.0).then_inc(consts_set, 1)
            eng.wait_ge(consts_set, 2)

            def step(k, s, live):
                def turn_into(t, r, m, parts):
                    eng.wait_ge(parts, 2 * t + 2)
                    after(eng, scx_made, t - 1)
                    for e in range(2):
                        eng.tensor_tensor(rot[:, r, m + e, :], ra[:, r, m + e, :], rb[:, r, m + 1 - e, :],
                                          ALU.add).then_inc(rot_set, 1)

                k2, r2 = at(k, s, 2)
                t2 = k2 * 2 + r2
                if live(2):
                    eng.wait_ge(mv1_set, 2 * t2 + 2)
                    eng.tensor_tensor(rstd1[:, r2, :], mv1[:, r2, 1:2], neg_half[:, 0:1], ALU.pow).then_inc(rstd1_set, 1)
                    turn_into(t2, r2, 0, rot_k)
                if live(3):
                    kk_, r = at(k, s, 3)
                    t = kk_ * 2 + r
                    eng.wait_ge(mv2_set, 2 * t + 2)
                    eng.tensor_tensor(rstd2[:, r, :], mv2[:, r, 1:2], neg_half[:, 0:1], ALU.pow).then_inc(rstd2_set, 1)
                if live(6):
                    kk_, r = at(k, s, 6)
                    eng.wait_ge(pos_set, kk_ * 2 + r + 1)
                if live(2):
                    turn_into(t2, r2, 2, rot_q)
                if isinstance(k, int) and 2 * k + s == 2:
                    eng.dma_start(sent[IDLE_ROW:XROWS, :].rearrange("(n p) d -> p n d", p=P),
                                  zeros[:, :].unsqueeze(1).broadcast_to([P, IDLE, D])).then_inc(idle_sent, 16)
                if live(6):
                    kk_, r = at(k, s, 6)
                    for j in range(TOPK):
                        eng.indirect_dma_start(sent, bass.IndirectOffsetOnAxis(ap=pos[:, r, j:j + 1], axis=0),
                                               x2s[:, r, :], None).then_inc(sent_in[r], 16)

            phases(eng, step)
            eng.wait_ge(plan_step, 1)
            for e in range(NE):
                eng.indirect_dma_start(sent, bass.IndirectOffsetOnAxis(ap=tail_rows[:, e:e + 1], axis=0),
                                       zeros[:, :], None).then_inc(zeros_sent, 16)

            for r in range(2):
                eng.wait_ge(yg_out[r], 16 * (TILES // 2))
            def fetch(r):
                for b in range(QB):
                    for j in range(TOPK):
                        eng.indirect_dma_start(got[:, r, b, j, :], None, back,
                                               bass.IndirectOffsetOnAxis(ap=pos4[:, r, b, j:j + 1], axis=0)
                                               ).then_inc(got_in[r], 16)

            def root(q, r):
                eng.wait_ge(mv3_set, (q + 1) * (QB + 1))
                eng.tensor_tensor(rstd3[:, r, :], var3[:, r, :], neg_half[:, :], ALU.pow).then_inc(rstd3_set, 1)

            eng.wait_ge(pos4_set, TOPK)
            for r in range(2):
                fetch(r)
            with eng.Fori(0, NQ // 2 - 1) as k:
                for r in range(2):
                    q = 2 * k + r
                    eng.wait_ge(mix_c, (q + 1) * QB)
                    eng.wait_ge(pos4_set, q + 3)
                    root(q, r)
                    fetch(r)
            for r in range(2):
                root(NQ - 2 + r, r)

        @block.tensor
        def _(eng):
            eng.wait_ge(ident_in, 16)
            def prepare(g):
                for what, loaded, turned, bank0 in ((xin, xin_in, x_turned, 0), (cin, cin_in, c_turned, 4)):
                    eng.wait_ge(loaded, g * 16 + 16)
                    for j in range(4):
                        if not isinstance(g, int):
                            eng.wait_ge(cTn_set if bank0 else kk_set, (g - 1) * 4 + j + 1)
                        for i in range(4):
                            mm = eng.transpose(ps[:, bank0 + j, i * P:(i + 1) * P],
                                               what[:, 2 * j + i // 2, (i % 2) * P:(i % 2 + 1) * P], ident)
                        mm.then_inc(turned, 1)
                if isinstance(g, int):
                    eng.wait_ge(w_in, 16)
                eng.wait_ge(xTu_set, g * 8 + 8)
                eng.wait_ge(xTn_set, g * 4 + 4)
                for j in range(4):
                    for i in range(2):
                        for c in range(DC):
                            mm = eng.matmul(ps[:, j, i * D:(i + 1) * D].rearrange("p (g c d) -> p g c d", c=2, d=DH),
                                            xTu[:, c, 2 * j + i, :, :].rearrange("p b i -> p (b i)"),
                                            wqkv_sb[:, c, D:2 * D].rearrange("p (c g d) -> p g c d", c=2, d=DH),
                                            start=(c == 0), stop=(c == DC - 1))
                    mm.then_inc(k_made, 1)
            groups(eng, prepare)
            eng.wait_ge(kk_set, 4 * NG)
            eng.wait_ge(cTn_set, 4 * NG)
            eng.wait_ge(tables_in, 32)
            eng.wait_ge(xw_in, 48)
            eng.wait_ge(small_in, 96)
            eng.wait_ge(consts_set, 2)

            def project(k, s, lag):
                kk_, r = at(k, s, lag)
                t = kk_ * 2 + r
                eng.wait_ge(xT_in[r], kk_ * 16 + 16)
                after(eng, res2_set, t - 3)
                after(eng, q_set, t)
                after(eng, v_set, t)
                for m in range(DC):
                    for c in range(DC):
                        eng.matmul(QV[:, m * P:(m + 1) * P], wqkv_sb[:, c, m * P:(m + 1) * P], xT[:, r, c, :],
                                   start=(c == 0), stop=(c == DC - 1))
                for c in range(DC):
                    mm = eng.matmul(QV[:, D:2 * D], xT[:, r, c, :], wqkv_sb[:, c, 2 * D:3 * D],
                                    start=(c == 0), stop=(c == DC - 1))
                mm.then_inc(qv_made, 1)

            def scores(k, s, u):
                kk_, r = at(k, s, 0)
                t = kk_ * 2 + r
                if u == 0:
                    eng.wait_ge(q_set, t + 1)
                    eng.wait_ge(kp_in[r], kk_ * 128 + 128)
                after(eng, expd, t * 4 + u - 1)
                bank = SCORE[u % 2]
                eng.matmul(bank.rearrange("p (h j) -> p h j", j=P), ident_bf,
                           causal_bf.unsqueeze(1).broadcast_to([P, 4, P]), start=True, stop=False,
                           skip_group_check=True)
                for c in range(2):
                    for e in range(2):
                        n = 2 * c + e
                        mm = eng.matmul(bank[:, n * P:(n + 1) * P].rearrange("p (d u) -> p d u", u=NU),
                                        qT[32 * u:32 * u + 32, r, c, :],
                                        kp[32 * u:32 * u + 32, r, e, c * DH:(c + 1) * DH, :],
                                        start=False, stop=(n == 3), skip_group_check=True)
                mm.then_inc(scored, 1)

            def turn_probs(k, s, u):
                kk_, r = at(k, s, 1)
                t = kk_ * 2 + r
                eng.wait_ge(expd, t * 4 + u + 1)
                after(eng, pT_set, t * 4 + u)
                for n in range(4):
                    mm = eng.transpose(PROBT[:, n * P:(n + 1) * P], prob[:, r, 4 * u + n, :], ident)
                mm.then_inc(p_turned, 1)

            def weigh(k, s, u0):
                kk_, r = at(k, s, 1)
                t = kk_ * 2 + r
                eng.wait_ge(pT_set, t * 4 + u0 + 2)
                if u0 == 0:
                    eng.wait_ge(v_set, t + 1)
                    after(eng, oT_set, t)
                for c in range(2):
                    for u in (u0, u0 + 1):
                        for e in range(2):
                            h = 8 * c + 2 * u + e
                            lo = h % CG * VW
                            mm = eng.matmul(HEADS_T[lo:lo + VW, h // CG, :], va[:, r, h, :], pT[:, u, 2 * c + e, :],
                                            start=True, stop=True)
                mm.then_inc(heads_made, 1)

            def step(k, s, live):
                n = 2 * k + s
                k2, r2 = at(k, s, 2)
                t2 = k2 * 2 + r2
                k3, r3 = at(k, s, 3)
                t3 = k3 * 2 + r3
                k4, r4 = at(k, s, 4)
                t4 = k4 * 2 + r4
                if live(0):
                    scores(k, s, 0)
                if live(1):
                    turn_probs(k, s, 0)
                if live(2):
                    eng.wait_ge(oT_set, t2 + 1)
                    after(eng, att_set, t2)
                    for b in range(H // CG):
                        mm = eng.transpose(ps[:, 3, b * P:(b + 1) * P], oT[:, b, :], ident)
                    mm.then_inc(heads_turned, 1)
                if live(4):
                    eng.wait_ge(x2_set, t4 + 1)
                    eng.wait_ge(rot_q, 2 * rows_done(t4 + 2))
                    for c in range(DC):
                        mm = eng.transpose(TR[:, c * P:(c + 1) * P], x2[:, r4, c * P:(c + 1) * P], ident)
                    mm.then_inc(x2_turned, 1)
                if live(3):
                    eng.wait_ge(rot_set, 4 * t3 + 4)
                    eng.wait_ge(xv_set, t3 + 1)
                    for m in range(2):
                        mm = eng.matmul(SCX, rot[:, r3, m, :], rot[:, r3, 2 + m, :], start=(m == 0), stop=(m == 1))
                    mm.then_inc(scx_made, 1)
                if live(0):
                    scores(k, s, 1)
                if live(1):
                    turn_probs(k, s, 1)
                if live(2):
                    eng.wait_ge(cT_in[r2], k2 * 16 + 16)
                    after(eng, scx_set, t2)
                    for m in range(2):
                        for c in range(DC):
                            eng.matmul(KQ[:, m, :], xwk_sb[:, c, m:D:2], cT[:, r2, c, :],
                                       start=(c == 0), stop=(c == DC - 1))
                    for c in range(DC):
                        mm = eng.matmul(XV, cT[:, r2, c, :], xwv_sb[:, c, :], start=(c == 0), stop=(c == DC - 1))
                    mm.then_inc(xkv_made, 1)
                if live(1):
                    weigh(k, s, 0)
                if live(0):
                    scores(k, s, 2)
                if live(1):
                    turn_probs(k, s, 2)
                if live(3):
                    eng.wait_ge(scx_set, t3 + 1)
                    eng.wait_ge(q_set, rows_done(t3 + 4))
                    eng.wait_ge(v_set, rows_done(t3 + 4))
                    eng.matmul(YX, scx[:, r3, :], xv[:, r3, :], start=True, stop=True).then_inc(yx_made, 1)
                if live(2) or live(3) or live(4) or live(5):
                    if live(2):
                        eng.wait_ge(x1_set, t2 + 1)
                    if live(4):
                        eng.wait_ge(x2T_set, t4 + 1)
                    if live(5):
                        k5, r5 = at(k, s, 5)
                        eng.wait_ge(picks_set, k5 * 2 + r5 + 1)
                        after(eng, gc_set, n - 4)
                    if live(2):
                        for c in range(DC):
                            mm = eng.transpose(TR[:, c * P:(c + 1) * P], x1[:, r2, c * P:(c + 1) * P], ident)
                    if live(4):
                        for c in range(DC):
                            mm = eng.matmul(GATE[:, 0:NE], x2T[:, r4, c, :], gate_w_sb[:, c, :], start=(c == 0), stop=(c == DC - 1))
                    if live(5):
                        eng.matmul(GATE[:, NE:2 * NE], before_bf, picks[:, r5, :], start=True, stop=True)
                        mm = eng.matmul(GATE[:, 2 * NE:3 * NE], ones_bf, picks[:, r5, :], start=True, stop=True)
                    mm.then_inc(mid_made, 1)
                if live(0):
                    scores(k, s, 3)
                if live(1):
                    turn_probs(k, s, 3)
                if live(-1):
                    project(k, s, -1)
                if live(1):
                    weigh(k, s, 2)
                if live(2):
                    eng.wait_ge(x1T_set, t2 + 1)
                    after(eng, gc_set, n - 3)
                    for m in range(2):
                        for c in range(DC):
                            mm = eng.matmul(KQ[:, 2 + m, :], xwq_sb[:, c, m:D:2], x1T[:, r2, c, :],
                                            start=(c == 0), stop=(c == DC - 1))
                    mm.then_inc(xq_made, 1)

            phases(eng, step)

            def shared(q, k, r, bank0=0):
                eng.wait_ge(x2T4_in[r], k * 16 + 16)
                for f in range(FFN // P):
                    if not isinstance(k, int):
                        eng.wait_ge(sgh_set, (q - 1) * 2 + f + 1)
                    for half in range(2):
                        cols = half * FFN + f * P
                        for c in range(DC):
                            mm = eng.matmul(ps[:, bank0 + 2 * f + half, :].rearrange("p (b t) -> p b t", b=QB),
                                            sw1_sb[:, c, cols:cols + P], x2T4[:, r, :, c, :],
                                            start=(c == 0), stop=(c == DC - 1))
                    mm.then_inc(shid_made, 1)

            eng.wait_ge(gc_set, B + 1)
            eng.wait_ge(ffn_in, 16 * (2 + 2 * NE))
            for r in range(2):
                shared(r, 0, r, 4 * r)

            eng.wait_ge(sgh_set, 2 * FFN // P)
            eng.wait_ge(bias_back, 16)
            eng.wait_ge(plan_step, PLAN_STEPS)
            XGT = ps[:, 2, 0:D]
            GHT = ps[:, 3, 0:FFN]

            def turn_x(i, slot, loads, r):
                eng.wait_ge(xg_in[slot], loads * 16)
                after(eng, xgT_set, i)
                for c in range(DC):
                    mm = eng.transpose(XGT[:, c * P:(c + 1) * P], xg[:, slot, c * P:(c + 1) * P], ident)
                mm.then_inc(xg_turned, 1)

            def turn_h(i, r):
                eng.wait_ge(gh_set, i + 1)
                after(eng, ghT_set, i)
                for c in range(FFN // P):
                    mm = eng.transpose(GHT[:, c * P:(c + 1) * P], gate_h[:, r, c * P:(c + 1) * P], ident)
                mm.then_inc(gh_turned, 1)

            def hidden(i, r, e):
                eng.wait_ge(xgT_set, i + 1)
                after(eng, gh_set, i - 1)
                eng.matmul(ps[:, r, :], ones_bf[0:3, :], bias_rows[0:3, bass.ds(e * (2 * FFN), 2 * FFN)],
                           start=True, stop=False)
                for c in range(DC):
                    mm = eng.matmul(ps[:, r, :], xgT[:, r, c, :],
                                    rw1_sb[:, bass.ds(e * (DC * 2 * FFN) + c * 2 * FFN, 2 * FFN)],
                                    start=False, stop=(c == DC - 1))
                mm.then_inc(hid_made, 1)

            def result(i, r, e):
                eng.wait_ge(ghT_set, i + 1)
                after(eng, yg_set, i - 1)
                eng.matmul(ps[:, 4 + r, 0:D], ones_bf[0:3, :], bias_rows[0:3, bass.ds(e * D + NE * 2 * FFN, D)],
                           start=True, stop=False)
                for c in range(FFN // P):
                    mm = eng.matmul(ps[:, 4 + r, 0:D], ghT[:, r, c, :],
                                    rw2_sb[:, bass.ds(e * (FFN // P * D) + c * D, D)],
                                    start=False, stop=(c == FFN // P - 1))
                mm.then_inc(yg_made, 1)

            def expert(i):
                return eng.value_load(tile_expert[0:1, bass.ds(i, 1)], min_val=0, max_val=NE - 1)

            def tiles(k, first=False, last=False):
                before = None if first else expert(4 * k - 1)
                for n in range(4):
                    i = 4 * k + n
                    this = expert(i)
                    if before is not None:
                        turn_h(i - 1, (n - 1) % 2)
                    hidden(i, n % 2, this)
                    if not (last and n == 3):
                        turn_x(i + 1, (n + 1) % 4, k + 1 + (n + 1) // 4, (n + 1) % 2)
                    if before is not None:
                        result(i - 1, (n - 1) % 2, before)
                    before = this

            turn_x(0, 0, 1, 0)
            tiles(0, first=True)
            with eng.Fori(1, TILES // 4 - 1) as k:
                tiles(k)
            tiles(TILES // 4 - 1, last=True)
            turn_h(TILES - 1, 1)
            result(TILES - 1, 1, expert(TILES - 1))

            eng.wait_ge(yg_set, TILES)

            def outputs(q, r):
                for b in range(QB):
                    if b == 0:
                        eng.wait_ge(sgh_set, 2 * q + 2)
                    after(eng, mix_a, (q - 1) * QB + b + 1)
                    eng.matmul(ps[:, 4 + b, 0:D], ones_bf[0:3, :], bias_rows[0:3, NBIAS - D:NBIAS], start=True, stop=False)
                    for c in range(FFN // P):
                        mm = eng.matmul(ps[:, 4 + b, 0:D], sgh[:, r, c, b * P:(b + 1) * P], sw2_sb[:, c, :],
                                        start=False, stop=(c == FFN // P - 1))
                    mm.then_inc(sy_made, 1)

            outputs(0, 0)
            with eng.Fori(1, NQ // 2) as k:
                for r in range(2):
                    shared(2 * k + r, k, r)
                    outputs(2 * k + r - 1, 1 - r)
            outputs(NQ - 1, 1)

        @block.scalar
        def _(eng):
            def prepare(g):
                after(eng, xT_stored, g * 16)
                for j in range(4):
                    eng.wait_ge(x_turned, g * 4 + j + 1)
                    eng.copy(xTn[:, 2 * j:2 * j + 2, :, :].rearrange("p b c t -> p (b c t)"), ps[:, j, :]).then_inc(xTn_set, 1)
                after(eng, cT_stored, g * 16)
                for j in range(4):
                    eng.wait_ge(c_turned, g * 4 + j + 1)
                    eng.copy(cTn[:, 2 * j:2 * j + 2, :, :].rearrange("p b c t -> p (b c t)"), ps[:, 4 + j, :]).then_inc(cTn_set, 1)

            groups(eng, prepare)

            def exps(k, s, u):
                kk_, r = at(k, s, 0)
                t = kk_ * 2 + r
                eng.wait_ge(maxed, t * 4 + u + 1)
                after(eng, p_turned, (t - 2) * 4 + u + 1)
                for n in range(4):
                    ins = eng.activation(prob[:, r, 4 * u + n, :], SCORE[u % 2][:, n * P:(n + 1) * P], ACT.Exp,
                                         bias=nmax[:, r, 4 * u + n:4 * u + n + 1])
                ins.then_inc(expd, 1)

            def out_probs(k, s, u):
                kk_, r = at(k, s, 1)
                t = kk_ * 2 + r
                eng.wait_ge(p_turned, t * 4 + u + 1)
                after(eng, heads_made, 2 * t - 1 + u // 2)
                eng.copy(pT[:, u, :, :].rearrange("p n t -> p (n t)"), PROBT).then_inc(pT_set, 1)

            def step(k, s, live):
                n = 2 * k + s
                kp_, rp = at(k, s, -1)
                tp = kp_ * 2 + rp
                k1, r1 = at(k, s, 1)
                t1 = k1 * 2 + r1
                k2, r2 = at(k, s, 2)
                t2 = k2 * 2 + r2
                k4, r4 = at(k, s, 4)
                t4 = k4 * 2 + r4
                if live(1):
                    out_probs(k, s, 0)
                if live(0):
                    exps(k, s, 0)
                if live(4):
                    eng.wait_ge(x2_turned, t4 + 1)
                    after(eng, x2T_stored[r4], k4 * 16)
                    after(eng, mid_made, n - 3)
                    eng.copy(x2T[:, r4, :, :].rearrange("p c t -> p (c t)"), TR).then_inc(x2T_set, 1)
                if live(1):
                    out_probs(k, s, 1)
                if live(0):
                    exps(k, s, 1)
                if live(2):
                    eng.wait_ge(xkv_made, t2 + 1)
                    after(eng, yx_made, t2 - 1)
                    eng.copy(xv[:, r2, :], XV).then_inc(xv_set, 1)
                if live(1):
                    out_probs(k, s, 2)
                if live(0):
                    exps(k, s, 2)
                if live(2):
                    eng.wait_ge(mid_made, t2 + 1)
                    after(eng, xq_made, t2 - 1)
                    eng.copy(x1T[:, r2, :, :].rearrange("p c t -> p (c t)"), TR).then_inc(x1T_set, 1)
                if live(1):
                    out_probs(k, s, 3)
                if live(0):
                    exps(k, s, 3)
                if live(4):
                    eng.wait_ge(lmax_set, t4 + 1)
                    eng.activation(gexp[:, r4, :], gc[:, r4, 0:NE], ACT.Exp, bias=lmax[:, r4, :],
                                   accum_out=gsum[:, r4, :]).then_inc(gexp_set, 1)
                if live(-1):
                    eng.wait_ge(qv_made, tp + 1)
                    after(eng, scored, (tp - 1) * 4)
                    eng.mul(qT[:, rp, :, :].rearrange("p c t -> p (c t)"), QV[:, 0:D], 1.0 / np.sqrt(DH)).then_inc(q_set, 1)
                    after(eng, heads_made, 2 * (tp - 1))
                    if isinstance(tp, int) and tp < 2:
                        eng.wait_ge(consts_set, 2)
                    eng.copy(va[:, rp, :, 0:DH], QV[:, D:2 * D].rearrange("p (h d) -> p h d", d=DH)).then_inc(v_set, 1)
                if live(1):
                    eng.wait_ge(heads_made, 2 * t1 + 2)
                    after(eng, heads_turned, t1)
                    eng.copy(oT[:, :, :].rearrange("p x t -> p (x t)"), ps[:, 4, :]).then_inc(oT_set, 1)

            phases(eng, step)

            def shared(q, r, bank0=0):
                for f in range(FFN // P):
                    eng.wait_ge(shid_made, 2 * q + f + 1)
                    after(eng, sgh_set, (q - 2) * 2 + f + 1)
                    eng.activation(ssil[:, r, f, :], ps[:, bank0 + 2 * f, :], ACT.Silu, bias=sb1_sb[:, f:f + 1]).then_inc(ssil_set, 1)

            for r in range(2):
                shared(r, r, 4 * r)

            eng.wait_ge(plan_step, PLAN_STEPS)
            for r in range(2):
                eng.wait_ge(sent_in[r], 32 * (B // 2))
            eng.wait_ge(zeros_sent, 16 * NE)
            eng.wait_ge(idle_sent, 16)

            def first_row(i):
                return eng.value_load(tile_row[0:1, bass.ds(i, 1)], min_val=0, max_val=XROWS - P)

            def load(i, slot):
                after(eng, xg_turned, i - 3)
                eng.dma_start(xg[:, slot, :], sent[bass.ds(first_row(i), P), :]).then_inc(xg_in[slot], 16)

            def silu(i, r):
                eng.wait_ge(hid_made, i + 1)
                after(eng, gh_set, i - 1)
                eng.activation(sil[:, r, :], ps[:, r, 0:FFN], ACT.Silu).then_inc(sil_set, 1)

            def out_x(i, r):
                eng.wait_ge(xg_turned, i + 1)
                after(eng, hid_made, i - 1)
                eng.copy(xgT[:, r, :, :].rearrange("p c t -> p (c t)"), ps[:, 2, 0:D]).then_inc(xgT_set, 1)

            def out_y(i, r, k):
                eng.wait_ge(yg_made, i + 1)
                after(eng, yg_out[r], k * 16)
                eng.copy(yg[:, r, :], ps[:, 4 + r, 0:D]).then_inc(yg_set, 1)
                eng.wait_ge(yg_set, i + 1)
                eng.dma_start(back[bass.ds(i * P, P), :], yg[:, r, :]).then_inc(yg_out[r], 16)

            def tiles(k, first=False, last=False):
                for n in range(4):
                    i = 4 * k + n
                    silu(i, n % 2)
                    if not (last and n == 3):
                        out_x(i + 1, (n + 1) % 2)
                    if not (first and n == 0):
                        out_y(i - 1, (n - 1) % 2, 2 * k + (n - 1) // 2)
                    if not (last and n > 0):
                        load(i + 3, (n + 3) % 4)

            for i in range(3):
                load(i, i)
            out_x(0, 0)
            tiles(0, first=True)
            with eng.Fori(1, TILES // 4 - 1) as k:
                tiles(k)
            tiles(TILES // 4 - 1, last=True)
            out_y(TILES - 1, 1, TILES // 2 - 1)

            def finish(q, k, r):
                eng.wait_ge(shift3_set, q + 1)
                after(eng, out_stored[r], k * 16)
                for b in range(QB):
                    eng.activation(y3[:, r, b, :], ya[:, r, b, :], ACT.Identity, bias=shift3[:, r, b:b + 1],
                                   scale=rstd3[:, r, b:b + 1]).then_inc(y3_set, 1)

            for r in range(2):
                shared(2 + r, r)
                finish(r, 0, r)
            with eng.Fori(1, NQ // 2 - 1) as k:
                for r in range(2):
                    shared(2 * k + r + 2, r)
                    finish(2 * k + r, k, r)
            for r in range(2):
                finish(NQ - 2 + r, NQ // 2 - 1, r)

        @block.vector
        def _(eng):
            def prepare(g):
                after(eng, k_made, g * 4)
                for j in range(4):
                    eng.wait_ge(xTn_set, g * 4 + j + 1)
                    for i in range(2):
                        eng.tensor_copy(xTu[:, :, :, 2 * j + i, :],
                                        ps[:, j, i * D:(i + 1) * D].rearrange("p (c u i) -> p c u i", c=DC, i=DH)
                                        ).then_inc(xTu_set, 1)
                after(eng, k_stored, g * 16)
                for j in range(4):
                    eng.wait_ge(k_made, g * 4 + j + 1)
                    eng.tensor_copy(kk[:, :, :, 2 * j:2 * j + 2].rearrange("p g a u -> p u (g a)"),
                                    ps[:, j, :].rearrange("p (u a) -> p u a", u=2)).then_inc(kk_set, 1)
                if isinstance(g, int):
                    eng.wait_ge(small_in, 96)
                    eng.tensor_copy(bias_parts[:, 0, :], bias_in[:, :]).then_inc(bias_split, 1)
                    for n in range(2):
                        eng.wait_ge(bias_split, 2 * n + 1)
                        left = bias_left[:, n, :]
                        eng.tensor_tensor(left, (bias_in[:, :], bias_left[:, 0, :])[n], bias_parts[:, n, :], ALU.subtract).then_inc(bias_split, 1)
                        eng.wait_ge(bias_split, 2 * n + 2)
                        eng.tensor_copy(bias_parts[:, n + 1, :], left).then_inc(bias_split, 1)
            groups(eng, prepare)
            eng.wait_ge(tables_in, 32)
            eng.wait_ge(consts_set, 2)
            eng.tensor_copy(base[:, :], region_rows).then_inc(base_set, 1)

            def maxes(k, s, u):
                kk_, r = at(k, s, 0)
                t = kk_ * 2 + r
                eng.wait_ge(scored, t * 4 + u + 1)
                after(eng, expd, (t - 2) * 4 + u + 1)
                eng.tensor_reduce(nmax[:, r, 4 * u:4 * u + 4], SCORE[u % 2].rearrange("p (h j) -> p h j", j=P),
                                  AX_X, ALU.max, negate=True).then_inc(maxed, 1)

            def stats(t, r, res, bn, res_set, bn_set):
                eng.wait_ge(res_set, t + 1)
                eng.bn_stats(bn[:, r, :], res[:, r, :]).then_inc(bn_set, 1)

            def moments(t, r, bn, mv, mv_set):
                eng.bn_aggr(mv[:, r, :], bn[:, r, :]).then_inc(mv_set, 1)
                eng.wait_ge(mv_set, 2 * t + 1)
                eng.tensor_scalar(mv[:, r, 1:2], mv[:, r, 1:2], EPS, None, ALU.add).then_inc(mv_set, 1)

            def step(k, s, live):
                n = 2 * k + s
                k2, r2 = at(k, s, 2)
                t2 = k2 * 2 + r2
                k3, r3 = at(k, s, 3)
                t3 = k3 * 2 + r3
                k5, r5 = at(k, s, 5)
                t5 = k5 * 2 + r5
                k6, r6 = at(k, s, 6)
                t6 = k6 * 2 + r6
                if live(5):
                    eng.wait_ge(gexp_set, t5 + 1)
                    eng.reciprocal(ginv[:, r5, :], gsum[:, r5, :]).then_inc(ginv_set, 1)
                    eng.wait_ge(ginv_set, t5 + 1)
                    eng.tensor_scalar(gprob[:, r5, :], gexp[:, r5, :], ginv[:, r5, :], None, ALU.mult).then_inc(gprob_set, 1)
                    eng.wait_ge(gprob_set, t5 + 1)
                if live(6):
                    eng.wait_ge(gc_set, t6 + 2)
                    eng.wait_ge(base_set, t6 + 1)
                    eng.tensor_tensor(place[:, r6, :], gc[:, 1 - r6, NE:2 * NE], base[:, :], ALU.add).then_inc(place_set, 1)
                if live(5):
                    eng.max(top_p[:, r5, :], gprob[:, r5, :]).then_inc(top_p_set, 1)
                    eng.wait_ge(top_p_set, t5 + 1)
                if live(6):
                    eng.wait_ge(place_set, t6 + 1)
                    eng.tensor_tensor(mine[:, r6, :, :], pick[:, r6, :, :],
                                      place[:, r6, :].unsqueeze(1).broadcast_to([P, TOPK, NE]), ALU.mult).then_inc(mine_set, 1)
                if live(5):
                    eng.max_index(top_i[:, r5, :], top_p[:, r5, :], gprob[:, r5, :]).then_inc(top_i_set, 1)
                if live(6):
                    eng.wait_ge(mine_set, t6 + 1)
                    with nc.allow_low_precision(reason="a whole number below 2**24, summed in float32: exact"):
                        eng.tensor_reduce(pos[:, r6, :], mine[:, r6, :, :], AX_X, ALU.add).then_inc(pos_set, 1)
                    eng.tensor_tensor(base[:, :], base[:, :], gc[:, 1 - r6, 2 * NE:3 * NE], ALU.add).then_inc(base_set, 1)
                if live(0):
                    maxes(k, s, 0)
                if live(3):
                    eng.wait_ge(scx_made, t3 + 1)
                    after(eng, yx_made, t3 - 1)
                    eng.tensor_tensor(scx[:, r3, :], SCX, decay, ALU.mult).then_inc(scx_set, 1)
                if live(2):
                    eng.wait_ge(heads_turned, t2 + 1)
                    eng.reciprocal(rden[:, r2, :], HEADS[:, :, DH]).then_inc(den_set, 1)
                    eng.wait_ge(den_set, t2 + 1)
                    eng.tensor_tensor(att[:, r2, :].rearrange("p (h d) -> p h d", d=DH), HEADS[:, :, 0:DH],
                                      rden[:, r2, :].unsqueeze(2).broadcast_to([P, H, DH]), ALU.mult).then_inc(att_set, 1)
                    eng.wait_ge(att_set, t2 + 1)
                    eng.wait_ge(xn_in[r2], k2 * 16 + 16)
                    after(eng, x1_set, t2 - 1)
                    eng.tensor_tensor(res1[:, r2, :], att[:, r2, :], xn[:, r2, :], ALU.add).then_inc(res1_set, 1)
                    stats(t2, r2, res1, bn1, res1_set, bn1_set)
                    eng.wait_ge(bn1_set, t2 + 1)
                if live(0):
                    maxes(k, s, 1)
                if live(2):
                    moments(t2, r2, bn1, mv1, mv1_set)
                if live(6):
                    eng.wait_ge(pos_set, t6 + 1)
                    eng.tensor_scalar(pos_all[:, t6, :], pos[:, r6, :], 0.0, None, ALU.add).then_inc(kept_set, 1)
                if live(5):
                    eng.tensor_scalar(cw_all[:, t5, :], top_p[:, r5, 0:TOPK], 1.0, None, ALU.mult).then_inc(kept_set, 1)
                    eng.wait_ge(top_i_set, t5 + 1)
                    eng.tensor_copy(top_f[:, r5, :], top_i[:, r5, 0:TOPK]).then_inc(top_f_set, 1)
                    eng.wait_ge(top_f_set, t5 + 1)
                    eng.tensor_tensor(pick[:, r5, :, :], expert_ids.unsqueeze(1).broadcast_to([P, TOPK, NE]),
                                      top_f[:, r5, :].unsqueeze(2).broadcast_to([P, TOPK, NE]), ALU.is_equal).then_inc(pick_set, 1)
                if live(2):
                    eng.wait_ge(rstd1_set, t2 + 1)
                    after(eng, mid_made, t2 - 1)
                    after(eng, res2_set, t2 - 1)
                    eng.tensor_scalar(x1[:, r2, :], res1[:, r2, :], mv1[:, r2, 0:1], rstd1[:, r2, :],
                                      ALU.subtract, ALU.mult).then_inc(x1_set, 1)
                if live(5):
                    eng.wait_ge(pick_set, t5 + 1)
                    eng.tensor_scalar(pick_all[:, t5, :, :], pick[:, r5, :, :], 1.0, None, ALU.mult).then_inc(kept_set, 1)
                    after(eng, mid_made, t5 + 2)
                    eng.tensor_tensor(picks[:, r5, :], pick[:, r5, 0, :], pick[:, r5, 1, :], ALU.add).then_inc(picks_set, 1)
                if live(2):
                    eng.wait_ge(xv_set, t2 + 1)
                    after(eng, rot_set, 4 * (t2 - 1))
                    for into, table in ((ra, rot_cos), (rb, rot_sin)):
                        eng.tensor_tensor(into[:, r2, 0:2, :], KQ[:, 0:2, :], table[:, 0:2, :], ALU.mult).then_inc(rot_k, 1)
                if live(0):
                    maxes(k, s, 2)
                if live(3):
                    eng.wait_ge(yx_made, t3 + 1)
                    eng.tensor_tensor(res2[:, r3, :], YX, x1[:, r3, :], ALU.add).then_inc(res2_set, 1)
                    stats(t3, r3, res2, bn2, res2_set, bn2_set)
                    eng.wait_ge(bn2_set, t3 + 1)
                if live(5):
                    after(eng, sent_in[r5], k5 * 32)
                    eng.tensor_copy(x2s[:, r5, :], x2[:, r5, :]).then_inc(x2s_set, 1)
                if live(3):
                    moments(t3, r3, bn2, mv2, mv2_set)
                if live(4) or live(5):
                    eng.wait_ge(mid_made, n - 1)
                    if live(2):
                        eng.wait_ge(x1T_set, t2 + 1)
                    lo, hi = (0 if live(4) else NE), (3 * NE if live(5) else NE)
                    eng.tensor_tensor(gc[:, s, lo:hi], GATE[:, lo:hi], gate_b_sb[:, lo:hi], ALU.add).then_inc(gc_set, 1)
                if live(0):
                    maxes(k, s, 3)
                if live(4):
                    k4, r4 = at(k, s, 4)
                    eng.wait_ge(gc_set, n - 3)
                    eng.tensor_reduce(lmax[:, r4, :], gc[:, r4, 0:NE], AX_X, ALU.max, negate=True).then_inc(lmax_set, 1)
                if live(3):
                    eng.wait_ge(rstd2_set, t3 + 1)
                    after(eng, x2_stored[r3], k3 * 16)
                    after(eng, x2s_set, t3 - 1)
                    after(eng, x2_turned, t3 - 1)
                    eng.tensor_scalar(x2[:, r3, :], res2[:, r3, :], mv2[:, r3, 0:1], rstd2[:, r3, :],
                                      ALU.subtract, ALU.mult).then_inc(x2_set, 1)
                if live(2):
                    eng.wait_ge(xq_made, t2 + 1)
                    for into, table in ((ra, rot_cos), (rb, rot_sin)):
                        eng.tensor_tensor(into[:, r2, 2:4, :], KQ[:, 2:4, :], table[:, 2:4, :], ALU.mult).then_inc(rot_q, 1)

            phases(eng, step)

            steps = [0]

            def planned(ins):
                steps[0] += 1
                ins.then_inc(plan_step, 1)
                eng.wait_ge(plan_step, steps[0])

            eng.wait_ge(base_set, B + 1)
            planned(eng.tensor_scalar(tail_rows[:, :], base[:, :], lane_id, None, ALU.add))
            planned(eng.tensor_tensor(counts[:, 0, :], base[:, :], region_rows, ALU.subtract))
            planned(eng.tensor_scalar(counts_i[:, 0, :], counts[:, 0, :], float(P - 1), None, ALU.add))
            planned(eng.tensor_scalar(counts_i[:, 1, :], counts_i[:, 0, :], P.bit_length() - 1, None, ALU.arith_shift_right))
            planned(eng.tensor_copy(counts[:, 1, :], counts_i[:, 1, :]))
            planned(eng.tensor_tensor(upto[:, :, :], counts[:, 1, :].unsqueeze(1).broadcast_to([P, NE, NE]),
                                      not_later, ALU.mult))
            planned(eng.tensor_reduce(counts[:, 2, :], upto[:, :, :], AX_X, ALU.add))
            planned(eng.tensor_scalar(counts[:, 3, :], counts[:, 1, :], -float(P), float(REGION), ALU.mult, ALU.add))
            planned(eng.tensor_tensor(counts[:, 0, :], counts[:, 2, :], counts[:, 1, :], ALU.subtract))
            planned(eng.tensor_scalar(shifts[:, :], counts[:, 0, :], float(P), None, ALU.mult))
            planned(eng.tensor_tensor(shifts[:, :], shifts[:, :], region_rows, ALU.subtract))
            planned(eng.tensor_tensor(shifted[:, :, :, :].rearrange("p b j e -> p (b j) e"),
                                      pick_all[:, :, :, :].rearrange("p b j e -> p (b j) e"),
                                      shifts[:, :].unsqueeze(1).broadcast_to([P, B * TOPK, NE]), ALU.mult))
            planned(eng.tensor_reduce(shift[:, :, :], shifted[:, :, :, :], AX_X, ALU.add))
            planned(eng.tensor_tensor(back_rows[:, :, :], shift[:, :, :], pos_all[:, :, :], ALU.add))
            planned(eng.tensor_tensor(passed[:, :, :], counts[0:1, 2, :].unsqueeze(1).broadcast_to([1, TILES, NE]),
                                      tile_ids[0:1, :].unsqueeze(2).broadcast_to([1, TILES, NE]), ALU.is_le))
            planned(eng.tensor_reduce(tile_f[:, 0, :], passed[:, :, :], AX_X, ALU.add))
            planned(eng.tensor_scalar(tile_expert[:, :], tile_f[:, 0, :], float(NE - 1), None, ALU.min))
            planned(eng.tensor_tensor(skipped[:, :, :], passed[:, :, :],
                                      counts[0:1, 3, :].unsqueeze(1).broadcast_to([1, TILES, NE]), ALU.mult))
            planned(eng.tensor_reduce(tile_f[:, 1, :], skipped[:, :, :], AX_X, ALU.add))
            planned(eng.tensor_tensor(tile_row[:, :], tile_f[:, 1, :], tile_rows[0:1, :], ALU.add))
            assert steps[0] == PLAN_STEPS

            def shared(q, r, bank0=0):
                for f in range(FFN // P):
                    eng.wait_ge(ssil_set, 2 * q + f + 1)
                    after(eng, sy_made, (q - 1) * QB)
                    eng.scalar_tensor_tensor(out=sgh[:, r, f, :], in0=ps[:, bank0 + 2 * f + 1, :],
                                             scalar=sb1_sb[:, 2 + f:3 + f], in1=ssil[:, r, f, :],
                                             op0=ALU.add, op1=ALU.mult).then_inc(sgh_set, 1)

            for r in range(2):
                shared(r, r, 4 * r)

            def product(i, r):
                eng.wait_ge(sil_set, i + 1)
                after(eng, gh_turned, i - 1)
                eng.tensor_tensor(gate_h[:, r, :], ps[:, r, FFN:2 * FFN], sil[:, r, :], ALU.mult).then_inc(gh_set, 1)

            def out_h(i, r):
                eng.wait_ge(gh_turned, i + 1)
                after(eng, yg_made, i - 1)
                eng.tensor_copy(ghT[:, r, :, :].rearrange("p c t -> p (c t)"), ps[:, 3, 0:FFN]).then_inc(ghT_set, 1)

            product(0, 0)
            out_h(0, 0)
            product(1, 1)
            out_h(1, 1)
            with eng.Fori(1, TILES // 2) as k:
                for r in range(2):
                    product(2 * k + r, r)
                    out_h(2 * k + r, r)

            for r in range(2):
                eng.wait_ge(yg_out[r], 16 * (TILES // 2))

            def indices(q, r):
                eng.tensor_scalar(pos4[:, r, :, :], back_rows[:, bass.ds(q * QB, QB), :], 0.0, None, ALU.add).then_inc(pos4_set, 1)

            def shifts_of(q, r):
                eng.wait_ge(rstd3_set, q + 1)
                eng.scalar_tensor_tensor(out=shift3[:, r, :], in0=mv3[:, r, :, 0], scalar=-1.0, in1=rstd3[:, r, :],
                                         op0=ALU.mult, op1=ALU.mult).then_inc(shift3_set, 1)

            def close(q, k, r, first=False, more=True):
                eng.tensor_scalar(cw4[:, r, :, :], cw_all[:, bass.ds(q * QB, QB), :], 1.0, None, ALU.mult).then_inc(cw4_set, 1)
                eng.wait_ge(x2n_in[r], k * 16 + 16)
                after(eng, y3_set, (q - 1) * QB)
                for b in range(QB):
                    eng.wait_ge(sy_made, q * QB + b + 1)
                    eng.tensor_tensor(ya[:, r, b, :], ps[:, 4 + b, 0:D], x2n[:, r, b, :], ALU.add).then_inc(mix_a, 1)
                if not first:
                    shifts_of(q - 1, 1 - r)
                eng.wait_ge(got_in[r], (k + 1) * (QB * TOPK * 16))
                eng.wait_ge(cw4_set, q + 1)
                for b in range(QB):
                    eng.wait_ge(mix_a, q * QB + b + 1)
                    eng.scalar_tensor_tensor(out=yb[:, r, b, :], in0=got[:, r, b, 0, :], scalar=cw4[:, r, b, 0:1],
                                             in1=ya[:, r, b, :], op0=ALU.mult, op1=ALU.add).then_inc(mix_b, 1)
                for b in range(QB):
                    eng.wait_ge(mix_b, q * QB + b + 1)
                    eng.scalar_tensor_tensor(out=ya[:, r, b, :], in0=got[:, r, b, 1, :], scalar=cw4[:, r, b, 1:2],
                                             in1=yb[:, r, b, :], op0=ALU.mult, op1=ALU.add).then_inc(mix_c, 1)
                for b in range(QB):
                    eng.wait_ge(mix_c, q * QB + b + 1)
                    eng.bn_stats(bn3[:, r, b, :], ya[:, r, b, :]).then_inc(bn3_set, 1)
                eng.wait_ge(bn3_set, (q + 1) * QB)
                if more:
                    indices(q + 2, r)
                for b in range(QB):
                    eng.bn_aggr(mv3[:, r, b, :], bn3[:, r, b, :]).then_inc(mv3_set, 1)
                eng.wait_ge(mv3_set, (q + 1) * QB + q)
                after(eng, rstd3_set, q - 1)
                eng.tensor_scalar(var3[:, r, :], mv3[:, r, :, 1], EPS, None, ALU.add).then_inc(mv3_set, 1)
                if more:
                    shared(q + 2, r)

            for r in range(2):
                indices(r, r)
            for r in range(2):
                close(r, 0, r, first=(r == 0))
            with eng.Fori(1, NQ // 2 - 1) as k:
                for r in range(2):
                    close(2 * k + r, k, r)
            for r in range(2):
                close(NQ - 2 + r, NQ // 2 - 1, r, more=False)
            shifts_of(NQ - 1, 1)


_INS = ['x', 'ctx_1024', 'L0_attn_qkv_weights', 'L0_xattn_Wq', 'L0_xattn_Wk', 'L0_xattn_Wv', 'L0_ffn_gate_w',
        'L0_ffn_gate_b', 'L0_ffn_sw1', 'L0_ffn_sb1', 'L0_ffn_sw2', 'L0_ffn_sb2', 'L0_ffn_rw1', 'L0_ffn_rb1',
        'L0_ffn_rw2', 'L0_ffn_rb2']


def kernel(**inputs):
    import concourse.bacc as _bacc
    from concourse.bass_utils import run_bass_kernel_spmd as _run
    import ml_dtypes

    nc = _bacc.Bacc("TRN2", target_bir_lowering=False, num_devices=1)
    arrays = {name: np.ascontiguousarray(inputs[name]) for name in _INS}
    table_f32, table_bf16 = shape_tables()
    arrays["table_f32"] = table_f32
    arrays["table_bf16"] = table_bf16.astype(ml_dtypes.bfloat16)
    args = [nc.dram_tensor(f"in_{name}", a.shape, mybir.dt.from_np(a.dtype), kind="ExternalInput").ap()
            for name, a in arrays.items()]
    out = nc.dram_tensor("out_0", (B, S, D), F32, kind="ExternalOutput").ap()
    decoder_kernel(nc, *args, out)
    r = _run(nc, [{f"in_{name}": a for name, a in arrays.items()}], core_ids=[0])
    return r.results[0]["out_0"]
```

```python
from contextlib import ExitStack

import numpy as np
import concourse.bass as bass
from concourse import mybir

F32 = mybir.dt.float32
BF16 = mybir.dt.bfloat16
U32 = mybir.dt.uint32
I32 = mybir.dt.int32
ALU = mybir.AluOpType
ACT = mybir.ActivationFunctionType
AX_X = mybir.AxisListType.X

P = 128
B, S, D = 32, 128, 256
DC = D // P
H, DH = 16, 16
NU = S // DH
GB = P // DH
NG = B // GB
NE, TOPK, FFN = 8, 2, 256
VW = 32
CG = P // VW
BANK = 512
REGION = B * S + P
TILES = B * S * TOPK // P + NE - 1
IDLE_ROW = NE * REGION
IDLE = TILES - B * S * TOPK // P
XROWS = IDLE_ROW + IDLE * P
PACKET = D + 1
PADDING = B * S * TOPK
QB = 4
NQ = B // QB
EPS = 1e-5
NEG_INF = -1000000000.0
GAMMA, THETA, SCALE_BASE = 0.96875, 10000.0, 512.0

assert S == P and GB * DH == P and H * DH == D


def shape_tables():
    i = np.arange(P)
    ident = np.eye(P, dtype=np.float32)
    causal = np.where(i[None, :] <= i[:, None], 0.0, NEG_INF).astype(np.float32)
    diff = (i[None, :] - i[:, None]).astype(np.float64)
    decay = np.where(diff >= 0, GAMMA ** np.maximum(diff, 0), 0.0).astype(np.float32)
    half = D // 2
    pos = i.astype(np.float32)
    scale_vec = (np.arange(0, D, 2, dtype=np.float32) + np.float32(0.4 * D)) / np.float32(1.4 * D)
    scale = scale_vec[:, None] ** (pos / np.float32(SCALE_BASE))[None, :]
    freqs = (1.0 / THETA ** (np.arange(half, dtype=np.float32) / half)).astype(np.float32)
    angle = freqs[:, None] * pos[None, :]
    cos, sin = np.cos(angle), np.sin(angle)
    kc, ks, qc, qs = cos / scale, sin / scale, cos * scale, sin * scale
    rot_cos = np.concatenate([kc, kc, qc, qc], 1)
    rot_sin = np.concatenate([ks, -ks, qs, -qs], 1)
    f32 = np.concatenate([ident, decay, rot_cos, rot_sin,
                          np.tile(np.arange(NE), (P, 1)), np.tile(np.arange(NE) * REGION, (P, 1)),
                          i[:, None], np.tile((np.arange(NE)[None, :] <= np.arange(NE)[:, None]).reshape(-1), (P, 1)),
                          np.tile(np.arange(TILES), (P, 1)), np.tile(np.arange(TILES) * P, (P, 1)),
                          ((np.arange(B)[None, :, None] * S + i[:, None, None]) * TOPK
                           + np.arange(TOPK)[None, None, :]).reshape(P, B * TOPK), PADDING + i[:, None]], 1)
    before = (i[:, None] < i[None, :]).astype(np.float32)
    bf = np.concatenate([ident, causal, before, np.ones((P, P))], 1)
    return np.ascontiguousarray(f32, np.float32), np.ascontiguousarray(bf, np.float32)


def at(k, s, lag):
    off = s - lag
    return k + off // 2, off % 2


def decoder_kernel(nc, x, ctx_1024, wqkv, xwq, xwk, xwv, gate_w, gate_b, sw1, sb1, sw2, sb2,
                   rw1, rb1, rw2, rb2, table_f32, table_bf16, out):
    ctx = ExitStack()
    with ctx:
        def sb(name, shape, dt=F32):
            return ctx.enter_context(nc.sbuf_tensor(name, shape, dt))

        def sem(name):
            return ctx.enter_context(nc.semaphore(name))

        xT_dram = nc.dram_tensor("xT_dram", (B, P, DC, P), F32).ap()
        k_dram = nc.dram_tensor("k_dram", (B, DH, GB, 2 * DH * NU), F32).ap()

        x2_dram = nc.dram_tensor("x2_dram", (B, P, D), F32).ap()
        x2T_dram = nc.dram_tensor("x2T_dram", (B, P, DC, P), F32).ap()
        sent = nc.dram_tensor("sent", (XROWS, PACKET), F32).ap()
        back = nc.dram_tensor("back", (PADDING + TILES * P, D), F32).ap()

        ps = ctx.enter_context(nc.psum_tensor("ps", [P, 8, BANK], F32))
        SCORE = [ps[:, 0, :], ps[:, 1, :]]
        PROBT = ps[:, 2, :]
        HEADS = ps[:, 3, :].rearrange("p (h v) -> p h v", v=VW)
        HEADS_T = ps[:, 4, :].rearrange("p (x t) -> p x t", t=P)
        QV = ps[:, 5, :]
        YX = ps[:, 5, 0:D]
        XV = ps[:, 6, 0:D]
        SCX = ps[:, 6, 0:P]
        KQ = ps[:, 6:8, :].rearrange("p b c -> p (b c)")[:, D:3 * D].rearrange("p (r t) -> p r t", t=P)
        TR = ps[:, 7, D:2 * D]
        GATE = ps[:, 7, 0:3 * NE]

        tf = sb("tf", [P, 10 * P + 2 * NE + 1 + NE * NE + 2 * TILES + B * TOPK + 1])
        ident = tf[:, 0:P]
        decay = tf[:, P:2 * P]
        rot_cos = tf[:, 2 * P:6 * P].rearrange("p (r t) -> p r t", t=P)
        rot_sin = tf[:, 6 * P:10 * P].rearrange("p (r t) -> p r t", t=P)
        o = 10 * P
        expert_ids = tf[:, o:o + NE]
        region_rows = tf[:, o + NE:o + 2 * NE]
        lane_id = tf[:, o + 2 * NE:o + 2 * NE + 1]
        o += 2 * NE + 1
        not_later = tf[:, o:o + NE * NE].rearrange("p (e f) -> p e f", f=NE)
        o += NE * NE
        tile_ids = tf[:, o:o + TILES]
        tile_rows = tf[:, o + TILES:o + 2 * TILES]
        o += 2 * TILES
        result_rows = tf[:, o:o + B * TOPK].rearrange("p (b j) -> p b j", j=TOPK)
        padding_row = tf[:, o + B * TOPK:o + B * TOPK + 1]
        tb = sb("tb", [P, 4 * P], BF16)
        before_bf = tb[:, 2 * P:3 * P]
        ones_bf = tb[:, 3 * P:4 * P]
        ident_bf = tb[:, 0:P]
        causal_bf = tb[:, P:2 * P]
        BH, BY = NE * 2 * FFN, NE * D
        attn_only = sb("attn_only", [P, BH + BY])
        taken = [0]

        def take(*dims):
            lo, names = taken[0], "abcd"[:len(dims)]
            taken[0] += int(np.prod(dims))
            assert taken[0] <= BH + BY
            return attn_only[:, lo:taken[0]].rearrange(f"p ({' '.join(names)}) -> p {' '.join(names)}",
                                                       **dict(zip(names, dims)))

        wqkv_sb = take(DC, 3 * D)
        xT = take(2, DC, P)
        kp = take(2, 2, 2 * DH, NU)
        qT = take(2, DC, P)
        FREE_EARLY = taken[0] // (2 * FFN)
        xwq_sb = take(DC, D)
        xwk_sb = take(DC, D)
        xwv_sb = take(DC, D)
        cT = take(2, DC, P)
        xn = take(2, D)
        cn = sb("cn", [P, 2, D])
        rb_h = attn_only[:, 0:BH]
        rb_y = attn_only[:, BH:BH + BY]

        gate_w_sb = sb("gate_w_sb", [P, DC, NE])
        gate_b_sb = sb("gate_b_sb", [P, 3 * NE])
        sw1_sb = sb("sw1_sb", [P, DC, 2 * FFN])
        sw2_sb = sb("sw2_sb", [P, FFN // P, D])
        sb1_sb = sb("sb1_sb", [P, 2 * FFN // P])
        sb2_sb = sb("sb2_sb", [P, D])

        first_use = sb("first_use", [P, 6 * GB * D])

        def part(n, *dims):
            names = "abcd"[:len(dims)]
            return first_use[:, n * GB * D:(n + 1) * GB * D].rearrange(
                f"p ({' '.join(names)}) -> p {' '.join(names)}", **dict(zip(names, dims)))

        xin = [part(NG + r, GB, D) for r in range(2)]
        RW1 = NE * DC * 2 * FFN
        rw1_sb = first_use[:, 0:RW1]
        rw2_sb = first_use[:, RW1:RW1 + NE * FFN // P * D]
        assert RW1 + NE * FFN // P * D <= 6 * GB * D

        va = sb("va", [P, 2, H, VW])
        nmax = sb("nmax", [P, 2, H])
        prob = sb("prob", [P, 2, H, P])
        pT = sb("pT", [P, 4, 4, P])
        oT = sb("oT", [P, H // CG, P])
        rden = sb("rden", [P, 2, H])
        xTn = pT[:, :, :, :].rearrange("p u n t -> p (u n t)").rearrange("p (b c t) -> p b c t", b=GB, c=DC)
        xTu = [prob[:, r, :, :].rearrange("p h t -> p (h t)").rearrange("p (c u b i) -> p c u b i", c=DC, u=NU, b=GB)
               for r in range(2)]
        att = sb("att", [P, 2, D])
        res1 = sb("res1", [P, 2, D])
        bn1 = sb("bn1", [P, 2, 6])
        mv1 = sb("mv1", [P, 2, 2])
        rstd1 = sb("rstd1", [P, 2, 1])
        x1 = sb("x1", [P, 2, D])
        x1T = sb("x1T", [P, 2, DC, P])
        xv = sb("xv", [P, 2, D])
        products = sb("products", [P, 2, 2, 4, P])
        ra, rb = products[:, 0, :, :, :], products[:, 1, :, :, :]
        rot = sb("rot", [P, 2, 4, P])
        scx = sb("scx", [P, 2, P])
        res2 = sb("res2", [P, 2, D])
        bn2 = sb("bn2", [P, 2, 6])
        mv2 = sb("mv2", [P, 2, 2])
        rstd2 = sb("rstd2", [P, 2, 1])
        x2 = sb("x2", [P, 2, D])
        neg_half = sb("neg_half", [P, QB])
        x2T = sb("x2T", [P, 2, DC, P])
        x2b = sb("x2b", [P, 2, D])
        x2s = sb("x2s", [P, 2, TOPK, PACKET])
        gc = sb("gc", [P, 2, 3 * NE])
        lmax = sb("lmax", [P, 2, 1])
        gexp = sb("gexp", [P, 2, NE])
        gsum = sb("gsum", [P, 2, 1])
        ginv = sb("ginv", [P, 2, 1])
        gprob = sb("gprob", [P, 2, NE])
        top_p = sb("top_p", [P, 2, 8])
        top_i = sb("top_i", [P, 2, 8], U32)
        top_f = sb("top_f", [P, 2, TOPK])
        pick = sb("pick", [P, 2, TOPK, NE])
        picks = sb("picks", [P, 2, NE], BF16)
        base = sb("base", [P, NE])
        place = sb("place", [P, 2, NE])
        mine = sb("mine", [P, 2, TOPK, NE])
        pos = sb("pos", [P, 2, TOPK], U32)
        cw_all = sb("cw_all", [P, B, TOPK])
        zeros = sb("zeros", [P, PACKET])
        tail_rows = sb("tail_rows", [P, NE], U32)
        counts = sb("counts", [P, 4, NE])
        counts_i = sb("counts_i", [P, 2, NE], I32)
        upto = sb("upto", [P, NE, NE])
        passed = sb("passed", [1, TILES, NE])
        skipped = sb("skipped", [1, TILES, NE])
        tile_f = sb("tile_f", [1, 2, TILES])
        tile_expert = sb("tile_expert", [1, TILES], I32)
        tile_row = sb("tile_row", [1, TILES], I32)

        xg = sb("xg", [P, 4, PACKET])
        pad_shift = sb("pad_shift", [P, 4])
        result_row = sb("result_row", [P, 4], U32)
        xgT = sb("xgT", [P, 2, DC, P])
        hid = sb("hid", [P, 2, 2 * FFN])
        sil = sb("sil", [P, 2, FFN])
        gate_h = sb("gate_h", [P, 2, FFN])
        ghT = sb("ghT", [P, 2, FFN // P, P])
        yg = sb("yg", [P, 2, D])

        x2T4 = prob[:, 0, :, :].rearrange("p h t -> p (h t)").rearrange("p (r b c t) -> p r b c t", r=2, b=QB, c=DC)
        x2n = prob[:, 1, :, :].rearrange("p h t -> p (h t)").rearrange("p (r b d) -> p r b d", r=2, b=QB)
        ssil = pT[:, :, :, :].rearrange("p (r f) n t -> p r f (n t)", r=2)
        sgh = products[:, :, :, :, :].rearrange("p r f n t -> p r f (n t)")
        ya = first_use[:, 4096:6144].rearrange("p (r b d) -> p r b d", r=2, b=QB)
        yb = first_use[:, 6144:8192].rearrange("p (r b d) -> p r b d", r=2, b=QB)
        got = first_use[:, 8192:12288].rearrange("p (r b j d) -> p r b j d", r=2, b=QB, j=TOPK)
        yc = sb("yc", [P, 2, QB, D])
        y3 = sb("y3", [P, 2, QB, D])
        cw4 = sb("cw4", [P, 2, QB, TOPK])
        bn3 = sb("bn3", [P, 2, QB, 6])
        mv3 = sb("mv3", [P, 2, QB, 2])
        var3 = sb("var3", [P, 2, QB])
        rstd3 = sb("rstd3", [P, 2, QB])
        shift3 = sb("shift3", [P, 2, QB])

        ident_in = sem("ident_in")
        tables_in = sem("tables_in")
        w_in = sem("w_in")
        xw_in = sem("xw_in")
        consts_set = sem("consts_set")
        xin_in = [[sem(f"xin_in{r}{half}") for half in range(2)] for r in range(2)]
        cn_in = [sem("cn_in0"), sem("cn_in1")]
        x_turned = sem("x_turned")
        c_turned = sem("c_turned")
        k_made = sem("k_made")
        xTn_set = sem("xTn_set")
        cT_set = sem("cT_set")
        xTu_set = sem("xTu_set")
        kk_set = sem("kk_set")
        xT_stored = sem("xT_stored")
        k_stored = sem("k_stored")

        xT_in = [sem("xT_in0"), sem("xT_in1")]
        xn_in = [sem("xn_in0"), sem("xn_in1")]
        kp_in = [sem("kp_in0"), sem("kp_in1")]
        qv_made = sem("qv_made")
        q_set = sem("q_set")
        v_set = sem("v_set")
        scored = sem("scored")
        maxed = sem("maxed")
        expd = sem("expd")
        p_turned = sem("p_turned")
        pT_set = sem("pT_set")
        oT_set = sem("oT_set")
        heads_turned = sem("heads_turned")
        heads_made = sem("heads_made")
        den_set = sem("den_set")
        att_set = sem("att_set")
        res1_set = sem("res1_set")
        bn1_set = sem("bn1_set")
        mv1_set = sem("mv1_set")
        rstd1_set = sem("rstd1_set")
        x1_set = sem("x1_set")
        x1T_set = sem("x1T_set")
        xkv_made = sem("xkv_made")
        xv_set = sem("xv_set")
        xq_made = sem("xq_made")
        rot_k = sem("rot_k")
        rot_q = sem("rot_q")
        rot_set = sem("rot_set")
        scx_made = sem("scx_made")
        scx_set = sem("scx_set")
        yx_made = sem("yx_made")
        res2_set = sem("res2_set")
        bn2_set = sem("bn2_set")
        mv2_set = sem("mv2_set")
        rstd2_set = sem("rstd2_set")
        x2_set = sem("x2_set")
        x2_stored = [sem("x2_stored0"), sem("x2_stored1")]
        x2T_stored = [sem("x2T_stored0"), sem("x2T_stored1")]
        small_in = sem("small_in")
        ffn_in = sem("ffn_in")
        x2b_set = sem("x2b_set")
        rb_in = sem("rb_in")
        hid_set = sem("hid_set")
        base_set = sem("base_set")
        x2_turned = sem("x2_turned")
        mid_made = sem("mid_made")
        x2T_set = sem("x2T_set")
        gc_set = sem("gc_set")
        x2s_set = sem("x2s_set")
        lmax_set = sem("lmax_set")
        gexp_set = sem("gexp_set")
        ginv_set = sem("ginv_set")
        gprob_set = sem("gprob_set")
        top_p_set = sem("top_p_set")
        top_i_set = sem("top_i_set")
        top_f_set = sem("top_f_set")
        pick_set = sem("pick_set")
        picks_set = sem("picks_set")
        place_set = sem("place_set")
        kept_set = sem("kept_set")
        zeros_set = sem("zeros_set")
        pad_shifted = sem("pad_shifted")
        packet_row = sem("packet_row")
        mine_set = sem("mine_set")
        pos_set = sem("pos_set")
        sent_in = [sem("sent_in0"), sem("sent_in1")]
        zeros_sent = sem("zeros_sent")
        zeros_put = sem("zeros_put")
        zeros_laid = sem("zeros_laid")
        idle_sent = sem("idle_sent")
        plan_step = sem("plan_step")
        xg_in = [sem(f"xg_in{i}") for i in range(4)]
        yg_out = [sem("yg_out0"), sem("yg_out1")]
        xg_turned = sem("xg_turned")
        xgT_set = sem("xgT_set")
        hid_made = sem("hid_made")
        sil_set = sem("sil_set")
        gh_set = sem("gh_set")
        gh_turned = sem("gh_turned")
        ghT_set = sem("ghT_set")
        yg_made = sem("yg_made")
        yg_set = sem("yg_set")
        x2T4_in = [sem("x2T4_in0"), sem("x2T4_in1")]
        x2n_in = [sem("x2n_in0"), sem("x2n_in1")]
        got_in = [sem("got_in0"), sem("got_in1")]
        shid_made = sem("shid_made")
        ssil_set = sem("ssil_set")
        sgh_set = sem("sgh_set")
        sy_made = sem("sy_made")
        mix_a = sem("mix_a")
        mix_b = sem("mix_b")
        mix_c = sem("mix_c")
        bn3_set = sem("bn3_set")
        mv3_set = sem("mv3_set")
        rstd3_set = sem("rstd3_set")
        shift3_set = sem("shift3_set")
        y3_set = sem("y3_set")
        cw4_set = sem("cw4_set")
        PLAN_STEPS = 14
        TAILS_POOL, TAILS_SP = NE // 4, NE // 4 + 3 * NE // 8
        out_stored = [sem("out_stored0"), sem("out_stored1")]

        block = ctx.enter_context(nc.Block())
        LOAD_AHEAD, LAST_LAG = 2, 6
        FIRST_K, END_K = LAST_LAG // 2 + 1, (B - LOAD_AHEAD) // 2

        def phases(eng, step):
            def peeled(first, end):
                for k in range(first, end):
                    for s in range(2):
                        step(k, s, lambda lag: 0 <= 2 * k + s - lag < B)

            peeled(-LOAD_AHEAD // 2, FIRST_K)
            with eng.Fori(FIRST_K, END_K) as k:
                for s in range(2):
                    step(k, s, lambda lag: True)
            peeled(END_K, (B + LAST_LAG + 1) // 2)

        def after(eng, what, count):
            if not isinstance(count, int) or count > 0:
                eng.wait_ge(what, count)

        def kk_of(g):
            return first_use[:, g * GB * D:(g + 1) * GB * D]

        def rows_done(count):
            return min(count, B) if isinstance(count, int) else count

        @block.sync
        def _(eng):
            def load_x(g):
                for half in range(2):
                    rows = GB // 2
                    eng.dma_start(xin[g % 2][:, half * rows:(half + 1) * rows, :],
                                  x[g * GB + half * rows:g * GB + (half + 1) * rows].rearrange("b p d -> p b d")
                                  ).then_inc(xin_in[g % 2][half], 16)

            eng.dma_start(ident, table_f32[:, 0:P]).then_inc(ident_in, 16)
            load_x(0)
            eng.dma_start(wqkv_sb[:, :, :], wqkv.rearrange("(c p) n -> p c n", p=P)).then_inc(w_in, 16)
            load_x(1)

            def load_small():
                eng.dma_start(gate_w_sb[:, :, :], gate_w.rearrange("(c p) n -> p c n", p=P)).then_inc(small_in, 16)
                eng.dma_start(gate_b_sb[:, 0:NE], gate_b.rearrange("(o n) -> o n", o=1).broadcast_to([P, NE])).then_inc(small_in, 16)
                eng.dma_start(sb1_sb[:, :], sb1[0].rearrange("(c p) -> p c", p=P), allow_slow_non_contiguous=True).then_inc(small_in, 16)
                eng.dma_start(sb2_sb[:, :], sb2.broadcast_to([P, D])).then_inc(small_in, 16)
                eng.dma_start(tf[:, P:], table_f32[:, P:]).then_inc(tables_in, 16)
                eng.dma_start(tb[:, :], table_bf16).then_inc(tables_in, 16)
                for w, src in ((xwq_sb, xwq), (xwk_sb, xwk), (xwv_sb, xwv)):
                    eng.dma_start(w[:, :, :], src.rearrange("(c p) n -> p c n", p=P)).then_inc(xw_in, 16)

            def store_k(g):
                eng.wait_ge(kk_set, g * 4 + 4)
                eng.dma_start(k_dram[g * GB:(g + 1) * GB].rearrange("b i g f -> (b i) (g f)"),
                              kk_of(g)).then_inc(k_stored, 16)

            def store_x(g):
                eng.wait_ge(xTn_set, g * 4 + 4)
                eng.dma_start(xT_dram[g * GB:(g + 1) * GB].rearrange("b p c t -> p b c t"), xTn[:, :, :, :]).then_inc(xT_stored, 16)

            for g in range(NG):
                store_x(g)
                if g + 2 < NG:
                    eng.wait_ge(x_turned, g * 4 + 4)
                    load_x(g + 2)
                if g == 0:
                    load_small()
                else:
                    store_k(g - 1)
            eng.wait_ge(xT_stored, 16)
            eng.wait_ge(k_stored, 16)

            def load_rb_h(first, end):
                for e in range(first, end):
                    eng.dma_start(rb_h[:, e * 2 * FFN:(e + 1) * 2 * FFN], rb1[e:e + 1, :].broadcast_to([P, 2 * FFN])
                                  ).then_inc(rb_in, 16)

            def load_turned(q, r):
                eng.dma_start(x2T4[:, r, :, :, :], x2T_dram[bass.ds(q * QB, QB)].rearrange("b p c t -> p b c t")
                              ).then_inc(x2T4_in[r], 16)

            def load_rows(q, r):
                eng.dma_start(x2n[:, r, :, :], x2_dram[bass.ds(q * QB, QB)].rearrange("b p d -> p b d")
                              ).then_inc(x2n_in[r], 16)

            def step(k, s, live):
                if live(-2):
                    kk_, r = at(k, s, -2)
                    t = kk_ * 2 + r
                    after(eng, qv_made, t - 1)
                    eng.dma_start(xT[:, r, :, :], xT_dram[t]).then_inc(xT_in[r], 16)
                if live(-1):
                    kk_, r = at(k, s, -1)
                    t = kk_ * 2 + r
                    after(eng, scored, (t - 1) * 4)
                    if isinstance(t, int) and t < 2:
                        eng.wait_ge(consts_set, 2)
                    for j in range(GB):
                        lo = 16 * j
                        eng.dma_start(kp[lo:lo + DH, r, j % 2, :, :].rearrange("p a u -> p (a u)"),
                                      k_dram[t, :, j, :]).then_inc(kp_in[r], 16)
                if isinstance(k, int) and 2 * k + s == -1:
                    store_k(NG - 1)
                if isinstance(k, int) and 2 * k + s == 1:
                    eng.wait_ge(xT_stored, 16 * NG)
                    eng.wait_ge(k_stored, 16 * NG)
                if isinstance(k, int) and 1 < 2 * k + s <= 1 + NE // 2:
                    if 2 * k + s == 2:
                        eng.dma_start(sw1_sb[:, :, :], sw1[0].rearrange("(c p) n -> p c n", p=P)).then_inc(ffn_in, 16)
                        eng.dma_start(sw2_sb[:, :, :], sw2[0].rearrange("(c p) n -> p c n", p=P)).then_inc(ffn_in, 16)
                    for e in range(2 * (2 * k + s - 2), 2 * (2 * k + s - 1)):
                        lo = e * DC * 2 * FFN
                        eng.dma_start(rw1_sb[:, lo:lo + DC * 2 * FFN].rearrange("p (c n) -> p c n", c=DC),
                                      rw1[e].rearrange("(c p) n -> p c n", p=P)).then_inc(ffn_in, 16)
                        lo = e * FFN // P * D
                        eng.dma_start(rw2_sb[:, lo:lo + FFN // P * D].rearrange("p (c n) -> p c n", c=FFN // P),
                                      rw2[e].rearrange("(c p) n -> p c n", p=P)).then_inc(ffn_in, 16)
                if live(0):
                    kk_, r = at(k, s, 0)
                    t = kk_ * 2 + r
                    after(eng, c_turned, t - 1)
                    eng.dma_start(cn[:, r, :], ctx_1024[t]).then_inc(cn_in[r], 16)
                if live(1):
                    kk_, r = at(k, s, 1)
                    t = kk_ * 2 + r
                    after(eng, res1_set, t - 1)
                    eng.dma_start(xn[:, r, :], x[t]).then_inc(xn_in[r], 16)
                if isinstance(k, int) and 2 * k + s == B:
                    eng.wait_ge(qv_made, B)
                    eng.wait_ge(scored, 4 * B)
                    load_rb_h(0, FREE_EARLY)
                if live(4):
                    kk_, r = at(k, s, 4)
                    t = kk_ * 2 + r
                    eng.wait_ge(x2b_set, t + 1)
                    eng.dma_start(x2_dram[t], x2b[:, r, :]).then_inc(x2_stored[r], 16)
                    eng.wait_ge(x2T_set, t + 1)
                    eng.dma_start(x2T_dram[t], x2T[:, r, :, :]).then_inc(x2T_stored[r], 16)
                if isinstance(k, int) and 2 * k + s == B:
                    eng.wait_ge(p_turned, 4 * B)
                    for row in range(2):
                        eng.wait_ge(x2T_stored[row], 16 * QB)
                    for q in range(2):
                        load_turned(q, q)
                if isinstance(k, int) and 2 * k + s == B + 1:
                    eng.wait_ge(xq_made, B)
                    eng.wait_ge(res1_set, B)
                    load_rb_h(FREE_EARLY, NE)
                    eng.dma_start(rb_y, rb2.rearrange("(o e) n -> o (e n)", o=1).broadcast_to([P, BY])).then_inc(rb_in, 16)

            phases(eng, step)
            for r in range(2):
                eng.wait_ge(x2_stored[r], 16 * (B // 2))
                eng.wait_ge(x2T_stored[r], 16 * (B // 2))
            eng.wait_ge(plan_step, 1)
            for e in range(TAILS_POOL, TAILS_SP):
                end = eng.value_load(tail_rows[0:1, e:e + 1], min_val=0, max_val=IDLE_ROW - P)
                eng.dma_start(sent[bass.ds(end, P), :], zeros[:, :]).then_inc(zeros_put, 16)

            def load_back(q, r):
                eng.dma_start(got[:, r, :, :, :].rearrange("p b j d -> p b (j d)"),
                              back[bass.ds(q * (QB * P * TOPK), QB * P * TOPK), :].rearrange("(b p j) d -> p b (j d)", p=P, j=TOPK)
                              ).then_inc(got_in[r], 16)

            eng.wait_ge(plan_step, PLAN_STEPS)
            for r in range(2):
                eng.wait_ge(sent_in[r], 32 * (B // 2))
            eng.wait_ge(zeros_sent, 16 * TAILS_POOL)
            eng.wait_ge(zeros_put, 16 * (TAILS_SP - TAILS_POOL))
            eng.wait_ge(zeros_laid, 16 * (NE - TAILS_SP))
            eng.wait_ge(idle_sent, 16)
            for i in range(3):
                row = eng.value_load(tile_row[0:1, i:i + 1], min_val=0, max_val=XROWS - P)
                eng.dma_start(xg[:, i, :], sent[bass.ds(row, P), :]).then_inc(xg_in[i], 16)
            for r in range(2):
                eng.wait_ge(xg_in[r], 32)
                load_rows(r, r)
            for r in range(2):
                eng.wait_ge(xg_in[2 + r], 32)
                eng.wait_ge(shid_made, 2 * r + 2)
                load_turned(r + 2, r)

            for r in range(2):
                eng.wait_ge(yg_out[r], 16 * ((TILES + 1 - r) // 2))
            for r in range(2):
                load_back(r, r)

            def store_out(q, r):
                eng.wait_ge(y3_set, (q + 1) * QB)
                eng.dma_start(out[bass.ds(q * QB, QB)].rearrange("b p d -> p b d"), y3[:, r, :, :]).then_inc(out_stored[r], 16)

            def turn(k, r, first=False, more=True, further=True):
                q = 2 * k + r
                if not first:
                    store_out(q - 1, 1 - r)
                if more:
                    eng.wait_ge(mix_a, (q + 2) * QB)
                    load_rows(q + 3, 1 - r)
                    eng.wait_ge(mix_b, (q + 2) * QB)
                    load_back(q + 3, 1 - r)
                if further:
                    eng.wait_ge(shid_made, 2 * (q + 2) + 2)
                    load_turned(q + 4, r)

            eng.wait_ge(mix_a, QB)
            load_rows(2, 0)
            eng.wait_ge(mix_c, QB)
            load_back(2, 0)
            turn(0, 0, first=True)
            turn(0, 1)
            with eng.Fori(1, NQ // 2 - 2) as k:
                for r in range(2):
                    turn(k, r)
            turn(NQ // 2 - 2, 0, further=False)
            turn(NQ // 2 - 2, 1, more=False, further=False)
            for r in range(2):
                turn(NQ // 2 - 1, r, more=False, further=False)
            store_out(NQ - 1, 1)
            for r in range(2):
                eng.wait_ge(out_stored[r], 16 * (NQ // 2))

        @block.gpsimd
        def _(eng):
            eng.memset(neg_half[:, :], -0.5)
            eng.memset(zeros[:, :], 0.0)
            eng.memset(gate_b_sb[:, NE:3 * NE], 0.0)
            eng.memset(va[:, :, :, :], 0.0).then_inc(consts_set, 1)
            eng.wait_ge(consts_set, 1)
            eng.memset(va[:, :, :, DH:DH + 1], 1.0)
            eng.memset(kp[:, :, :, :, :], 0.0).then_inc(consts_set, 1)
            eng.wait_ge(consts_set, 2)

            def step(k, s, live):
                def turn_into(t, r, m, parts):
                    eng.wait_ge(parts, 2 * t + 2)
                    after(eng, scx_made, t - 1)
                    for e in range(2):
                        eng.tensor_tensor(rot[:, r, m + e, :], ra[:, r, m + e, :], rb[:, r, m + 1 - e, :],
                                          ALU.add).then_inc(rot_set, 1)

                k2, r2 = at(k, s, 2)
                t2 = k2 * 2 + r2
                if live(2):
                    eng.wait_ge(mv1_set, 2 * t2 + 2)
                    eng.tensor_tensor(rstd1[:, r2, :], mv1[:, r2, 1:2], neg_half[:, 0:1], ALU.pow).then_inc(rstd1_set, 1)
                    turn_into(t2, r2, 0, rot_k)
                if live(4):
                    kk_, r = at(k, s, 4)
                    t = kk_ * 2 + r
                    eng.wait_ge(x2_set, t + 1)
                    if isinstance(t, int) and t < 2:
                        eng.wait_ge(small_in, 64)
                    after(eng, x2_stored[r], kk_ * 16)
                    eng.tensor_tensor(x2b[:, r, :], x2[:, r, :], sb2_sb[:, :], ALU.add).then_inc(x2b_set, 1)
                if live(3):
                    kk_, r = at(k, s, 3)
                    t = kk_ * 2 + r
                    eng.wait_ge(mv2_set, 2 * t + 2)
                    eng.tensor_tensor(rstd2[:, r, :], mv2[:, r, 1:2], neg_half[:, 0:1], ALU.pow).then_inc(rstd2_set, 1)
                if live(6):
                    kk_, r = at(k, s, 6)
                    eng.wait_ge(pos_set, kk_ * 2 + r + 1)
                if live(2):
                    turn_into(t2, r2, 2, rot_q)
                if isinstance(k, int) and 2 * k + s == 2:
                    eng.wait_ge(zeros_set, 1)
                    eng.dma_start(sent[IDLE_ROW:XROWS, :].rearrange("(n p) d -> p n d", p=P),
                                  zeros[:, :].unsqueeze(1).broadcast_to([P, IDLE, PACKET])).then_inc(idle_sent, 16)
                if live(6):
                    kk_, r = at(k, s, 6)
                    for j in range(TOPK):
                        eng.indirect_dma_start(sent, bass.IndirectOffsetOnAxis(ap=pos[:, r, j:j + 1], axis=0),
                                               x2s[:, r, j, :], None).then_inc(sent_in[r], 16)

            phases(eng, step)
            eng.wait_ge(plan_step, 1)
            for e in range(TAILS_POOL):
                eng.indirect_dma_start(sent, bass.IndirectOffsetOnAxis(ap=tail_rows[:, e:e + 1], axis=0),
                                       zeros[:, :], None).then_inc(zeros_sent, 16)

            def product(i, r, more=True):
                eng.wait_ge(sil_set, i + 1)
                after(eng, gh_turned, i - 1)
                if more:
                    eng.wait_ge(yg_set, i - 1)
                    eng.wait_ge(packet_row, i - 1)
                eng.tensor_tensor(gate_h[:, r, :], hid[:, r, FFN:2 * FFN], sil[:, r, :], ALU.mult).then_inc(gh_set, 1)

            def send_back(slot):
                eng.indirect_dma_start(back, bass.IndirectOffsetOnAxis(ap=result_row[:, slot:slot + 1], axis=0),
                                       yg[:, slot % 2, :], None).then_inc(yg_out[slot % 2], 16)

            for i in range(2):
                product(i, i, more=False)
            for i in range(2, 4):
                product(i, i % 2)
                send_back(i - 2)
            with eng.Fori(1, TILES // 4) as k:
                for n in range(4):
                    product(4 * k + n, n % 2)
                    send_back((n - 2) % 4)
            for i in range(TILES // 4 * 4, TILES):
                product(i, i % 2)
                send_back((i - 2) % 4)
            for i in range(TILES - 2, TILES):
                eng.wait_ge(yg_set, i + 1)
                eng.wait_ge(packet_row, i + 1)
                send_back(i % 4)

            def root(q, r):
                eng.wait_ge(mv3_set, (q + 1) * (QB + 1))
                eng.tensor_tensor(rstd3[:, r, :], var3[:, r, :], neg_half[:, :], ALU.pow).then_inc(rstd3_set, 1)

            with eng.Fori(0, NQ // 2) as k:
                for r in range(2):
                    root(2 * k + r, r)

        @block.tensor
        def _(eng):
            eng.wait_ge(ident_in, 16)
            def turn_group(g):
                for j in range(4):
                    if j % 2 == 0:
                        eng.wait_ge(xin_in[g % 2][j // 2], g // 2 * 16 + 16)
                    if g > 0:
                        eng.wait_ge(xTu_set, (g - 1) * 8 + 2 * j + 2)
                    for i in range(4):
                        mm = eng.transpose(ps[:, j, i * P:(i + 1) * P],
                                           xin[g % 2][:, 2 * j + i // 2, (i % 2) * P:(i % 2 + 1) * P], ident)
                    mm.then_inc(x_turned, 1)

            def project_k(g):
                if g == 0:
                    eng.wait_ge(w_in, 16)
                eng.wait_ge(xTu_set, g * 8 + 8)
                for j in range(4):
                    if g > 0:
                        eng.wait_ge(kk_set, (g - 1) * 4 + j + 1)
                    for i in range(2):
                        for c in range(DC):
                            mm = eng.matmul(ps[:, 4 + j, i * D:(i + 1) * D].rearrange("p (g c d) -> p g c d", c=2, d=DH),
                                            xTu[g % 2][:, c, 2 * j + i, :, :].rearrange("p b i -> p (b i)"),
                                            wqkv_sb[:, c, D:2 * D].rearrange("p (c g d) -> p g c d", c=2, d=DH),
                                            start=(c == 0), stop=(c == DC - 1))
                    mm.then_inc(k_made, 1)

            turn_group(0)
            for g in range(NG):
                if g + 1 < NG:
                    turn_group(g + 1)
                project_k(g)
            eng.wait_ge(kk_set, 4 * NG - 2)
            eng.wait_ge(tables_in, 32)
            eng.wait_ge(xw_in, 48)
            eng.wait_ge(small_in, 64)
            eng.wait_ge(consts_set, 2)

            def project(k, s, lag):
                kk_, r = at(k, s, lag)
                t = kk_ * 2 + r
                eng.wait_ge(xT_in[r], kk_ * 16 + 16)
                after(eng, res2_set, t - 3)
                after(eng, q_set, t)
                after(eng, v_set, t)
                for m in range(DC):
                    for c in range(DC):
                        eng.matmul(QV[:, m * P:(m + 1) * P], wqkv_sb[:, c, m * P:(m + 1) * P], xT[:, r, c, :],
                                   start=(c == 0), stop=(c == DC - 1))
                for c in range(DC):
                    mm = eng.matmul(QV[:, D:2 * D], xT[:, r, c, :], wqkv_sb[:, c, 2 * D:3 * D],
                                    start=(c == 0), stop=(c == DC - 1))
                mm.then_inc(qv_made, 1)

            def scores(k, s, u):
                kk_, r = at(k, s, 0)
                t = kk_ * 2 + r
                if u == 0:
                    eng.wait_ge(q_set, t + 1)
                    eng.wait_ge(kp_in[r], kk_ * 128 + 128)
                after(eng, expd, t * 4 + u - 1)
                bank = SCORE[u % 2]
                eng.matmul(bank.rearrange("p (h j) -> p h j", j=P), ident_bf,
                           causal_bf.unsqueeze(1).broadcast_to([P, 4, P]), start=True, stop=False,
                           skip_group_check=True)
                for c in range(2):
                    for e in range(2):
                        n = 2 * c + e
                        mm = eng.matmul(bank[:, n * P:(n + 1) * P].rearrange("p (d u) -> p d u", u=NU),
                                        qT[32 * u:32 * u + 32, r, c, :],
                                        kp[32 * u:32 * u + 32, r, e, c * DH:(c + 1) * DH, :],
                                        start=False, stop=(n == 3), skip_group_check=True)
                mm.then_inc(scored, 1)

            def turn_probs(k, s, u):
                kk_, r = at(k, s, 1)
                t = kk_ * 2 + r
                eng.wait_ge(expd, t * 4 + u + 1)
                after(eng, pT_set, t * 4 + u)
                for n in range(4):
                    mm = eng.transpose(PROBT[:, n * P:(n + 1) * P], prob[:, r, 4 * u + n, :], ident)
                mm.then_inc(p_turned, 1)

            def weigh(k, s, u0):
                kk_, r = at(k, s, 1)
                t = kk_ * 2 + r
                eng.wait_ge(pT_set, t * 4 + u0 + 2)
                if u0 == 0:
                    eng.wait_ge(v_set, t + 1)
                    after(eng, oT_set, t)
                for c in range(2):
                    for u in (u0, u0 + 1):
                        for e in range(2):
                            h = 8 * c + 2 * u + e
                            lo = h % CG * VW
                            mm = eng.matmul(HEADS_T[lo:lo + VW, h // CG, :], va[:, r, h, :], pT[:, u, 2 * c + e, :],
                                            start=True, stop=True)
                mm.then_inc(heads_made, 1)

            def shared_half(r, f, half, bank0=0):
                cols = half * FFN + f * P
                for c in range(DC):
                    mm = eng.matmul(ps[:, bank0 + 2 * f + half, :].rearrange("p (b t) -> p b t", b=QB),
                                    sw1_sb[:, c, cols:cols + P], x2T4[:, r, :, c, :],
                                    start=(c == 0), stop=(c == DC - 1))
                if half == 1:
                    mm.then_inc(shid_made, 1)

            def shared(q, k, r, bank0=0):
                eng.wait_ge(x2T4_in[r], k * 16 + 16)
                for f in range(FFN // P):
                    after(eng, sgh_set, (q - 1) * 2 + f + 1 if not isinstance(q, int) or q >= 2 else 0)
                    for half in range(2):
                        shared_half(r, f, half, bank0)

            def shared_first(n):
                if n == B + 1:
                    eng.wait_ge(x2T4_in[0], 16)
                    eng.wait_ge(ffn_in, 16 * (2 + 2 * NE))
                    eng.wait_ge(expd, 4 * B)
                    shared_half(0, 0, 0)
                if n == B + 2:
                    shared_half(0, 0, 1)
                if n == B + 3:
                    eng.wait_ge(pT_set, 4 * B)
                    shared_half(0, 1, 0)
                if n == B + 4:
                    eng.wait_ge(att_set, B)
                    shared_half(0, 1, 1)

            def step(k, s, live):
                n = 2 * k + s
                k2, r2 = at(k, s, 2)
                t2 = k2 * 2 + r2
                k3, r3 = at(k, s, 3)
                t3 = k3 * 2 + r3
                k4, r4 = at(k, s, 4)
                t4 = k4 * 2 + r4
                if isinstance(k, int) and n == 0:
                    eng.wait_ge(kk_set, 4 * NG)
                if live(0):
                    scores(k, s, 0)
                if live(1):
                    turn_probs(k, s, 0)
                if live(2):
                    eng.wait_ge(oT_set, t2 + 1)
                    after(eng, att_set, t2)
                    for b in range(H // CG):
                        mm = eng.transpose(ps[:, 3, b * P:(b + 1) * P], oT[:, b, :], ident)
                    mm.then_inc(heads_turned, 1)
                if live(1):
                    k1, r1 = at(k, s, 1)
                    t1 = k1 * 2 + r1
                    eng.wait_ge(cn_in[r1], k1 * 16 + 16)
                    after(eng, rot_q, 2 * (t1 - 1))
                    after(eng, cT_set, t1)
                    for c in range(DC):
                        mm = eng.transpose(ps[:, 7, c * P:(c + 1) * P], cn[:, r1, c * P:(c + 1) * P], ident)
                    mm.then_inc(c_turned, 1)
                if live(4):
                    eng.wait_ge(x2_set, t4 + 1)
                    eng.wait_ge(rot_q, 2 * rows_done(t4 + 2))
                    for c in range(DC):
                        mm = eng.transpose(TR[:, c * P:(c + 1) * P], x2[:, r4, c * P:(c + 1) * P], ident)
                    mm.then_inc(x2_turned, 1)
                if live(3):
                    eng.wait_ge(rot_set, 4 * t3 + 4)
                    eng.wait_ge(xv_set, t3 + 1)
                    for m in range(2):
                        mm = eng.matmul(SCX, rot[:, r3, m, :], rot[:, r3, 2 + m, :], start=(m == 0), stop=(m == 1))
                    mm.then_inc(scx_made, 1)
                if live(0):
                    scores(k, s, 1)
                if live(1):
                    turn_probs(k, s, 1)
                if live(2):
                    eng.wait_ge(cT_set, t2 + 1)
                    after(eng, scx_set, t2)
                    for m in range(2):
                        for c in range(DC):
                            eng.matmul(KQ[:, m, :], xwk_sb[:, c, m:D:2], cT[:, r2, c, :],
                                       start=(c == 0), stop=(c == DC - 1))
                    for c in range(DC):
                        mm = eng.matmul(XV, cT[:, r2, c, :], xwv_sb[:, c, :], start=(c == 0), stop=(c == DC - 1))
                    mm.then_inc(xkv_made, 1)
                if live(1):
                    weigh(k, s, 0)
                if live(0):
                    scores(k, s, 2)
                if live(1):
                    turn_probs(k, s, 2)
                if live(3):
                    eng.wait_ge(scx_set, t3 + 1)
                    eng.wait_ge(q_set, rows_done(t3 + 4))
                    eng.wait_ge(v_set, rows_done(t3 + 4))
                    eng.matmul(YX, scx[:, r3, :], xv[:, r3, :], start=True, stop=True).then_inc(yx_made, 1)
                if live(2) or live(3) or live(4) or live(5):
                    if live(2):
                        eng.wait_ge(x1_set, t2 + 1)
                    if live(1):
                        eng.wait_ge(cT_set, t1 + 1)
                    if live(4):
                        eng.wait_ge(x2T_set, t4 + 1)
                    if live(5):
                        k5, r5 = at(k, s, 5)
                        eng.wait_ge(picks_set, k5 * 2 + r5 + 1)
                        after(eng, gc_set, n - 4)
                    if live(2):
                        for c in range(DC):
                            mm = eng.transpose(TR[:, c * P:(c + 1) * P], x1[:, r2, c * P:(c + 1) * P], ident)
                    if live(4):
                        for c in range(DC):
                            mm = eng.matmul(GATE[:, 0:NE], x2T[:, r4, c, :], gate_w_sb[:, c, :], start=(c == 0), stop=(c == DC - 1))
                    if live(5):
                        eng.matmul(GATE[:, NE:2 * NE], before_bf, picks[:, r5, :], start=True, stop=True)
                        mm = eng.matmul(GATE[:, 2 * NE:3 * NE], ones_bf, picks[:, r5, :], start=True, stop=True)
                    mm.then_inc(mid_made, 1)
                if isinstance(k, int):
                    shared_first(2 * k + s)
                if live(0):
                    scores(k, s, 3)
                if live(1):
                    turn_probs(k, s, 3)
                if live(-1):
                    project(k, s, -1)
                if live(1):
                    weigh(k, s, 2)
                if live(2):
                    eng.wait_ge(x1T_set, t2 + 1)
                    after(eng, gc_set, n - 3)
                    for m in range(2):
                        for c in range(DC):
                            mm = eng.matmul(KQ[:, 2 + m, :], xwq_sb[:, c, m:D:2], x1T[:, r2, c, :],
                                            start=(c == 0), stop=(c == DC - 1))
                    mm.then_inc(xq_made, 1)

            phases(eng, step)

            eng.wait_ge(gc_set, B + 1)
            shared(1, 0, 1, 4)

            eng.wait_ge(sgh_set, FFN // P)
            eng.wait_ge(plan_step, PLAN_STEPS)
            XGT = ps[:, 2, 0:D]
            GHT = ps[:, 3, 0:FFN]

            def turn_x(i, slot, loads):
                eng.wait_ge(xg_in[slot], loads * 16)
                after(eng, xgT_set, i)
                for c in range(DC):
                    mm = eng.transpose(XGT[:, c * P:(c + 1) * P], xg[:, slot, c * P:(c + 1) * P], ident)
                mm.then_inc(xg_turned, 1)

            def turn_h(i, r):
                eng.wait_ge(gh_set, i + 1)
                after(eng, ghT_set, i)
                for c in range(FFN // P):
                    mm = eng.transpose(GHT[:, c * P:(c + 1) * P], gate_h[:, r, c * P:(c + 1) * P], ident)
                mm.then_inc(gh_turned, 1)

            def hidden(i, r, e):
                eng.wait_ge(xgT_set, i + 1)
                after(eng, hid_set, i - 1)
                for c in range(DC):
                    mm = eng.matmul(ps[:, r, :], xgT[:, r, c, :],
                                    rw1_sb[:, bass.ds(e * (DC * 2 * FFN) + c * 2 * FFN, 2 * FFN)],
                                    start=(c == 0), stop=(c == DC - 1))
                mm.then_inc(hid_made, 1)

            def result(i, r, e):
                if isinstance(i, int) and i == 0:
                    eng.wait_ge(sgh_set, 2 * FFN // P)
                eng.wait_ge(ghT_set, i + 1)
                after(eng, yg_set, i - 1)
                for c in range(FFN // P):
                    mm = eng.matmul(ps[:, 4 + r, 0:D], ghT[:, r, c, :],
                                    rw2_sb[:, bass.ds(e * (FFN // P * D) + c * D, D)],
                                    start=(c == 0), stop=(c == FFN // P - 1))
                mm.then_inc(yg_made, 1)

            def expert(i):
                return eng.value_load(tile_expert[0:1, bass.ds(i, 1)], min_val=0, max_val=NE - 1)

            def tiles(k, many=4):
                first, last = isinstance(k, int) and k == 0, isinstance(k, int) and k > 0
                read = {}
                for n in range(many):
                    i = 4 * k + n
                    ends = last and n == many - 1
                    if not (first and n < 2) and n - 2 not in read:
                        read[n - 2] = expert(i - 2)
                    if not ends:
                        read[n + 1] = expert(i + 1)
                        turn_x(i + 1, (n + 1) % 4, k + 1 + (n + 1) // 4)
                    if not (first and n == 0):
                        turn_h(i - 1, (n - 1) % 2)
                    if not (first and n < 2):
                        result(i - 2, n % 2, read[n - 2])
                    if not ends:
                        hidden(i + 1, (n + 1) % 2, read[n + 1])

            turn_x(0, 0, 1)
            hidden(0, 0, expert(0))
            tiles(0)
            with eng.Fori(1, TILES // 4) as k:
                tiles(k)
            tiles(TILES // 4, TILES % 4)
            two_before, before = expert(TILES - 2), expert(TILES - 1)

            def output(q, r, b):
                for c in range(FFN // P):
                    mm = eng.matmul(ps[:, 4 + b, 0:D], sgh[:, r, c, b * P:(b + 1) * P], sw2_sb[:, c, :],
                                    start=(c == 0), stop=(c == FFN // P - 1))
                mm.then_inc(sy_made, 1)

            def outputs(q, r):
                eng.wait_ge(sgh_set, 2 * q + 2)
                for b in range(QB):
                    if isinstance(q, int) and q == 1:
                        eng.wait_ge(mix_a, b + 1)
                    else:
                        eng.wait_ge(mix_c, (q - 1) * QB + b + 1)
                    output(q, r, b)

            result(TILES - 2, TILES % 2, two_before)
            output(0, 0, 2)
            turn_h(TILES - 1, (TILES - 1) % 2)
            output(0, 0, 3)
            result(TILES - 1, (TILES - 1) % 2, before)
            eng.wait_ge(yg_set, TILES - 1)
            output(0, 0, 1)
            eng.wait_ge(yg_set, TILES)
            output(0, 0, 0)

            for r in range(2):
                shared(2 + r, 1, r)
                outputs(1 + r, 1 - r)
            with eng.Fori(2, NQ // 2) as k:
                for r in range(2):
                    shared(2 * k + r, k, r)
                    outputs(2 * k + r - 1, 1 - r)
            outputs(NQ - 1, 1)

        @block.scalar
        def _(eng):
            for g in range(NG):
                if g > 0:
                    eng.wait_ge(xT_stored, g * 16)
                for j in range(4):
                    eng.wait_ge(x_turned, g * 4 + j + 1)
                    eng.copy(xTn[:, 2 * j:2 * j + 2, :, :].rearrange("p b c t -> p (b c t)"), ps[:, j, :]).then_inc(xTn_set, 1)

            def exps(k, s, u):
                kk_, r = at(k, s, 0)
                t = kk_ * 2 + r
                eng.wait_ge(maxed, t * 4 + u + 1)
                after(eng, p_turned, (t - 2) * 4 + u + 1)
                for n in range(4):
                    ins = eng.activation(prob[:, r, 4 * u + n, :], SCORE[u % 2][:, n * P:(n + 1) * P], ACT.Exp,
                                         bias=nmax[:, r, 4 * u + n:4 * u + n + 1])
                ins.then_inc(expd, 1)

            def out_probs(k, s, u):
                kk_, r = at(k, s, 1)
                t = kk_ * 2 + r
                eng.wait_ge(p_turned, t * 4 + u + 1)
                after(eng, heads_made, 2 * t - 1 + u // 2)
                eng.copy(pT[:, u, :, :].rearrange("p n t -> p (n t)"), PROBT).then_inc(pT_set, 1)

            def step(k, s, live):
                n = 2 * k + s
                kp_, rp = at(k, s, -1)
                tp = kp_ * 2 + rp
                k1, r1 = at(k, s, 1)
                t1 = k1 * 2 + r1
                k2, r2 = at(k, s, 2)
                t2 = k2 * 2 + r2
                k4, r4 = at(k, s, 4)
                t4 = k4 * 2 + r4
                if live(1):
                    out_probs(k, s, 0)
                if live(0):
                    exps(k, s, 0)
                if live(4):
                    eng.wait_ge(x2_turned, t4 + 1)
                    after(eng, x2T_stored[r4], k4 * 16)
                    after(eng, mid_made, n - 3)
                    eng.copy(x2T[:, r4, :, :].rearrange("p c t -> p (c t)"), TR).then_inc(x2T_set, 1)
                if live(1):
                    eng.wait_ge(c_turned, t1 + 1)
                    after(eng, xkv_made, t1 - 1)
                    eng.copy(cT[:, r1, :, :].rearrange("p c t -> p (c t)"), ps[:, 7, 0:D]).then_inc(cT_set, 1)
                if live(1):
                    out_probs(k, s, 1)
                if live(0):
                    exps(k, s, 1)
                if live(2):
                    eng.wait_ge(xkv_made, t2 + 1)
                    after(eng, yx_made, t2 - 1)
                    eng.copy(xv[:, r2, :], XV).then_inc(xv_set, 1)
                if live(1):
                    out_probs(k, s, 2)
                if live(0):
                    exps(k, s, 2)
                if live(2):
                    eng.wait_ge(mid_made, t2 + 1)
                    after(eng, xq_made, t2 - 1)
                    eng.copy(x1T[:, r2, :, :].rearrange("p c t -> p (c t)"), TR).then_inc(x1T_set, 1)
                if live(1):
                    out_probs(k, s, 3)
                if live(0):
                    exps(k, s, 3)
                if live(4):
                    eng.wait_ge(lmax_set, t4 + 1)
                    eng.activation(gexp[:, r4, :], gc[:, r4, 0:NE], ACT.Exp, bias=lmax[:, r4, :],
                                   accum_out=gsum[:, r4, :]).then_inc(gexp_set, 1)
                if live(-1):
                    eng.wait_ge(qv_made, tp + 1)
                    after(eng, scored, (tp - 1) * 4)
                    eng.mul(qT[:, rp, :, :].rearrange("p c t -> p (c t)"), QV[:, 0:D], 1.0 / np.sqrt(DH)).then_inc(q_set, 1)
                    after(eng, heads_made, 2 * (tp - 1))
                    if isinstance(tp, int) and tp < 2:
                        eng.wait_ge(consts_set, 2)
                    eng.copy(va[:, rp, :, 0:DH], QV[:, D:2 * D].rearrange("p (h d) -> p h d", d=DH)).then_inc(v_set, 1)
                if live(1):
                    eng.wait_ge(heads_made, 2 * t1 + 2)
                    after(eng, heads_turned, t1)
                    eng.copy(oT[:, :, :].rearrange("p x t -> p (x t)"), ps[:, 4, :]).then_inc(oT_set, 1)

            phases(eng, step)

            def shared(q, r, bank0=0, chunks=range(FFN // P)):
                for f in chunks:
                    eng.wait_ge(shid_made, 2 * q + f + 1)
                    after(eng, sgh_set, (q - 2) * 2 + f + 1)
                    eng.activation(ssil[:, r, f, :], ps[:, bank0 + 2 * f, :], ACT.Silu, bias=sb1_sb[:, f:f + 1]).then_inc(ssil_set, 1)

            shared(0, 0)
            eng.wait_ge(plan_step, 1)
            for e in range(TAILS_SP, NE):
                end = eng.value_load(tail_rows[0:1, e:e + 1], min_val=0, max_val=IDLE_ROW - P)
                eng.dma_start(sent[bass.ds(end, P), :], zeros[:, :]).then_inc(zeros_laid, 16)

            shared(1, 1, 4)

            def first_row(i):
                return eng.value_load(tile_row[0:1, bass.ds(i, 1)], min_val=0, max_val=XROWS - P)

            def load(i, slot):
                after(eng, xg_turned, i - 3)
                after(eng, packet_row, i - 3)
                eng.dma_start(xg[:, slot, :], sent[bass.ds(first_row(i), P), :]).then_inc(xg_in[slot], 16)

            def silu(i, r):
                eng.wait_ge(hid_set, i + 1)
                after(eng, gh_set, i - 1)
                eng.activation(sil[:, r, :], hid[:, r, 0:FFN], ACT.Silu).then_inc(sil_set, 1)

            def out_x(i, r):
                eng.wait_ge(xg_turned, i + 1)
                after(eng, hid_made, i - 1)
                eng.copy(xgT[:, r, :, :].rearrange("p c t -> p (c t)"), ps[:, 2, 0:D]).then_inc(xgT_set, 1)

            def out_h(i, r):
                eng.wait_ge(gh_turned, i + 1)
                after(eng, yg_made, i - 1)
                eng.copy(ghT[:, r, :, :].rearrange("p c t -> p (c t)"), ps[:, 3, 0:FFN]).then_inc(ghT_set, 1)

            def tiles(k, many=4):
                first, last = isinstance(k, int) and k == 0, isinstance(k, int) and k > 0
                for n in range(many):
                    i = 4 * k + n
                    if not (last and n == many - 1):
                        out_x(i + 1, (n + 1) % 2)
                    silu(i, n % 2)
                    if not (first and n == 0):
                        out_h(i - 1, (n - 1) % 2)
                    if not last:
                        load(i + 3, (n + 3) % 4)

            out_x(0, 0)
            eng.wait_ge(xg_in[2], 16)
            tiles(0)
            with eng.Fori(1, TILES // 4) as k:
                tiles(k)
            assert TILES % 4 == 3
            tiles(TILES // 4, TILES % 4)
            out_h(TILES - 1, (TILES - 1) % 2)

            def finish(q, k, r):
                eng.wait_ge(shift3_set, q + 1)
                after(eng, out_stored[r], k * 16)
                for b in range(QB):
                    eng.activation(y3[:, r, b, :], yc[:, r, b, :], ACT.Identity, bias=shift3[:, r, b:b + 1],
                                   scale=rstd3[:, r, b:b + 1]).then_inc(y3_set, 1)

            def gate_and_finish(q, k, r):
                shared(q + 2, r, chunks=[0])
                finish(q, k, r)
                shared(q + 2, r, chunks=[1])

            for r in range(2):
                shared(2 + r, r)
                finish(r, 0, r)
            with eng.Fori(1, NQ // 2 - 1) as k:
                for r in range(2):
                    gate_and_finish(2 * k + r, k, r)
            for r in range(2):
                finish(NQ - 2 + r, NQ // 2 - 1, r)

        @block.vector
        def _(eng):
            def out_turned(g):
                if g >= 2:
                    eng.wait_ge(k_made, (g - 1) * 4)
                for j in range(4):
                    eng.wait_ge(xTn_set, g * 4 + j + 1)
                    for i in range(2):
                        eng.tensor_copy(xTu[g % 2][:, :, :, 2 * j + i, :],
                                        ps[:, j, i * D:(i + 1) * D].rearrange("p (c u i) -> p c u i", c=DC, i=DH)
                                        ).then_inc(xTu_set, 1)

            out_turned(0)
            for g in range(NG):
                if g + 1 < NG:
                    out_turned(g + 1)
                for j in range(4):
                    eng.wait_ge(k_made, g * 4 + j + 1)
                    eng.tensor_copy(kk_of(g).rearrange("p (a u) -> p u a", u=NU)[:, 2 * j:2 * j + 2, :],
                                    ps[:, 4 + j, :].rearrange("p (u a) -> p u a", u=2)).then_inc(kk_set, 1)
            eng.wait_ge(tables_in, 32)
            eng.wait_ge(consts_set, 2)
            eng.tensor_copy(base[:, :], region_rows).then_inc(base_set, 1)

            eng.tensor_scalar(zeros[:, D:PACKET], padding_row, 0.0, None, ALU.add).then_inc(zeros_set, 1)

            def maxes(k, s, u):
                kk_, r = at(k, s, 0)
                t = kk_ * 2 + r
                eng.wait_ge(scored, t * 4 + u + 1)
                after(eng, expd, (t - 2) * 4 + u + 1)
                eng.tensor_reduce(nmax[:, r, 4 * u:4 * u + 4], SCORE[u % 2].rearrange("p (h j) -> p h j", j=P),
                                  AX_X, ALU.max, negate=True).then_inc(maxed, 1)

            def stats(t, r, res, bn, res_set, bn_set):
                eng.wait_ge(res_set, t + 1)
                eng.bn_stats(bn[:, r, :], res[:, r, :]).then_inc(bn_set, 1)

            def moments(t, r, bn, mv, mv_set):
                eng.bn_aggr(mv[:, r, :], bn[:, r, :]).then_inc(mv_set, 1)
                eng.wait_ge(mv_set, 2 * t + 1)
                eng.tensor_scalar(mv[:, r, 1:2], mv[:, r, 1:2], EPS, None, ALU.add).then_inc(mv_set, 1)

            def step(k, s, live):
                n = 2 * k + s
                k2, r2 = at(k, s, 2)
                t2 = k2 * 2 + r2
                k3, r3 = at(k, s, 3)
                t3 = k3 * 2 + r3
                k5, r5 = at(k, s, 5)
                t5 = k5 * 2 + r5
                k6, r6 = at(k, s, 6)
                t6 = k6 * 2 + r6
                if live(5):
                    eng.wait_ge(gexp_set, t5 + 1)
                    eng.reciprocal(ginv[:, r5, :], gsum[:, r5, :]).then_inc(ginv_set, 1)
                    eng.wait_ge(ginv_set, t5 + 1)
                    eng.tensor_scalar(gprob[:, r5, :], gexp[:, r5, :], ginv[:, r5, :], None, ALU.mult).then_inc(gprob_set, 1)
                    eng.wait_ge(gprob_set, t5 + 1)
                if live(6):
                    eng.wait_ge(gc_set, t6 + 2)
                    eng.wait_ge(base_set, t6 + 1)
                    eng.tensor_tensor(place[:, r6, :], gc[:, 1 - r6, NE:2 * NE], base[:, :], ALU.add).then_inc(place_set, 1)
                if live(5):
                    eng.max(top_p[:, r5, :], gprob[:, r5, :]).then_inc(top_p_set, 1)
                    eng.wait_ge(top_p_set, t5 + 1)
                if live(6):
                    eng.wait_ge(place_set, t6 + 1)
                    eng.tensor_tensor(mine[:, r6, :, :], pick[:, r6, :, :],
                                      place[:, r6, :].unsqueeze(1).broadcast_to([P, TOPK, NE]), ALU.mult).then_inc(mine_set, 1)
                if live(5):
                    eng.max_index(top_i[:, r5, :], top_p[:, r5, :], gprob[:, r5, :]).then_inc(top_i_set, 1)
                if live(6):
                    eng.wait_ge(mine_set, t6 + 1)
                    with nc.allow_low_precision(reason="a whole number below 2**24, summed in float32: exact"):
                        eng.tensor_reduce(pos[:, r6, :], mine[:, r6, :, :], AX_X, ALU.add).then_inc(pos_set, 1)
                    eng.tensor_tensor(base[:, :], base[:, :], gc[:, 1 - r6, 2 * NE:3 * NE], ALU.add).then_inc(base_set, 1)
                if live(0):
                    maxes(k, s, 0)
                if live(3):
                    eng.wait_ge(scx_made, t3 + 1)
                    after(eng, yx_made, t3 - 1)
                    eng.tensor_tensor(scx[:, r3, :], SCX, decay, ALU.mult).then_inc(scx_set, 1)
                if live(2):
                    eng.wait_ge(heads_turned, t2 + 1)
                    eng.reciprocal(rden[:, r2, :], HEADS[:, :, DH]).then_inc(den_set, 1)
                    eng.wait_ge(den_set, t2 + 1)
                    eng.tensor_tensor(att[:, r2, :].rearrange("p (h d) -> p h d", d=DH), HEADS[:, :, 0:DH],
                                      rden[:, r2, :].unsqueeze(2).broadcast_to([P, H, DH]), ALU.mult).then_inc(att_set, 1)
                    eng.wait_ge(att_set, t2 + 1)
                    eng.wait_ge(xn_in[r2], k2 * 16 + 16)
                    after(eng, x1_set, t2 - 1)
                    eng.tensor_tensor(res1[:, r2, :], att[:, r2, :], xn[:, r2, :], ALU.add).then_inc(res1_set, 1)
                    stats(t2, r2, res1, bn1, res1_set, bn1_set)
                    eng.wait_ge(bn1_set, t2 + 1)
                if live(0):
                    maxes(k, s, 1)
                if live(2):
                    moments(t2, r2, bn1, mv1, mv1_set)
                if live(5):
                    eng.tensor_scalar(cw_all[:, t5, :], top_p[:, r5, 0:TOPK], 1.0, None, ALU.mult).then_inc(kept_set, 1)
                    eng.wait_ge(top_i_set, t5 + 1)
                    eng.tensor_copy(top_f[:, r5, :], top_i[:, r5, 0:TOPK]).then_inc(top_f_set, 1)
                    eng.wait_ge(top_f_set, t5 + 1)
                    eng.tensor_tensor(pick[:, r5, :, :], expert_ids.unsqueeze(1).broadcast_to([P, TOPK, NE]),
                                      top_f[:, r5, :].unsqueeze(2).broadcast_to([P, TOPK, NE]), ALU.is_equal).then_inc(pick_set, 1)
                if live(2):
                    eng.wait_ge(rstd1_set, t2 + 1)
                    after(eng, mid_made, t2 - 1)
                    after(eng, res2_set, t2 - 1)
                    eng.tensor_scalar(x1[:, r2, :], res1[:, r2, :], mv1[:, r2, 0:1], rstd1[:, r2, :],
                                      ALU.subtract, ALU.mult).then_inc(x1_set, 1)
                if live(5):
                    eng.wait_ge(pick_set, t5 + 1)
                    after(eng, mid_made, t5 + 2)
                    eng.tensor_tensor(picks[:, r5, :], pick[:, r5, 0, :], pick[:, r5, 1, :], ALU.add).then_inc(picks_set, 1)
                if live(2):
                    eng.wait_ge(xv_set, t2 + 1)
                    after(eng, rot_set, 4 * (t2 - 1))
                    for into, table in ((ra, rot_cos), (rb, rot_sin)):
                        eng.tensor_tensor(into[:, r2, 0:2, :], KQ[:, 0:2, :], table[:, 0:2, :], ALU.mult).then_inc(rot_k, 1)
                if live(0):
                    maxes(k, s, 2)
                if live(3):
                    eng.wait_ge(yx_made, t3 + 1)
                    eng.tensor_tensor(res2[:, r3, :], YX, x1[:, r3, :], ALU.add).then_inc(res2_set, 1)
                    stats(t3, r3, res2, bn2, res2_set, bn2_set)
                    eng.wait_ge(bn2_set, t3 + 1)
                if live(5):
                    after(eng, sent_in[r5], k5 * 32)
                    eng.tensor_copy(x2s[:, r5, :, 0:D], x2[:, r5, :].unsqueeze(1).broadcast_to([P, TOPK, D])).then_inc(x2s_set, 1)
                    eng.tensor_scalar(x2s[:, r5, :, D], result_rows[:, t5, :], 0.0, None, ALU.add).then_inc(x2s_set, 1)
                if live(3):
                    moments(t3, r3, bn2, mv2, mv2_set)
                if live(4) or live(5):
                    eng.wait_ge(mid_made, n - 1)
                    if live(2):
                        eng.wait_ge(x1T_set, t2 + 1)
                    lo, hi = (0 if live(4) else NE), (3 * NE if live(5) else NE)
                    eng.tensor_tensor(gc[:, s, lo:hi], GATE[:, lo:hi], gate_b_sb[:, lo:hi], ALU.add).then_inc(gc_set, 1)
                if live(0):
                    maxes(k, s, 3)
                if live(4):
                    k4, r4 = at(k, s, 4)
                    eng.wait_ge(gc_set, n - 3)
                    eng.tensor_reduce(lmax[:, r4, :], gc[:, r4, 0:NE], AX_X, ALU.max, negate=True).then_inc(lmax_set, 1)
                if live(3):
                    eng.wait_ge(rstd2_set, t3 + 1)
                    after(eng, x2b_set, t3 - 1)
                    after(eng, x2s_set, 2 * (t3 - 1))
                    after(eng, x2_turned, t3 - 1)
                    eng.tensor_scalar(x2[:, r3, :], res2[:, r3, :], mv2[:, r3, 0:1], rstd2[:, r3, :],
                                      ALU.subtract, ALU.mult).then_inc(x2_set, 1)
                if live(2):
                    eng.wait_ge(xq_made, t2 + 1)
                    for into, table in ((ra, rot_cos), (rb, rot_sin)):
                        eng.tensor_tensor(into[:, r2, 2:4, :], KQ[:, 2:4, :], table[:, 2:4, :], ALU.mult).then_inc(rot_q, 1)

            phases(eng, step)

            steps = [0]

            def planned(ins):
                steps[0] += 1
                ins.then_inc(plan_step, 1)
                eng.wait_ge(plan_step, steps[0])

            eng.wait_ge(base_set, B + 1)
            planned(eng.tensor_scalar(tail_rows[:, :], base[:, :], lane_id, None, ALU.add))
            planned(eng.tensor_tensor(counts[:, 0, :], base[:, :], region_rows, ALU.subtract))
            planned(eng.tensor_scalar(counts_i[:, 0, :], counts[:, 0, :], float(P - 1), None, ALU.add))
            planned(eng.tensor_scalar(counts_i[:, 1, :], counts_i[:, 0, :], P.bit_length() - 1, None, ALU.arith_shift_right))
            planned(eng.tensor_copy(counts[:, 1, :], counts_i[:, 1, :]))
            planned(eng.tensor_tensor(upto[:, :, :], counts[:, 1, :].unsqueeze(1).broadcast_to([P, NE, NE]),
                                      not_later, ALU.mult))
            planned(eng.tensor_reduce(counts[:, 2, :], upto[:, :, :], AX_X, ALU.add))
            planned(eng.tensor_scalar(counts[:, 3, :], counts[:, 1, :], -float(P), float(REGION), ALU.mult, ALU.add))
            planned(eng.tensor_tensor(passed[:, :, :], counts[0:1, 2, :].unsqueeze(1).broadcast_to([1, TILES, NE]),
                                      tile_ids[0:1, :].unsqueeze(2).broadcast_to([1, TILES, NE]), ALU.is_le))
            planned(eng.tensor_reduce(tile_f[:, 0, :], passed[:, :, :], AX_X, ALU.add))
            planned(eng.tensor_scalar(tile_expert[:, :], tile_f[:, 0, :], float(NE - 1), None, ALU.min))
            planned(eng.tensor_tensor(skipped[:, :, :], passed[:, :, :],
                                      counts[0:1, 3, :].unsqueeze(1).broadcast_to([1, TILES, NE]), ALU.mult))
            planned(eng.tensor_reduce(tile_f[:, 1, :], skipped[:, :, :], AX_X, ALU.add))
            planned(eng.tensor_tensor(tile_row[:, :], tile_f[:, 1, :], tile_rows[0:1, :], ALU.add))
            assert steps[0] == PLAN_STEPS

            def shared(q, r, bank0=0, chunks=range(FFN // P)):
                for f in chunks:
                    eng.wait_ge(ssil_set, 2 * q + f + 1)
                    after(eng, sy_made, (q - 1) * QB)
                    eng.scalar_tensor_tensor(out=sgh[:, r, f, :], in0=ps[:, bank0 + 2 * f + 1, :],
                                             scalar=sb1_sb[:, 2 + f:3 + f], in1=ssil[:, r, f, :],
                                             op0=ALU.add, op1=ALU.mult).then_inc(sgh_set, 1)

            for r in range(2):
                shared(r, r, 4 * r)

            eng.wait_ge(rb_in, 16 * (NE + 1))

            def biased(i, r, e):
                eng.wait_ge(hid_made, i + 1)
                after(eng, gh_set, i - 1)
                eng.tensor_tensor(hid[:, r, :], ps[:, r, :], rb_h[:, bass.ds(e * (2 * FFN), 2 * FFN)], ALU.add).then_inc(hid_set, 1)

            def pad_rows(i, slot, loads):
                eng.wait_ge(xg_in[slot], loads * 16)
                eng.scalar_tensor_tensor(out=pad_shift[:, slot:slot + 1], in0=xg[:, slot, D:PACKET], scalar=float(PADDING),
                                         in1=tile_rows[:, bass.ds(i, 1)], op0=ALU.is_ge, op1=ALU.mult).then_inc(pad_shifted, 1)

            def packet_rows(i, slot):
                eng.wait_ge(pad_shifted, i + 1)
                eng.tensor_tensor(result_row[:, slot:slot + 1], pad_shift[:, slot:slot + 1], xg[:, slot, D:PACKET],
                                  ALU.add).then_inc(packet_row, 1)

            def out_y(i, r, sent_before, e):
                eng.wait_ge(yg_made, i + 1)
                after(eng, yg_out[r], sent_before * 16)
                eng.tensor_tensor(yg[:, r, :], ps[:, 4 + r, 0:D], rb_y[:, bass.ds(e * D, D)], ALU.add).then_inc(yg_set, 1)

            def expert(i):
                return eng.value_load(tile_expert[0:1, bass.ds(i, 1)], min_val=0, max_val=NE - 1)

            def tiles(k, many=4):
                first = isinstance(k, int) and k == 0
                two_before, before = None, None
                for n in range(many):
                    i = 4 * k + n
                    this = expert(i)
                    biased(i, n % 2, this)
                    pad_rows(i, n, k + 1)
                    if n < 2 and not first:
                        two_before = expert(i - 2)
                    if two_before is not None:
                        out_y(i - 2, n % 2, 2 * k + n // 2 - 1, two_before)
                    packet_rows(i, n)
                    two_before, before = before, this
                return two_before, before

            tiles(0)
            with eng.Fori(1, TILES // 4) as k:
                tiles(k)
            two_before, before = tiles(TILES // 4, TILES % 4)
            out_y(TILES - 2, TILES % 2, (TILES - 2) // 2, two_before)
            out_y(TILES - 1, (TILES - 1) % 2, (TILES - 1) // 2, before)

            def weights_of(q, r):
                eng.tensor_scalar(cw4[:, r, :, :], cw_all[:, bass.ds(q * QB, QB), :], 1.0, None, ALU.mult).then_inc(cw4_set, 1)

            def shifts_of(q, r):
                eng.wait_ge(rstd3_set, q + 1)
                eng.scalar_tensor_tensor(out=shift3[:, r, :], in0=mv3[:, r, :, 0], scalar=-1.0, in1=rstd3[:, r, :],
                                         op0=ALU.mult, op1=ALU.mult).then_inc(shift3_set, 1)

            def weighted(q, r, j, source, target, done, source_done):
                for b in range(QB):
                    if source_done is not None:
                        eng.wait_ge(source_done, q * QB + b + 1)
                    eng.scalar_tensor_tensor(out=target[:, r, b, :], in0=got[:, r, b, j, :], scalar=cw4[:, r, b, j:j + 1],
                                             in1=source[:, r, b, :], op0=ALU.mult, op1=ALU.add).then_inc(done, 1)

            def mix(q, k, r):
                eng.wait_ge(x2n_in[r], k * 16 + 16)
                eng.wait_ge(got_in[r], k * 16 + 16)
                eng.wait_ge(cw4_set, q + 1)
                weighted(q, r, 0, x2n, yb, mix_a, None)
                weighted(q, r, 1, yb, ya, mix_b, mix_a)

            def add_shared(q, r, source, target, done):
                for b in range(QB):
                    eng.wait_ge(sy_made, q * QB + b + 1)
                    if done is mix_c:
                        eng.wait_ge(mix_b, q * QB + b + 1)
                    eng.tensor_tensor(target[:, r, b, :], ps[:, 4 + b, 0:D], source[:, r, b, :], ALU.add).then_inc(done, 1)

            def moments(q, r, weights_next=None):
                for b in range(QB):
                    eng.wait_ge(mix_c, q * QB + b + 1)
                    eng.bn_stats(bn3[:, r, b, :], yc[:, r, b, :]).then_inc(bn3_set, 1)
                eng.wait_ge(bn3_set, (q + 1) * QB)
                if weights_next is not None:
                    weights_of(weights_next, r)
                for b in range(QB):
                    eng.bn_aggr(mv3[:, r, b, :], bn3[:, r, b, :]).then_inc(mv3_set, 1)
                eng.wait_ge(mv3_set, (q + 1) * QB + q)
                after(eng, rstd3_set, q - 1)
                eng.tensor_scalar(var3[:, r, :], mv3[:, r, :, 1], EPS, None, ALU.add).then_inc(mv3_set, 1)

            for r in range(2):
                weights_of(r, r)
            eng.wait_ge(sy_made, QB)
            eng.wait_ge(x2n_in[0], 16)
            add_shared(0, 0, x2n, ya, mix_a)
            shared(2, 0, chunks=[0])
            eng.wait_ge(got_in[0], 16)
            eng.wait_ge(cw4_set, 1)
            weighted(0, 0, 0, ya, yb, mix_b, mix_a)
            weighted(0, 0, 1, yb, yc, mix_c, mix_b)
            mix(1, 0, 1)
            shared(2, 0, chunks=[1])
            moments(0, 0, weights_next=2)

            def close(q, k, r, hidden=True):
                after(eng, y3_set, (q - 1) * QB)
                add_shared(q, r, ya, yc, mix_c)
                if isinstance(q, int) and q in (1, NQ - 1):
                    shifts_of(q - 1, 1 - r)
                moments(q, r, weights_next=q + 2 if hidden else None)
                if hidden:
                    shared(q + 2, r, chunks=[0])
                    if isinstance(q, int):
                        shared(q + 2, r, chunks=[1])
                    shifts_of(q, r)
                    if isinstance(q, int):
                        mix(q + 1, k + r, 1 - r)
                        mix(q + 2, k + 1, r)
                    else:
                        mix(q + 2, k + 1, r)
                        shared(q + 2, r, chunks=[1])

            close(1, 0, 1)
            with eng.Fori(1, NQ // 2 - 1) as k:
                for r in range(2):
                    close(2 * k + r, k, r)
            for r in range(2):
                close(NQ - 2 + r, NQ // 2 - 1, r, hidden=False)
            shifts_of(NQ - 1, 1)



_INS = ['x', 'ctx_1024', 'L0_attn_qkv_weights', 'L0_xattn_Wq', 'L0_xattn_Wk', 'L0_xattn_Wv', 'L0_ffn_gate_w',
        'L0_ffn_gate_b', 'L0_ffn_sw1', 'L0_ffn_sb1', 'L0_ffn_sw2', 'L0_ffn_sb2', 'L0_ffn_rw1', 'L0_ffn_rb1',
        'L0_ffn_rw2', 'L0_ffn_rb2']


def kernel(**inputs):
    import concourse.bacc as _bacc
    from concourse.bass_utils import run_bass_kernel_spmd as _run
    import ml_dtypes

    nc = _bacc.Bacc("TRN2", target_bir_lowering=False, num_devices=1)
    arrays = {name: np.ascontiguousarray(inputs[name]) for name in _INS}
    table_f32, table_bf16 = shape_tables()
    arrays["table_f32"] = table_f32
    arrays["table_bf16"] = table_bf16.astype(ml_dtypes.bfloat16)
    args = [nc.dram_tensor(f"in_{name}", a.shape, mybir.dt.from_np(a.dtype), kind="ExternalInput").ap()
            for name, a in arrays.items()]
    out = nc.dram_tensor("out_0", (B, S, D), F32, kind="ExternalOutput").ap()
    decoder_kernel(nc, *args, out)
    r = _run(nc, [{f"in_{name}": a for name, a in arrays.items()}], core_ids=[0])
    return r.results[0]["out_0"]
```
